# Optimizing a Trainium2 kernel written in Bass

```python
import numpy as np
import jax
import jax.numpy as jnp

def _softmax(x, axis=-1):
    return jax.nn.softmax(x, axis=axis)
def _gelu(x):
    return jax.nn.gelu(x, approximate=True)
def _silu(x):
    return jax.nn.silu(x)
def _sigmoid(x):
    return jax.nn.sigmoid(x)
def _layernorm(x, axis=-1, eps=1e-5):
    m = jnp.mean(x, axis=axis, keepdims=True)
    v = jnp.var(x, axis=axis, keepdims=True)
    return (x - m) / jnp.sqrt(v + eps)
def _scatter_add(tgt, idx, src, axis=0):
    return tgt.at[idx].add(src)
def _segment_sum(src, seg, n):
    return jax.ops.segment_sum(src, seg, n)

kernel_name = 'mk_adj_ffn_d1_adj_256_592363'

def setup_inputs(seed: int = 0):
    np.random.seed(seed)
    _w = jnp.asarray
    def _rec_inputs():
        import jax
        import jax.numpy as jnp
        _gk = jax.random.key(seed)
        x = -0.000929 + 1 * jax.random.normal(jax.random.fold_in(_gk, 1), (2708, 256), jnp.float32)
        _a = jax.random.bernoulli(jax.random.fold_in(_gk, 2), 0.00295421, (2708, 2708))
        _a = jnp.logical_or(_a, jnp.swapaxes(_a, -1, -2))
        _a = jnp.logical_or(_a, jnp.eye(2708, dtype=bool))
        _af = _a.astype(jnp.float32)
        _af = _af * jax.random.uniform(jax.random.fold_in(_gk, 3), (2708, 2708), jnp.float32, 0.05, 1)
        adj = _af
        return x, adj
    x, adj = _rec_inputs()
    def _L0_gnn_setup():
        import jax, jax.numpy as jnp
        import numpy as np
        N, H, HEADS = (4096, 256, 3)
        ALPHA = 0.2
        NEG_INF = -9000000000000000.0

        def _sign_adj(key, n, density):
            k1, k2 = jax.random.split(key)
            mask = jax.random.uniform(k1, (n, n)) < density
            sign = jnp.where(jax.random.uniform(k2, (n, n)) < 0.5, -1.0, 1.0)
            adj = jnp.where(mask, sign, 0.0).astype(jnp.float32)
            idx = jnp.arange(n)
            return adj.at[idx, idx].set(1.0)

        def _gru_cell(x, hstate, Wih, Whh, bih, bhh):
            gi = x @ Wih.T + bih
            gh = hstate @ Whh.T + bhh
            ir, iz, inn = jnp.split(gi, 3, axis=1)
            hr, hz, hn = jnp.split(gh, 3, axis=1)
            r = jax.nn.sigmoid(ir + hr)
            z = jax.nn.sigmoid(iz + hz)
            n = jnp.tanh(inn + r * hn)
            return (1.0 - z) * n + z * hstate

        def _gat_head(h, node_adj, edge_adj, W, a):
            hW = h @ W
            hp = (node_adj > 0).astype(hW.dtype) @ hW
            hm = (node_adj < 0).astype(hW.dtype) @ hW
            e_plus = jax.nn.leaky_relu(jnp.concatenate([hp, hm], axis=1) @ a, ALPHA)[:, 0]
            e_minus = jax.nn.leaky_relu(jnp.concatenate([hm, hp], axis=1) @ a, ALPHA)[:, 0]
            att = jnp.where(edge_adj > 0, e_plus[None, :], NEG_INF)
            att = jnp.where(edge_adj < 0, e_minus[None, :], att)
            att = jax.nn.softmax(att, axis=1)
            return att * edge_adj @ hW
        key = jax.random.key(seed)
        ks = jax.random.split(key, 16)
        std = 0.01
        gain = 1.414
        return {'h': jax.random.normal(ks[0], (N, H), jnp.float32), 'node_adj': _sign_adj(ks[1], N, 0.005), 'edge_adj': _sign_adj(ks[2], N, 0.005), 'gat_W': jax.random.normal(ks[3], (HEADS, H, H), jnp.float32) * (gain / np.sqrt(H, dtype=np.float32)), 'gat_a': jax.random.normal(ks[4], (HEADS, 2 * H, 1), jnp.float32) * 0.1, 'edge_Wih': jax.random.normal(ks[5], (3 * H, H), jnp.float32) * std, 'edge_Whh': jax.random.normal(ks[6], (3 * H, H), jnp.float32) * std, 'edge_bih': jnp.zeros((3 * H,), jnp.float32), 'edge_bhh': jnp.zeros((3 * H,), jnp.float32), 'node_Wih': jax.random.normal(ks[7], (3 * H, H), jnp.float32) * std, 'node_Whh': jax.random.normal(ks[8], (3 * H, H), jnp.float32) * std, 'node_bih': jnp.zeros((3 * H,), jnp.float32), 'node_bhh': jnp.zeros((3 * H,), jnp.float32)}
    _L0_gnn_all = _L0_gnn_setup()
    _L0_gnn_in = {k: v for k, v in _L0_gnn_all.items() if k in ('gat_W', 'gat_a', 'edge_Wih', 'edge_Whh', 'edge_bih', 'edge_bhh', 'node_Wih', 'node_Whh', 'node_bih', 'node_bhh', )}
    del _L0_gnn_all

    def _L0_ffn_setup():
        import math
        import jax, jax.numpy as jnp
        import numpy as np
        CAPACITY_FACTOR = 1.25
        TOP_K = 2
        LN_EPS = 1e-05

        def _layer_norm(x, gamma, beta):
            mu = jnp.mean(x, axis=-1, keepdims=True)
            var = jnp.var(x, axis=-1, keepdims=True)
            return (x - mu) * jax.lax.rsqrt(var + LN_EPS) * gamma + beta
        key = jax.random.key(seed)
        ks = jax.random.split(key, 4)
        B, S, D, F, E = (8, 4096, 256, 512, 8)
        x = jax.random.normal(ks[0], (B, S, D), dtype=jnp.float32)
        Wr = jax.random.normal(ks[1], (D, E), dtype=jnp.float32) / np.sqrt(D)
        br = jnp.zeros((E,), jnp.float32)
        W1 = jax.random.normal(ks[2], (E, D, F), dtype=jnp.float32) / np.sqrt(D)
        b1 = jnp.zeros((E, F), jnp.float32)
        W2 = jax.random.normal(ks[3], (E, F, D), dtype=jnp.float32) / np.sqrt(F)
        b2 = jnp.zeros((E, D), jnp.float32)
        gamma = jnp.ones((D,), jnp.float32)
        beta = jnp.zeros((D,), jnp.float32)
        return {'x': x, 'Wr': Wr, 'br': br, 'W1': W1, 'b1': b1, 'W2': W2, 'b2': b2, 'gamma': gamma, 'beta': beta}
    _L0_ffn_all = _L0_ffn_setup()
    _L0_ffn_in = {k: v for k, v in _L0_ffn_all.items() if k in ('Wr', 'br', 'W1', 'b1', 'W2', 'b2', 'gamma', 'beta', )}
    del _L0_ffn_all

    return {
        "x": x,
        "adj": adj,
        "L0_gnn_gat_W": _L0_gnn_in["gat_W"],
        "L0_gnn_gat_a": _L0_gnn_in["gat_a"],
        "L0_gnn_edge_Wih": _L0_gnn_in["edge_Wih"],
        "L0_gnn_edge_Whh": _L0_gnn_in["edge_Whh"],
        "L0_gnn_edge_bih": _L0_gnn_in["edge_bih"],
        "L0_gnn_edge_bhh": _L0_gnn_in["edge_bhh"],
        "L0_gnn_node_Wih": _L0_gnn_in["node_Wih"],
        "L0_gnn_node_Whh": _L0_gnn_in["node_Whh"],
        "L0_gnn_node_bih": _L0_gnn_in["node_bih"],
        "L0_gnn_node_bhh": _L0_gnn_in["node_bhh"],
        "L0_ffn_Wr": _L0_ffn_in["Wr"],
        "L0_ffn_br": _L0_ffn_in["br"],
        "L0_ffn_W1": _L0_ffn_in["W1"],
        "L0_ffn_b1": _L0_ffn_in["b1"],
        "L0_ffn_W2": _L0_ffn_in["W2"],
        "L0_ffn_b2": _L0_ffn_in["b2"],
        "L0_ffn_gamma": _L0_ffn_in["gamma"],
        "L0_ffn_beta": _L0_ffn_in["beta"],
    }

def reference(x, adj, L0_gnn_gat_W, L0_gnn_gat_a, L0_gnn_edge_Wih, L0_gnn_edge_Whh, L0_gnn_edge_bih, L0_gnn_edge_bhh, L0_gnn_node_Wih, L0_gnn_node_Whh, L0_gnn_node_bih, L0_gnn_node_bhh, L0_ffn_Wr, L0_ffn_br, L0_ffn_W1, L0_ffn_b1, L0_ffn_W2, L0_ffn_b2, L0_ffn_gamma, L0_ffn_beta):
    import jax
    import jax.numpy as jnp
    def _L0_gnn_ref(h, node_adj, edge_adj, gat_W, gat_a, edge_Wih, edge_Whh, edge_bih, edge_bhh, node_Wih, node_Whh, node_bih, node_bhh):
        import jax, jax.numpy as jnp
        import numpy as np
        N, H, HEADS = (4096, 256, 3)
        ALPHA = 0.2
        NEG_INF = -9000000000000000.0

        def _sign_adj(key, n, density):
            k1, k2 = jax.random.split(key)
            mask = jax.random.uniform(k1, (n, n)) < density
            sign = jnp.where(jax.random.uniform(k2, (n, n)) < 0.5, -1.0, 1.0)
            adj = jnp.where(mask, sign, 0.0).astype(jnp.float32)
            idx = jnp.arange(n)
            return adj.at[idx, idx].set(1.0)

        def _gru_cell(x, hstate, Wih, Whh, bih, bhh):
            gi = x @ Wih.T + bih
            gh = hstate @ Whh.T + bhh
            ir, iz, inn = jnp.split(gi, 3, axis=1)
            hr, hz, hn = jnp.split(gh, 3, axis=1)
            r = jax.nn.sigmoid(ir + hr)
            z = jax.nn.sigmoid(iz + hz)
            n = jnp.tanh(inn + r * hn)
            return (1.0 - z) * n + z * hstate

        def _gat_head(h, node_adj, edge_adj, W, a):
            hW = h @ W
            hp = (node_adj > 0).astype(hW.dtype) @ hW
            hm = (node_adj < 0).astype(hW.dtype) @ hW
            e_plus = jax.nn.leaky_relu(jnp.concatenate([hp, hm], axis=1) @ a, ALPHA)[:, 0]
            e_minus = jax.nn.leaky_relu(jnp.concatenate([hm, hp], axis=1) @ a, ALPHA)[:, 0]
            att = jnp.where(edge_adj > 0, e_plus[None, :], NEG_INF)
            att = jnp.where(edge_adj < 0, e_minus[None, :], att)
            att = jax.nn.softmax(att, axis=1)
            return att * edge_adj @ hW
        dn = jnp.diag(node_adj)
        de = jnp.diag(edge_adj)
        idx = jnp.arange(node_adj.shape[0])
        node_adj_norm = node_adj.at[idx, idx].add(-dn)
        edge_adj_norm = edge_adj.at[idx, idx].add(-de)
        node_support = node_adj_norm @ h
        edge_output = _gru_cell(node_support, h, edge_Wih, edge_Whh, edge_bih, edge_bhh)
        edge_support = _gat_head(h, node_adj_norm, edge_adj_norm, gat_W[0], gat_a[0])
        for i in range(1, HEADS):
            edge_support = edge_support + _gat_head(h, node_adj_norm, edge_adj_norm, gat_W[i], gat_a[i])
        edge_support = edge_support / HEADS
        node_output = _gru_cell(edge_support, h, node_Wih, node_Whh, node_bih, node_bhh)
        return de[:, None] * edge_output + dn[:, None] * node_output

    def _L0_ffn_ref(x, Wr, br, W1, b1, W2, b2, gamma, beta):
        import math
        import jax, jax.numpy as jnp
        import numpy as np
        CAPACITY_FACTOR = 1.25
        TOP_K = 2
        LN_EPS = 1e-05

        def _layer_norm(x, gamma, beta):
            mu = jnp.mean(x, axis=-1, keepdims=True)
            var = jnp.var(x, axis=-1, keepdims=True)
            return (x - mu) * jax.lax.rsqrt(var + LN_EPS) * gamma + beta
        B, S, D = x.shape
        E = Wr.shape[1]
        N = B * S
        K = TOP_K
        logits = jnp.mean(x, axis=1) @ Wr + br
        routing_weights = jax.nn.softmax(logits, axis=-1)
        capacity = float(math.ceil(N * CAPACITY_FACTOR / E))
        expected_loads = routing_weights.sum(axis=0) * (N / B)
        scale = jnp.where(expected_loads > capacity, capacity / expected_loads, 1.0)
        routing_weights = jax.nn.softmax(routing_weights * scale, axis=-1)
        rw_tok = jnp.broadcast_to(routing_weights[:, None, :], (B, S, E)).reshape(N, E)
        top_w, top_i = jax.lax.top_k(rw_tok, K)
        top_w = jax.nn.softmax(top_w, axis=-1)
        xf = x.reshape(N, D)
        h = jax.nn.gelu(jnp.einsum('nd,edf->enf', xf, W1) + b1[:, None, :], approximate=False)
        y = jnp.einsum('enf,efd->end', h, W2) + b2[:, None, :]
        w_dense = jnp.zeros((N, E), x.dtype).at[jnp.arange(N)[:, None], top_i].add(top_w)
        out = jnp.einsum('ne,end->nd', w_dense, y).reshape(B, S, D)
        out = _layer_norm(out + x, gamma, beta)
        return out

    x = x + _L0_gnn_ref(_layernorm(x, axis=-1), adj, adj, L0_gnn_gat_W, L0_gnn_gat_a, L0_gnn_edge_Wih, L0_gnn_edge_Whh, L0_gnn_edge_bih, L0_gnn_edge_bhh, L0_gnn_node_Wih, L0_gnn_node_Whh, L0_gnn_node_bih, L0_gnn_node_bhh)
    x = x + _L0_ffn_ref((_layernorm(x, axis=-1))[None], L0_ffn_Wr, L0_ffn_br, L0_ffn_W1, L0_ffn_b1, L0_ffn_W2, L0_ffn_b2, L0_ffn_gamma, L0_ffn_beta)[0]
    return x


_drawn_inputs = setup_inputs


def setup_inputs(seed=0):
    import zlib

    import numpy as np

    out = dict(_drawn_inputs(seed))
    spreads = {'L0_gnn_edge_bih': (0.0, 0.413),
     'L0_gnn_edge_bhh': (0.0, 0.655),
     'L0_gnn_node_bih': (0.0, 0.397),
     'L0_gnn_node_bhh': (0.0, 0.601),
     'L0_ffn_br': (0.0, 0.1),
     'L0_ffn_b1': (0.0, 0.471),
     'L0_ffn_b2': (0.0, 0.317),
     'L0_ffn_gamma': (1.0, 0.2),
     'L0_ffn_beta': (0.0, 0.1)}
    factors = {'L0_gnn_gat_W': 4.057,
     'L0_gnn_gat_a': 4.262,
     'L0_gnn_edge_Whh': 2.819,
     'L0_gnn_node_Wih': 4.063,
     'L0_gnn_node_Whh': 2.764,
     'L0_ffn_Wr': 8.0}
    for name, (base, spread) in spreads.items():
        noise = np.random.default_rng([zlib.crc32(name.encode()), seed]).standard_normal(out[name].shape)
        drawn = base * np.exp(spread * noise) if base else spread * noise
        out[name] = jnp.asarray(drawn.astype(out[name].dtype))
    for name, factor in factors.items():
        out[name] = (out[name] * factor).astype(out[name].dtype)
    return out
```

```python
from contextlib import ExitStack

import concourse.bass as bass
from concourse import mybir

P = 128
N = 2708
D = 256
KD = D // P
NT = (N + P - 1) // P
NP = NT * P
HEADS = 3
NC2 = 2 * HEADS
ALPHA = 0.2
NEG_INF = -9000000000000000.0
LN_EPS = 1e-5
E = 8
F = 512
FT = F // P
TOP_K = 2
CAPACITY = float(-(-N * 5 // (4 * E)))
GB = 4
NG = (NT + GB - 1) // GB
GSIZE = [min(GB, NT - GB * g) for g in range(NG)]
CH = GB * P
NCH = NG
LAST = NCH - 1

F32 = mybir.dt.float32
F32R = mybir.dt.float32r
BF16 = mybir.dt.bfloat16
U32 = mybir.dt.uint32
U8 = mybir.dt.uint8
ALU = mybir.AluOpType
ACT = mybir.ActivationFunctionType
AX = mybir.AxisListType


class Chain:

    def __init__(self, eng, sem):
        self.eng, self.sem, self.n = eng, sem, 0

    def __call__(self, ins):
        self.n += 1
        ins.then_inc(self.sem, 1)
        self.eng.wait_ge(self.sem, self.n)


def build(nc, x_in, adj_t, adj_n, diag_in, ident_in, notid_in, gat_wt_in, gat_w_in, gat_a_in,
          gru_w_in, gru_b_in, wr_in, br_in, w1_in, b1_in, w2_in, b2_in, gamma_in, beta_in, out):
    s_dram = nc.dram_tensor("supportT_scratch", (P, KD, NP), F32, kind="Internal").ap()
    es_dram = nc.dram_tensor("attentionT_scratch", (P, KD, NP), F32, kind="Internal").ap()
    h_dram = nc.dram_tensor("normedT_scratch", (P, KD, NP), F32, kind="Internal").ap()
    with ExitStack() as keep:
        def sb(name, shape, dt, ctx=keep):
            return ctx.enter_context(nc.sbuf_tensor(name, shape, dt))

        ident = sb("ident", [P, P], F32)
        eps = sb("eps", [P, 1], F32)
        with ExitStack() as graph:
            shared = dict(
                ident=ident, eps=eps,
                notid=sb("notid", [P, P], F32, graph),
                h_mov=sb("h_mov", [P, NT, 2 * D], F32R, graph),
                logit=sb("logit", [P, NC2, NP], F32, graph),
                a_ring=sb("a_ring", [P, 2, NP], F32, graph),
                neg=sb("neg", [P, NT], F32, graph),
                negtot=sb("negtot", [P, 1], U32, graph),
            )
            with ExitStack() as sums:
                shared["up"] = sb("up", [P, NT, 20], BF16, sums)
                shared["ones"] = sb("ones", [P, P], F32, sums)
                shared["um"] = sb("um", [P, NT, 20], BF16, sums)
                norm_stage(nc, shared, x_in, ident_in, notid_in, gat_wt_in, gat_a_in, h_dram)
                support_stage(nc, shared, adj_t, s_dram)
            attention_stage(nc, shared, adj_n, gat_w_in, es_dram)
        x1 = sb("x1", [P, NT, D], F32)
        stats = sb("stats", [P, NT, 6], F32)
        gru_stage(nc, ident, x1, stats, x_in, diag_in, gru_w_in, gru_b_in, s_dram, es_dram, h_dram)
        ffn_stage(nc, ident, eps, x1, stats, wr_in, br_in, w1_in, b1_in, w2_in, b2_in,
                  gamma_in, beta_in, out)


def moments(dve, chain, st, mean, var, tmp):
    chain(dve.tensor_tensor(mean, st[:, :, 1], st[:, :, 4], ALU.add))
    chain(dve.tensor_scalar(mean, mean, 0.5, None, ALU.mult))
    chain(dve.tensor_tensor(tmp, st[:, :, 1], st[:, :, 4], ALU.subtract))
    chain(dve.scalar_tensor_tensor(tmp, tmp, 0.25, tmp, ALU.mult, ALU.mult))
    chain(dve.tensor_tensor(var, st[:, :, 2], st[:, :, 5], ALU.add))
    chain(dve.scalar_tensor_tensor(var, var, 1.0 / D, tmp, ALU.mult, ALU.add))


def norm_stage(nc, sh, x_in, ident_in, notid_in, gat_wt_in, gat_a_in, h_dram):
    ident, h_mov, up, um = sh["ident"], sh["h_mov"], sh["up"], sh["um"]
    XC = [0, 6, 12, 18, NT]
    with ExitStack() as ctx:
        def sb(name, shape, dt):
            return ctx.enter_context(nc.sbuf_tensor(name, shape, dt))

        def sem(name):
            return ctx.enter_context(nc.semaphore(name))

        x = sb("n_x", [P, NT, D], F32)
        st = sb("n_st", [P, NT, 6], F32)
        mean = sb("n_mean", [P, NT], F32)
        var = sb("n_var", [P, NT], F32)
        tmp = sb("n_tmp", [P, NT], F32)
        rstd = sb("n_rstd", [P, NT], F32)
        h = sb("n_h", [P, 2, D], F32)
        hT = sb("n_hT", [P, 2, KD, P], F32)
        gwt = sb("n_gwt", [P, HEADS, KD, D], F32)
        ga = sb("n_ga", [P, HEADS, 2, KD], F32)
        wa = sb("n_wa", [P, KD, 2, HEADS], F32)
        r1 = sb("n_r1", [P, NT, NC2], F32)
        psT = ctx.enter_context(nc.psum_tensor("n_psT", [P, 2, 512], F32))
        psV = ctx.enter_context(nc.psum_tensor("n_psV", [P, KD, 2, HEADS], F32))
        psU = ctx.enter_context(nc.psum_tensor("n_psU", [P, 512], F32))
        x_here = [sem(f"n_x_here{c}") for c in range(len(XC) - 1)]
        consts_here = sem("n_consts_here")
        consts_set = sem("n_consts_set")
        dve_step = sem("n_dve_step")
        stats_done = sem("n_stats_done")
        var_done = sem("n_var_done")
        std_done = sem("n_std_done")
        rstd_done = sem("n_rstd_done")
        h_done = sem("n_h_done")
        hi_done = sem("n_hi_done")
        lo_done = sem("n_lo_done")
        tr_done = sem("n_tr_done")
        hT_done = sem("n_hT_done")
        u_done = sem("n_u_done")
        wa_ready = sem("n_wa_ready")
        wa_copied = sem("n_wa_copied")
        hT_out = sem("n_hT_out")
        block = ctx.enter_context(nc.Block())

        @block.sync
        def _(sp):
            for c in range(len(XC) - 1):
                sp.dma_start(x[:, XC[c]:XC[c + 1], :],
                             x_in[XC[c]:XC[c + 1]].rearrange("t p d -> p t d")).then_inc(x_here[c], 16)
        @block.gpsimd
        def _(pool):
            pool.memset(sh["ones"][:], 1.0).then_inc(consts_set, 1)
            pool.memset(sh["eps"][:], LN_EPS).then_inc(consts_set, 1)
            pool.memset(up[:], 0.0).then_inc(consts_set, 1)
            pool.memset(um[:], 1.0).then_inc(consts_set, 1)

        @block.scalar
        def _(act):
            act.dma_start(ident[:], ident_in).then_inc(consts_here, 16)
            act.dma_start(sh["notid"][:], notid_in).then_inc(consts_here, 16)
            act.dma_start(gwt[:], gat_wt_in).then_inc(consts_here, 16)
            act.dma_start(ga[:], gat_a_in).then_inc(consts_here, 16)
            act.wait_ge(wa_ready, 1)
            act.copy(wa[:], psV[:]).then_inc(wa_copied, 1)
            act.wait_ge(var_done, 1)
            act.wait_ge(consts_set, 4)
            act.activation(tmp[:], var[:], ACT.Sqrt, bias=eps_of(sh)).then_inc(std_done, 1)

            def tile(t):
                act.wait_ge(h_done, t + 1)
                act.copy(h_mov[:, t, 0:D], h[:, t % 2]).then_inc(hi_done, 1)
                act.wait_ge(tr_done, t + 1)
                if not isinstance(t, int):
                    act.wait_ge(u_done, t - 1)
                    act.wait_ge(hT_out, 16 * (t - 1))
                act.copy(hT[:, t % 2], psT[:, t % 2, 0:D].rearrange("p (k n) -> p k n", k=KD)).then_inc(hT_done, 1)
                act.wait_ge(hT_done, t + 1)
                if not isinstance(t, int):
                    act.wait_ge(hT_out, 16 * t)
                elif t:
                    act.wait_ge(hT_out, 16)
                act.dma_start(h_dram[:, :, bass.ds(t * P, P)], hT[:, t % 2]).then_inc(hT_out, 16)
            for t in range(2):
                tile(t)
            with act.Fori(2, NT) as t:
                tile(t)
            act.wait_ge(hT_out, 16 * NT)

        @block.vector
        def _(dve):
            chain = Chain(dve, dve_step)
            for c in range(len(XC) - 1):
                dve.wait_ge(x_here[c], 16)
                with dve.Fori(XC[c], XC[c + 1]) as t:
                    dve.bn_stats(st[:, t], x[:, t]).then_inc(stats_done, 1)
            dve.wait_ge(stats_done, NT)
            moments(dve, chain, st, mean[:], var[:], tmp[:])
            dve.nop().then_inc(var_done, 1)
            dve.wait_ge(std_done, 1)
            dve.reciprocal(rstd[:], tmp[:]).then_inc(rstd_done, 1)
            dve.wait_ge(rstd_done, 1)

            def tile(t):
                if not isinstance(t, int):
                    dve.wait_ge(hi_done, t - 1)
                    dve.wait_ge(tr_done, t - 1)
                dve.tensor_scalar(h[:, t % 2], x[:, t], mean[:, bass.ds(t, 1)], rstd[:, bass.ds(t, 1)],
                                  ALU.subtract, ALU.mult).then_inc(h_done, 1)
                dve.wait_ge(hi_done, t + 1)
                dve.tensor_tensor(h_mov[:, t, D:2 * D], h[:, t % 2], h_mov[:, t, 0:D].bitcast(F32),
                                  ALU.subtract).then_inc(lo_done, 1)
            for t in range(2):
                tile(t)
            with dve.Fori(2, NT) as t:
                tile(t)
            dve.wait_ge(u_done, NT)
            dve.wait_ge(consts_set, 4)
            u = psU[:, 0:NT * NC2].rearrange("p (t c) -> p t c", c=NC2)
            chain(dve.tensor_copy(up[:, :, 0:NC2], u))
            chain(dve.tensor_tensor(r1[:], u, up[:, :, 0:NC2], ALU.subtract))
            chain(dve.tensor_copy(up[:, :, NC2:2 * NC2], r1[:]))
            chain(dve.tensor_tensor(r1[:], r1[:], up[:, :, NC2:2 * NC2], ALU.subtract))
            chain(dve.tensor_copy(up[:, :, 2 * NC2:3 * NC2], r1[:]))
            upv = up[:, :, 0:3 * NC2].rearrange("p t (q s h) -> p t q s h", q=3, s=2)
            umv = um[:, :, 0:3 * NC2].rearrange("p t (q s h) -> p t q s h", q=3, s=2)
            for s in range(2):
                for q in range(3):
                    chain(dve.tensor_copy(umv[:, :, q, s, :], upv[:, :, q, 1 - s, :]))

        @block.tensor
        def _(pe):
            pe.wait_ge(consts_here, 64)
            for hd in range(HEADS):
                for m in range(KD):
                    for k in range(KD):
                        last = pe.matmul(psV[:, m, :, hd], gwt[:, hd, k, m * P:(m + 1) * P], ga[:, hd, :, k],
                                         start=(k == 0), stop=(k == KD - 1))
            last.then_inc(wa_ready, 1)
            pe.wait_ge(wa_copied, 1)

            def transposes(u):
                for k in range(KD):
                    last = pe.transpose(psT[:, u, k * P:(k + 1) * P], h[:, u, k * P:(k + 1) * P], ident[:])
                last.then_inc(tr_done, 1)

            def project(t, u):
                for k in range(KD):
                    last = pe.matmul(psU[:, bass.ds(t * NC2, NC2)], hT[:, u, k, :],
                                     wa[:, k].rearrange("p s h -> p (s h)"), start=(k == 0), stop=(k == KD - 1))
                last.then_inc(u_done, 1)
            def pair(i, first):
                for u in range(2):
                    t = 2 * i + u
                    pe.wait_ge(h_done, t + 1)
                    if not first:
                        pe.wait_ge(hT_done, t - 1)
                    transposes(u)
                    pe.wait_ge(hT_done, t + 1)
                    project(t, u)
            pair(0, True)
            with pe.Fori(1, NT // 2) as i:
                pair(i, False)


def eps_of(sh):
    return sh["eps"][:, 0:1]


def support_stage(nc, sh, adj_t, s_dram):
    ident, ones, notid, h_mov, logit = sh["ident"], sh["ones"], sh["notid"], sh["h_mov"], sh["logit"]
    a_ring, up, um, neg = sh["a_ring"], sh["up"], sh["um"], sh["neg"]
    with ExitStack() as ctx:
        def sb(name, shape, dt):
            return ctx.enter_context(nc.sbuf_tensor(name, shape, dt))

        def sem(name):
            return ctx.enter_context(nc.semaphore(name))

        hi = sb("s_hi", [P, 2, NP], F32R)
        lo = sb("s_lo", [P, 2, NP], F32R)
        pos = sb("s_pos", [P, 2, NP], BF16)
        ngt = sb("s_neg", [P, 2, NP], BF16)
        half = sb("s_half", [P, D], F32)
        s = sb("s_s", [P, D], F32)
        sT = sb("s_sT", [P, KD, P], F32)
        e0 = sb("s_e0", [P, NC2], F32)
        e1 = sb("s_e1", [P, NC2], F32)
        negsum = sb("s_negsum", [P, 1], F32)
        psS = ctx.enter_context(nc.psum_tensor("s_psS", [P, 2, 512], F32))
        psE = ctx.enter_context(nc.psum_tensor("s_psE", [P, 2, 512], F32))
        psT = ctx.enter_context(nc.psum_tensor("s_psT", [P, 512], F32))
        psB = ctx.enter_context(nc.psum_tensor("s_psB", [P, 2, 512], F32))
        a_here = sem("s_a_here")
        diag_off = sem("s_diag_off")
        hi_done = sem("s_hi_done")
        lo_done = sem("s_lo_done")
        masks_done = sem("s_masks_done")
        mains_done = sem("s_mains_done")
        half_done = sem("s_half_done")
        s_done = sem("s_s_done")
        sum_done = sem("s_sum_done")
        e_done = sem("s_e_done")
        posts_done = sem("s_posts_done")
        sT_done = sem("s_sT_done")
        bcast_done = sem("s_bcast_done")
        sT_out = sem("s_sT_out")
        neg_here = sem("s_neg_here")
        neg_all = sem("s_neg_all")
        block = ctx.enter_context(nc.Block())
        LASTP = NT // 2 - 1

        @block.sync
        def _(sp):
            sp.dma_start(a_ring[:, 0], adj_t[0]).then_inc(a_here, 16)
            sp.wait_ge(a_here, 16)
            sp.dma_start(a_ring[:, 1], adj_t[1]).then_inc(a_here, 16)

        @block.gpsimd
        def _(pool):
            def store(t):
                pool.wait_ge(sT_done, t + 1)
                pool.dma_start(s_dram[:, :, bass.ds(t * P, P)], sT[:]).then_inc(sT_out, 16)
                pool.wait_ge(sT_out, 16 * (t + 1))
            with pool.Fori(0, NT) as t:
                store(t)

        @block.scalar
        def _(act):
            def main(i, u, first):
                t = 2 * i + u
                act.wait_ge(diag_off, t + 1)
                if not first:
                    act.wait_ge(mains_done, t - 1)
                act.copy(hi[:, u], a_ring[:, u]).then_inc(hi_done, 1)

            def post(t, u):
                act.wait_ge(mains_done, t + 1)
                if not isinstance(t, int) or t:
                    act.wait_ge(s_done, t)
                act.copy(half[:], psS[:, u, D:2 * D]).then_inc(half_done, 1)
                act.wait_ge(posts_done, t + 1)
                if not isinstance(t, int) or t:
                    act.wait_ge(sT_out, 16 * t)
                act.copy(sT[:], psT[:, 0:D].rearrange("p (k n) -> p k n", k=KD)).then_inc(sT_done, 1)
                for c in range(2):
                    last = act.copy(logit[:, c * HEADS:(c + 1) * HEADS, bass.ds(t * P, P)],
                                    psB[:, c, 0:HEADS * P].rearrange("p (c n) -> p c n", c=HEADS))
                last.then_inc(bcast_done, 1)
            def load(t, u):
                act.wait_ge(a_here, 16 * t)
                act.wait_ge(lo_done, t - 1)
                act.wait_ge(masks_done, t - 1)
                act.dma_start(a_ring[:, u], adj_t[t]).then_inc(a_here, 16)
            main(0, 0, True)
            load(2, 0)
            main(0, 1, True)
            load(3, 1)
            post(0, 0)
            with act.Fori(1, NT // 2 - 1) as i:
                main(i, 0, False)
                post(2 * i - 1, 1)
                load(2 * i + 2, 0)
                main(i, 1, False)
                post(2 * i, 0)
                load(2 * i + 3, 1)
            main(NT // 2 - 1, 0, False)
            post(NT - 3, 1)
            main(NT // 2 - 1, 1, False)
            post(NT - 2, 0)
            post(NT - 1, 1)

        @block.vector
        def _(dve):
            def main(i, u, first):
                t = 2 * i + u
                dve.wait_ge(a_here, 16 * (t + 1))
                d = a_ring[:, u, bass.ds(t * P, P)]
                dve.tensor_tensor(d, d, notid[:], ALU.mult).then_inc(diag_off, 1)
                dve.wait_ge(diag_off, t + 1)
                if not first:
                    dve.wait_ge(mains_done, t - 1)
                dve.tensor_scalar(pos[:, u], a_ring[:, u], 0.0, None, ALU.is_gt)
                dve.tensor_scalar(ngt[:, u], a_ring[:, u], 0.0, None, ALU.is_lt).then_inc(masks_done, 1)
                dve.wait_ge(hi_done, t + 1)
                dve.tensor_tensor(lo[:, u], a_ring[:, u], hi[:, u].bitcast(F32), ALU.subtract).then_inc(lo_done, 1)

            def post(t, u):
                dve.wait_ge(mains_done, t + 1)
                if not isinstance(t, int) or t:
                    dve.wait_ge(posts_done, t)
                dve.tensor_reduce(e0[:], psE[:, u, 0:3 * NC2].rearrange("p (q c) -> p c q", q=3), AX.X,
                                  ALU.add).then_inc(sum_done, 1)
                dve.tensor_copy(neg[:, bass.ds(t, 1)], psE[:, u, 3 * NC2:3 * NC2 + 1])
                dve.wait_ge(sum_done, t + 1)
                dve.scalar_tensor_tensor(e1[:], e0[:], ALPHA, e0[:], ALU.mult, ALU.max).then_inc(e_done, 1)
                dve.wait_ge(half_done, t + 1)
                dve.tensor_tensor(s[:], psS[:, u, 0:D], half[:], ALU.add).then_inc(s_done, 1)
            main(0, 0, True)
            main(0, 1, True)
            post(0, 0)
            with dve.Fori(1, NT // 2) as i:
                main(i, 0, False)
                post(2 * i - 1, 1)
                main(i, 1, False)
                post(2 * i, 0)
            post(NT - 1, 1)
            dve.wait_ge(e_done, NT)
            dve.tensor_reduce(negsum[:], neg[:], AX.X, ALU.add).then_inc(neg_here, 1)
            dve.wait_ge(neg_all, 1)
            dve.tensor_copy(sh["negtot"][:], psT[:, 256:257])

        @block.tensor
        def _(pe):
            def main(i, u, first):
                t = 2 * i + u
                if not first:
                    pe.wait_ge(s_done, t - 1)
                    pe.wait_ge(e_done, t - 1)
                pe.wait_ge(masks_done, t + 1)
                for j in range(NT):
                    b = slice(j * P, (j + 1) * P)
                    pe.matmul(psE[:, u, 0:19], pos[:, u, b], up[:, j, 0:19], start=(j == 0), stop=False)
                    pe.matmul(psE[:, u, 0:19], ngt[:, u, b], um[:, j, 0:19], start=False, stop=(j == NT - 1))
                pe.wait_ge(hi_done, t + 1)
                pe.wait_ge(lo_done, t + 1)
                for j in range(NT):
                    b = slice(j * P, (j + 1) * P)
                    pe.matmul(psS[:, u, :], hi[:, u, b], h_mov[:, j, :], start=(j == 0), stop=False)
                    last = pe.matmul(psS[:, u, 0:D], lo[:, u, b], h_mov[:, j, 0:D], start=False,
                                     stop=(j == NT - 1))
                last.then_inc(mains_done, 1)

            def post(t):
                pe.wait_ge(e_done, t + 1)
                if not isinstance(t, int) or t:
                    pe.wait_ge(bcast_done, t)
                for c in range(NC2):
                    pe.matmul(psB[:, c // HEADS, (c % HEADS) * P:(c % HEADS + 1) * P],
                              e1[:, c:c + 1].to_broadcast([P, P]), ident[:], start=True, stop=True)
                pe.wait_ge(s_done, t + 1)
                for k in range(KD):
                    last = pe.transpose(psT[:, k * P:(k + 1) * P], s[:, k * P:(k + 1) * P], ident[:])
                last.then_inc(posts_done, 1)
            main(0, 0, True)
            main(0, 1, True)
            post(0)
            with pe.Fori(1, NT // 2) as i:
                main(i, 0, False)
                post(2 * i - 1)
                main(i, 1, False)
                post(2 * i)
            post(NT - 1)
            pe.wait_ge(neg_here, 1)
            pe.wait_ge(bcast_done, NT)
            pe.matmul(psT[:, 256:257], ones[:], negsum[:], start=True, stop=True).then_inc(neg_all, 1)


def attention_stage(nc, sh, adj_n, gat_w_in, es_dram):
    ident, notid, h_mov, logit, a_ring = sh["ident"], sh["notid"], sh["h_mov"], sh["logit"], sh["a_ring"]
    LT = 3
    WR = 4
    TR = 3
    SPI = 2 * HEADS
    GPI = SPI * NG
    STEPS = NT * HEADS
    ITERS = NT // 2
    assert GPI % WR == 0 and GPI % TR == 0
    with ExitStack() as ctx:
        def sb(name, shape, dt):
            return ctx.enter_context(nc.sbuf_tensor(name, shape, dt))

        def sem(name):
            return ctx.enter_context(nc.semaphore(name))

        w_nat = sb("a_w", [P, 3, NP], F32)
        mask = sb("a_mask", [P, NP], BF16)
        isneg = sb("a_isneg", [P, NP], U8)
        wt_hi = sb("a_wt_hi", [P, WR, GB * P], F32R)
        wt_lo = sb("a_wt_lo", [P, WR, GB * P], F32R)
        gw = sb("a_gw", [P, HEADS, KD, 2 * D], F32R)
        gw_raw = w_nat[:, 2, 0:HEADS * KD * D].rearrange("p (h k d) -> p h k d", h=HEADS, k=KD)
        mx = sb("a_mx", [P, SPI], F32)
        carrier = sb("a_carrier", [P, SPI], F32)
        nmx = sb("a_nmx", [P, SPI], F32)
        ssum = sb("a_ssum", [P, SPI], F32)
        s3 = sb("a_s3", [P, SPI], F32)
        rs = sb("a_rs", [P, SPI], F32)
        ghalf = sb("a_ghalf", [P, D], F32)
        g = sb("a_g", [P, D], F32)
        gT_hi = sb("a_gT_hi", [P, D], F32R)
        gT_lo = sb("a_gT_lo", [P, D], F32R)
        ehalf = ghalf
        es = g
        esT = sb("a_esT", [P, KD, P], F32)
        psW = ctx.enter_context(nc.psum_tensor("a_psW", [P, TR, 512], F32))
        psO = ctx.enter_context(nc.psum_tensor("a_psO", [P, 2, 512], F32))
        psG = ctx.enter_context(nc.psum_tensor("a_psG", [P, 512], F32))
        psX = ctx.enter_context(nc.psum_tensor("a_psX", [P, 512], F32))
        a_here = sem("a_a_here")
        gw_here = sem("a_gw_here")
        gw_hi = sem("a_gw_hi")
        gw_lo = sem("a_gw_lo")
        diag_off = sem("a_diag_off")
        mask_done = sem("a_mask_done")
        logits_done = sem("a_logits_done")
        nmx_done = sem("a_nmx_done")
        exp_done = sem("a_exp_done")
        w_pool = sem("a_w_pool")
        w_dve = sem("a_w_dve")
        tr_done = sem("a_tr_done")
        hi_done = sem("a_hi_done")
        lo_done = sem("a_lo_done")
        mm_done = sem("a_mm_done")
        rs_step = sem("a_rs_step")
        rs_done = sem("a_rs_done")
        ghalf_done = sem("a_ghalf_done")
        g_done = sem("a_g_done")
        gt_done = sem("a_gt_done")
        gT_hi_done = sem("a_gT_hi_done")
        gT_lo_done = sem("a_gT_lo_done")
        proj_done = sem("a_proj_done")
        ehalf_done = sem("a_ehalf_done")
        es_done = sem("a_es_done")
        est_done = sem("a_est_done")
        esT_done = sem("a_esT_done")
        esT_out = sem("a_esT_out")
        rare = sem("a_rare")
        block = ctx.enter_context(nc.Block())

        def at_least(eng, s, v):
            if not isinstance(v, int) or v > 0:
                eng.wait_ge(s, v)

        @block.sync
        def _(sp):
            sp.dma_start(a_ring[:, 0], adj_n[0]).then_inc(a_here, 16)
            sp.wait_ge(a_here, 16)
            sp.dma_start(a_ring[:, 1], adj_n[1]).then_inc(a_here, 16)

        @block.gpsimd
        def _(pool):
            def weights(i, k):
                s = SPI * i + k
                if k % HEADS == HEADS - 1:
                    return
                pool.wait_ge(exp_done, s + 1)
                w = w_nat[:, k % 3]
                pool.tensor_tensor(w, w, a_ring[:, k // HEADS], ALU.mult).then_inc(w_pool, 1)

            def store(t):
                pool.wait_ge(esT_done, t + 1)
                pool.dma_start(es_dram[:, :, bass.ds(t * P, P)], esT[:]).then_inc(esT_out, 16)

            def body(i):
                for k in range(SPI):
                    weights(i, k)
                    if k == 2 and (not isinstance(i, int) or i):
                        store(2 * i - 1)
                    if k == 5:
                        store(2 * i)
            body(0)
            with pool.Fori(1, ITERS) as i:
                body(i)
            store(NT - 1)
            pool.wait_ge(esT_out, 16 * NT)

        @block.scalar
        def _(act):
            act.dma_start(gw_raw, gat_w_in).then_inc(gw_here, 16)
            act.wait_ge(gw_here, 16)
            act.copy(gw[:, :, :, 0:D], gw_raw).then_inc(gw_hi, 1)

            def exps(i, k):
                s = SPI * i + k
                act.wait_ge(nmx_done, s + 1)
                w = w_nat[:, k % 3]
                at_least(act, rs_done, s - SPI + 1)
                act.activation(w, w, ACT.Exp, bias=nmx[:, k % SPI:k % SPI + 1],
                               accum_out=ssum[:, k % SPI:k % SPI + 1]).then_inc(exp_done, 1)

            def hi_group(i, k, gi):
                q = GPI * i + k * NG + gi
                n = GSIZE[gi] * P
                act.wait_ge(tr_done, q + 1)
                at_least(act, mm_done, q - WR + 1)
                act.copy(wt_hi[:, (k * NG + gi) % WR, 0:n],
                         psW[:, (k * NG + gi) % TR, 0:n]).then_inc(hi_done, 1)

            def scaled_half(s, k, i=None):
                act.wait_ge(rs_done, s + 1)
                act.wait_ge(mm_done, NG * (s + 1))
                at_least(act, g_done, s)
                if k % HEADS == 0:
                    at_least(act, es_done, 2 * i + k // HEADS)
                act.mul(ghalf[:], psO[:, k % 2, D:2 * D], rs[:, k:k + 1]).then_inc(ghalf_done, 1)

            def gT_half(s, k):
                act.wait_ge(gt_done, s + 1)
                at_least(act, proj_done, s)
                act.copy(gT_hi[:], psG[:, 0:D]).then_inc(gT_hi_done, 1)

            def es_half(t):
                act.wait_ge(proj_done, HEADS * (t + 1))
                act.wait_ge(g_done, HEADS * (t + 1))
                act.copy(ehalf[:], psX[:, D:2 * D]).then_inc(ehalf_done, 1)

            def esT_copy(t):
                act.wait_ge(est_done, t + 1)
                at_least(act, esT_out, 16 * t)
                act.copy(esT[:], psG[:, 0:D].rearrange("p (k n) -> p k n", k=KD)).then_inc(esT_done, 1)

            def body(i, last):
                for k in range(SPI):
                    s = SPI * i + k
                    if not (last and k == SPI - 1):
                        exps(i + (k + 1) // SPI, (k + 1) % SPI)
                    hi_group(i, k, 0)
                    if k % HEADS == 1 and (k > 1 or not isinstance(i, int) or i):
                        esT_copy(2 * i + k // HEADS - 1)
                    hi_group(i, k, 1)
                    before = k > 0 or not isinstance(i, int) or i > 0
                    if before:
                        scaled_half(s - 1, (k - 1) % SPI, i)
                    hi_group(i, k, 2)
                    if before:
                        gT_half(s - 1, (k - 1) % SPI)
                    hi_group(i, k, 3)
                    hi_group(i, k, 4)
                    if before and k % HEADS == 0:
                        es_half(2 * i + k // HEADS - 1)
                    hi_group(i, k, 5)
                    if k % HEADS == HEADS - 1 and not last:
                        load(2 * i + k // HEADS + 2, k // HEADS)

            def load(t, u):
                act.wait_ge(a_here, 16 * t)
                act.wait_ge(w_pool, 2 * (t - 1))
                act.wait_ge(w_dve, t - 1)
                act.dma_start(a_ring[:, u], adj_n[t]).then_inc(a_here, 16)
            exps(0, 0)
            body(0, False)
            with act.Fori(1, ITERS - 1) as i:
                body(i, False)
            body(ITERS - 1, True)
            scaled_half(STEPS - 1, SPI - 1)
            gT_half(STEPS - 1, SPI - 1)
            es_half(NT - 1)
            esT_copy(NT - 1)

        @block.vector
        def _(dve):
            has_negatives = dve.value_load(sh["negtot"][0:1, 0:1])
            dve.wait_ge(gw_hi, 1)
            dve.tensor_tensor(gw[:, :, :, D:2 * D], gw_raw, gw[:, :, :, 0:D].bitcast(F32),
                              ALU.subtract).then_inc(gw_lo, 1)
            dve.wait_ge(gw_lo, 1)

            def masks(i, u):
                t = 2 * i + u
                dve.wait_ge(a_here, 16 * (t + 1))
                d = a_ring[:, u, bass.ds(t * P, P)]
                dve.tensor_tensor(d, d, notid[:], ALU.mult).then_inc(diag_off, 1)
                dve.wait_ge(diag_off, t + 1)
                at_least(dve, logits_done, HEADS * t)
                dve.tensor_scalar(mask[:], a_ring[:, u], 0.0, NEG_INF, ALU.is_equal, ALU.mult).then_inc(mask_done, 1)
                dve.wait_ge(mask_done, t + 1)

            def logits(i, k):
                s = SPI * i + k
                if k % HEADS == 0:
                    masks(i, k // HEADS)
                hd = k % HEADS
                w = w_nat[:, k % 3]
                at_least(dve, tr_done, NG * (s - 2))
                at_least(dve, exp_done, s - SPI + 1)
                dve.memset(carrier[:, k:k + 1], 0.0)
                dve.tensor_tensor_reduce(w, mask[:], logit[:, hd], 1.0, -3.0e38, ALU.add, ALU.max,
                                         mx[:, k:k + 1]).then_inc(logits_done, 1)
                with dve.If(has_negatives > 0):
                    dve.tensor_scalar(isneg[:], a_ring[:, k // HEADS], 0.0, None, ALU.is_lt)
                    dve.drain()
                    dve.copy_predicated(w, isneg[:], logit[:, HEADS + hd])
                    dve.drain()
                    dve.tensor_reduce(mx[:, k:k + 1], w, AX.X, ALU.max)
                    dve.drain()
                dve.wait_ge(logits_done, s + 1)
                dve.tensor_scalar(nmx[:, k:k + 1], mx[:, k:k + 1], -1.0, None, ALU.mult).then_inc(nmx_done, 1)

            def weights(i, k):
                s = SPI * i + k
                if k % HEADS != HEADS - 1:
                    return
                dve.wait_ge(exp_done, s + 1)
                w = w_nat[:, k % 3]
                dve.tensor_tensor(w, w, a_ring[:, k // HEADS], ALU.mult).then_inc(w_dve, 1)

            def lo_group(i, k, gi):
                q = GPI * i + k * NG + gi
                n = GSIZE[gi] * P
                slot = (k * NG + gi) % WR
                dve.wait_ge(hi_done, q + 1)
                dve.tensor_tensor(wt_lo[:, slot, 0:n], psW[:, (k * NG + gi) % TR, 0:n],
                                  wt_hi[:, slot, 0:n].bitcast(F32), ALU.subtract).then_inc(lo_done, 1)

            def scale(i, k):
                s = SPI * i + k
                dve.wait_ge(exp_done, s + 1)
                at_least(dve, g_done, s - SPI + 1)
                dve.tensor_scalar(s3[:, k:k + 1], ssum[:, k:k + 1], float(HEADS), None, ALU.mult).then_inc(rs_step, 1)
                dve.wait_ge(rs_step, s + 1)
                dve.reciprocal(rs[:, k:k + 1], s3[:, k:k + 1]).then_inc(rs_done, 1)

            def gather(s, k, i=None):
                dve.wait_ge(ghalf_done, s + 1)
                at_least(dve, gt_done, s)
                if k % HEADS == 0:
                    at_least(dve, est_done, 2 * i + k // HEADS)
                dve.scalar_tensor_tensor(g[:], psO[:, k % 2, 0:D], rs[:, k:k + 1], ghalf[:],
                                         ALU.mult, ALU.add).then_inc(g_done, 1)

            def gT_half(s):
                dve.wait_ge(gT_hi_done, s + 1)
                dve.tensor_tensor(gT_lo[:], psG[:, 0:D], gT_hi[:].bitcast(F32), ALU.subtract).then_inc(gT_lo_done, 1)

            def es_sum(t):
                dve.wait_ge(ehalf_done, t + 1)
                dve.tensor_tensor(es[:], psX[:, 0:D], ehalf[:], ALU.add).then_inc(es_done, 1)

            def body(i, last):
                for k in range(SPI):
                    s = SPI * i + k
                    if not (last and k >= SPI - 2):
                        logits(i + (k + 2) // SPI, (k + 2) % SPI)
                    lo_group(i, k, 0)
                    lo_group(i, k, 1)
                    before = k > 0 or not isinstance(i, int) or i > 0
                    if before:
                        gather(s - 1, (k - 1) % SPI, i)
                    lo_group(i, k, 2)
                    if before:
                        gT_half(s - 1)
                    lo_group(i, k, 3)
                    if not (last and k == SPI - 1):
                        scale(i + (k + 1) // SPI, (k + 1) % SPI)
                        weights(i + (k + 1) // SPI, (k + 1) % SPI)
                    lo_group(i, k, 4)
                    if before and k % HEADS == 0:
                        es_sum(2 * i + k // HEADS - 1)
                    lo_group(i, k, 5)
            logits(0, 0)
            logits(0, 1)
            scale(0, 0)
            body(0, False)
            with dve.Fori(1, ITERS - 1) as i:
                body(i, False)
            body(ITERS - 1, True)
            gather(STEPS - 1, SPI - 1)
            gT_half(STEPS - 1)
            es_sum(NT - 1)

        @block.tensor
        def _(pe):
            def transposes(i, k, gi):
                s = SPI * i + k
                q = GPI * i + k * NG + gi
                if gi == 0:
                    t = 2 * i + k // HEADS
                    if k % HEADS == HEADS - 1:
                        pe.wait_ge(w_dve, t + 1)
                    else:
                        pe.wait_ge(w_pool, 2 * t + k % HEADS + 1)
                bank = (k * NG + gi) % TR
                for b in range(GSIZE[gi]):
                    j = gi * GB + b
                    last = pe.transpose(psW[:, bank, b * P:(b + 1) * P], w_nat[:, k % 3, j * P:(j + 1) * P], ident[:])
                last.then_inc(tr_done, 1)

            def products(i, k, gi):
                q = GPI * i + k * NG + gi
                s = SPI * i + k
                slot = (k * NG + gi) % WR
                pe.wait_ge(lo_done, q + 1)
                if gi == 0:
                    at_least(pe, g_done, s - 1)
                for b in range(GSIZE[gi]):
                    j = gi * GB + b
                    c = slice(b * P, (b + 1) * P)
                    pe.matmul(psO[:, k % 2, :], wt_hi[:, slot, c], h_mov[:, j, :], start=(j == 0), stop=False)
                    last = pe.matmul(psO[:, k % 2, 0:D], wt_lo[:, slot, c], h_mov[:, j, 0:D], start=False,
                                     stop=(j == NT - 1))
                last.then_inc(mm_done, 1)

            def g_transposes(s, k, i=None):
                pe.wait_ge(g_done, s + 1)
                at_least(pe, gT_lo_done, s)
                if k % HEADS == 0:
                    at_least(pe, esT_done, 2 * i + k // HEADS)
                for c in range(KD):
                    last = pe.transpose(psG[:, c * P:(c + 1) * P], g[:, c * P:(c + 1) * P], ident[:])
                last.then_inc(gt_done, 1)

            def project(s, k, i=None):
                hd = k % HEADS
                pe.wait_ge(gT_lo_done, s + 1)
                if hd == 0:
                    at_least(pe, es_done, 2 * i + k // HEADS)
                for c in range(KD):
                    pe.matmul(psX[:], gT_hi[:, c * P:(c + 1) * P], gw[:, hd, c, :],
                              start=(hd == 0 and c == 0), stop=False)
                    last = pe.matmul(psX[:, 0:D], gT_lo[:, c * P:(c + 1) * P], gw[:, hd, c, 0:D],
                                     start=False, stop=(hd == HEADS - 1 and c == KD - 1))
                last.then_inc(proj_done, 1)

            def es_transposes(t):
                pe.wait_ge(es_done, t + 1)
                for c in range(KD):
                    last = pe.transpose(psG[:, c * P:(c + 1) * P], es[:, c * P:(c + 1) * P], ident[:])
                last.then_inc(est_done, 1)

            def body(i, last):
                for k in range(SPI):
                    s = SPI * i + k
                    before = k > 0 or not isinstance(i, int) or i > 0
                    for gi in range(NG):
                        products(i, k, gi)
                        ahead = k * NG + gi + LT
                        if not (last and ahead >= GPI):
                            transposes(i + ahead // GPI, ahead % GPI // NG, ahead % NG)
                        if gi == 1 and before:
                            g_transposes(s - 1, (k - 1) % SPI, i)
                        if gi == 3 and before:
                            project(s - 1, (k - 1) % SPI, i)
                        if gi == 5 and before and k % HEADS == 0:
                            es_transposes(2 * i + k // HEADS - 1)
            pe.wait_ge(gw_lo, 1)
            for gi in range(LT):
                transposes(0, 0, gi)
            body(0, False)
            with pe.Fori(1, ITERS - 1) as i:
                body(i, False)
            body(ITERS - 1, True)
            g_transposes(STEPS - 1, SPI - 1)
            project(STEPS - 1, SPI - 1)
            es_transposes(NT - 1)


def gru_stage(nc, ident, x1, stats, x_in, diag_in, gru_w_in, gru_b_in, s_dram, es_dram, h_dram):
    WIDTHS = [CH] * (NCH - 1) + [GSIZE[LAST] * P]
    UNITS = 4
    with ExitStack() as ctx:
        def sb(name, shape, dt):
            return ctx.enter_context(nc.sbuf_tensor(name, shape, dt))

        def sem(name):
            return ctx.enter_context(nc.semaphore(name))

        x = sb("r_x", [P, NT, D], F32)
        diag = sb("r_diag", [P, NT], F32)
        w_raw = sb("r_w_raw", [P, 2, KD, 3 * D], F32)
        w_hi = sb("r_w_hi", [P, 4, KD, 3 * D], F32R)
        w_lo = sb("r_w_lo", [P, 4, KD, 3 * D], F32R)
        b = sb("r_b", [P, 4, 3 * KD], F32)
        brz = sb("r_brz", [P, 2, 2 * KD], F32)
        raw = sb("r_raw", [P, 2, 3, KD, CH], F32)
        v_hi = sb("r_hi", [P, 2, 3, KD, CH], F32R)
        v_lo = sb("r_lo", [P, 2, 3, KD, CH], F32R)
        r = sb("r_r", [P, 2, CH], F32)
        z = sb("r_z", [P, 2, CH], F32)
        t1 = sb("r_t1", [P, CH], F32)
        t2 = sb("r_t2", [P, CH], F32)
        n = sb("r_n", [P, CH], F32)
        t3 = sb("r_t3", [P, CH], F32)
        t4 = sb("r_t4", [P, CH], F32)
        total = sb("r_total", [P, KD, CH], F32)
        psR = ctx.enter_context(nc.psum_tensor("r_psR", [P, 2, 512], F32))
        psZ = ctx.enter_context(nc.psum_tensor("r_psZ", [P, 2, 512], F32))
        psH = ctx.enter_context(nc.psum_tensor("r_psH", [P, 512], F32))
        psN = ctx.enter_context(nc.psum_tensor("r_psN", [P, 512], F32))
        psX = ctx.enter_context(nc.psum_tensor("r_psX", [P, 2, 512], F32))
        consts_here = sem("r_consts_here")
        x_here = sem("r_x_here")
        w_here = [sem(f"r_w_here{g}") for g in range(4)]
        w_hi_done = sem("r_w_hi_done")
        w_lo_done = sem("r_w_lo_done")
        brz_done = sem("r_brz_done")
        raw_here = sem("r_raw_here")
        v_hi_done = sem("r_v_hi_done")
        v_lo_done = sem("r_v_lo_done")
        r_ready = sem("r_r_ready")
        z_ready = sem("r_z_ready")
        h_ready = sem("r_h_ready")
        n_ready = sem("r_n_ready")
        r_done = sem("r_r_done")
        z_done = sem("r_z_done")
        t_step = sem("r_t_step")
        t2_done = sem("r_t2_done")
        n_done = sem("r_n_done")
        mix_step = sem("r_mix_step")
        mix_done = sem("r_mix_done")
        tr_done = sem("r_tr_done")
        x1_done = sem("r_x1_done")
        st_done = sem("r_st_done")
        block = ctx.enter_context(nc.Block())

        def positive(eng, s, v):
            if not isinstance(v, int) or v > 0:
                eng.wait_ge(s, v)

        def chunks(eng, body):
            body(0, WIDTHS[0])
            with eng.Fori(1, LAST) as c:
                body(c, CH)
            body(LAST, WIDTHS[LAST])

        @block.sync
        def _(sp):
            for g in range(4):
                if g >= 2:
                    sp.wait_ge(w_lo_done, g - 1)
                sp.dma_start(w_raw[:, g % 2], gru_w_in[g]).then_inc(w_here[g], 16)
                if g == 1:
                    sp.dma_start(b[:], gru_b_in).then_inc(consts_here, 16)
                    sp.dma_start(diag[:], diag_in).then_inc(consts_here, 16)
                    sp.dma_start(x[:], x_in.rearrange("t p d -> p t d")).then_inc(x_here, 16)

        @block.scalar
        def _(act):
            def load(c, w):
                positive(act, raw_here, 48 * c)
                positive(act, mix_done, UNITS * (c - 1))
                for m, src in enumerate((s_dram, es_dram, h_dram)):
                    act.dma_start(raw[:, c % 2, m, :, 0:w], src[:, :, bass.ds(c * CH, w)]).then_inc(raw_here, 16)

            def split(c, w):
                act.wait_ge(raw_here, 48 * (c + 1))
                positive(act, n_ready, UNITS * (c - 1))
                for m in range(3):
                    act.copy(v_hi[:, c % 2, m, :, 0:w], raw[:, c % 2, m, :, 0:w]).then_inc(v_hi_done, 1)

            def unit(c, u, w):
                g, f = u // KD, u % KD
                k = UNITS * c + u
                act.wait_ge(r_ready, k + 1)
                positive(act, mix_done, k - 1)
                act.activation(r[:, u % 2, 0:w], psR[:, u % 2, 0:w], ACT.Sigmoid,
                               bias=brz[:, g, f:f + 1]).then_inc(r_done, 1)
                act.wait_ge(z_ready, k + 1)
                act.activation(z[:, u % 2, 0:w], psZ[:, u % 2, 0:w], ACT.Sigmoid,
                               bias=brz[:, g, KD + f:KD + f + 1]).then_inc(z_done, 1)
                act.wait_ge(t2_done, k + 1)
                positive(act, mix_done, k)
                act.activation(n[:, 0:w], t2[:, 0:w], ACT.Tanh,
                               bias=b[:, 2 * g, 2 * KD + f:2 * KD + f + 1]).then_inc(n_done, 1)

            load(0, WIDTHS[0])
            for g in range(4):
                act.wait_ge(w_here[g], 16)
                act.copy(w_hi[:, g], w_raw[:, g % 2]).then_inc(w_hi_done, 1)
            load(1, WIDTHS[1])
            act.wait_ge(brz_done, 1)
            split(0, WIDTHS[0])

            def body(c, w):
                first = isinstance(c, int) and c == 0
                last = isinstance(c, int) and c == LAST
                for u in range(UNITS):
                    unit(c, u, w)
                    if u == 1 and not last:
                        split_next(c)
                if not last:
                    load_after(c)

            def split_next(c):
                if isinstance(c, int):
                    split(c + 1, WIDTHS[c + 1])
                else:
                    split(c + 1, CH)

            def load_after(c):
                if isinstance(c, int):
                    load(c + 2, WIDTHS[c + 2])
                else:
                    load(c + 2, CH)
            body(0, WIDTHS[0])
            with act.Fori(1, LAST - 2) as c:
                body(c, CH)
            for c in (LAST - 2, LAST - 1, LAST):
                for u in range(UNITS):
                    unit(c, u, WIDTHS[c])
                    if u == 1 and c < LAST:
                        split(c + 1, WIDTHS[c + 1])
                if c + 2 <= LAST:
                    load(c + 2, WIDTHS[c + 2])

        @block.vector
        def _(dve):
            dve.wait_ge(consts_here, 32)
            for g in range(2):
                last = dve.tensor_tensor(brz[:, g], b[:, 2 * g, 0:2 * KD], b[:, 2 * g + 1, 0:2 * KD], ALU.add)
            last.then_inc(brz_done, 1)
            for g in range(4):
                dve.wait_ge(w_hi_done, g + 1)
                dve.tensor_tensor(w_lo[:, g], w_raw[:, g % 2], w_hi[:, g].bitcast(F32),
                                  ALU.subtract).then_inc(w_lo_done, 1)

            def split(c, w):
                for m in range(3):
                    dve.wait_ge(v_hi_done, 3 * c + m + 1)
                    dve.tensor_tensor(v_lo[:, c % 2, m, :, 0:w], raw[:, c % 2, m, :, 0:w],
                                      v_hi[:, c % 2, m, :, 0:w].bitcast(F32), ALU.subtract).then_inc(v_lo_done, 1)

            def unit(c, u, w):
                g, f = u // KD, u % KD
                k = UNITS * c + u
                dve.wait_ge(r_done, k + 1)
                dve.wait_ge(h_ready, k + 1)
                dve.scalar_tensor_tensor(t1[:, 0:w], psH[:, 0:w], b[:, 2 * g + 1, 2 * KD + f:2 * KD + f + 1],
                                         r[:, u % 2, 0:w], ALU.add, ALU.mult).then_inc(t_step, 1)
                dve.wait_ge(t_step, k + 1)
                dve.wait_ge(n_ready, k + 1)
                positive(dve, n_done, k)
                dve.tensor_tensor(t2[:, 0:w], psN[:, 0:w], t1[:, 0:w], ALU.add).then_inc(t2_done, 1)
                dve.wait_ge(n_done, k + 1)
                dve.wait_ge(z_done, k + 1)
                hraw = raw[:, c % 2, 2, f, 0:w]
                dve.tensor_tensor(t3[:, 0:w], hraw, n[:, 0:w], ALU.subtract).then_inc(mix_step, 1)
                dve.wait_ge(mix_step, 3 * k + 1)
                dve.tensor_tensor(t4[:, 0:w], t3[:, 0:w], z[:, u % 2, 0:w], ALU.mult).then_inc(mix_step, 1)
                dve.wait_ge(mix_step, 3 * k + 2)
                if g == 0:
                    dve.tensor_tensor(total[:, f, 0:w], n[:, 0:w], t4[:, 0:w], ALU.add).then_inc(mix_step, 1)
                    dve.wait_ge(mix_step, 3 * k + 3)
                    dve.nop().then_inc(mix_done, 1)
                else:
                    dve.tensor_tensor(t3[:, 0:w], n[:, 0:w], t4[:, 0:w], ALU.add).then_inc(mix_step, 1)
                    dve.wait_ge(mix_step, 3 * k + 3)
                    dve.tensor_tensor(total[:, f, 0:w], total[:, f, 0:w], t3[:, 0:w], ALU.add).then_inc(mix_done, 1)

            def finish(c, tiles):
                for q in range(tiles):
                    t = GB * c + q
                    dve.wait_ge(tr_done, t + 1)
                    dve.scalar_tensor_tensor(x1[:, t], psX[:, q % 2, 0:D], diag[:, bass.ds(t, 1)], x[:, t],
                                             ALU.mult, ALU.add).then_inc(x1_done, 1)
                    dve.wait_ge(x1_done, t + 1)
                    dve.bn_stats(stats[:, t], x1[:, t]).then_inc(st_done, 1)

            split(0, WIDTHS[0])
            dve.wait_ge(x_here, 16)

            def body(c, w, nxt):
                if not (isinstance(c, int) and c == 0):
                    finish(c - 1, GB)
                for u in range(UNITS):
                    unit(c, u, w)
                    if u == 1 and nxt:
                        split(c + 1, nxt)
            body(0, WIDTHS[0], WIDTHS[1])
            with dve.Fori(1, LAST - 1) as c:
                body(c, CH, CH)
            body(LAST - 1, WIDTHS[LAST - 1], WIDTHS[LAST])
            body(LAST, WIDTHS[LAST], 0)
            finish(LAST, GSIZE[LAST])

        @block.tensor
        def _(pe):
            pe.wait_ge(w_lo_done, 4)

            def gate(ps, col, sources, c, w):
                terms = [(g, m, k, a, v) for g, m in sources for k in range(KD)
                         for a, v in ((w_hi, v_hi), (w_hi, v_lo), (w_lo, v_hi))]
                for j, (g, m, k, a, v) in enumerate(terms):
                    last = pe.matmul(ps[:, 0:w], a[:, g, k, col:col + P], v[:, c % 2, m, k, 0:w],
                                     start=(j == 0), stop=(j == len(terms) - 1))
                return last

            def unit(c, u, w):
                g, f = u // KD, u % KD
                k = UNITS * c + u
                ih, hh = (2 * g, g), (2 * g + 1, 2)
                positive(pe, r_done, k - 1)
                gate(psR[:, u % 2], f * P, (ih, hh), c, w).then_inc(r_ready, 1)
                positive(pe, z_done, k - 1)
                gate(psZ[:, u % 2], D + f * P, (ih, hh), c, w).then_inc(z_ready, 1)
                positive(pe, t_step, k)
                gate(psH, 2 * D + f * P, (hh,), c, w).then_inc(h_ready, 1)
                positive(pe, t2_done, k)
                gate(psN, 2 * D + f * P, (ih,), c, w).then_inc(n_ready, 1)

            def natural(c, tiles):
                pe.wait_ge(mix_done, UNITS * (c + 1))
                for q in range(tiles):
                    t = GB * c + q
                    if q >= 2:
                        pe.wait_ge(x1_done, t - 1)
                    for f in range(KD):
                        last = pe.transpose(psX[:, q % 2, f * P:(f + 1) * P], total[:, f, q * P:(q + 1) * P], ident[:])
                    last.then_inc(tr_done, 1)

            def body(c, w):
                pe.wait_ge(v_lo_done, 3 * (c + 1))
                unit(c, 0, w)
                if not (isinstance(c, int) and c == 0):
                    natural(c - 1, GB)
                for u in range(1, UNITS):
                    unit(c, u, w)
            chunks(pe, body)
            natural(LAST, GSIZE[LAST])


def ffn_stage(nc, ident, eps, x1, stats, wr_in, br_in, w1_in, b1_in, w2_in, b2_in,
              gamma_in, beta_in, out):
    WIDTHS = [CH] * (NCH - 1) + [GSIZE[LAST] * P]
    ROWS_LAST = N - (NT - 1) * P
    EF = TOP_K * FT
    with ExitStack() as ctx:
        def sb(name, shape, dt):
            return ctx.enter_context(nc.sbuf_tensor(name, shape, dt))

        def sem(name):
            return ctx.enter_context(nc.semaphore(name))

        mean = sb("f_mean", [P, NT], F32)
        var = sb("f_var", [P, NT], F32)
        tmp = sb("f_tmp", [P, NT], F32)
        rstd = sb("f_rstd", [P, NT], F32)
        xn = sb("f_xn", [P, NT, D], F32)
        xT_hi = sb("f_xT_hi", [P, KD, NP], F32R)
        xT_lo = sb("f_xT_lo", [P, KD, NP], F32R)
        ones = sb("f_ones", [P, P], F32)
        mT = sb("f_mT", [P, KD], F32)
        wr = sb("f_wr", [P, KD, E], F32)
        br = sb("f_br", [1, E], F32)
        row = sb("f_row", [1, 16, E], F32)
        col = sb("f_col", [1, 16], F32)
        idx = sb("f_idx", [1, E], U32)
        wb = sb("f_wb", [P, TOP_K], F32)
        w1r = sb("f_w1r", [P, TOP_K, KD, F], F32)
        w1_hi = sb("f_w1_hi", [P, TOP_K, KD, F], F32R)
        w1_lo = sb("f_w1_lo", [P, TOP_K, KD, F], F32R)
        w2r = sb("f_w2r", [P, TOP_K, FT, D], F32)
        w2 = sb("f_w2", [P, EF, 2 * D], F32R)
        b1 = sb("f_b1", [P, TOP_K, FT], F32)
        b2 = sb("f_b2", [P, TOP_K, D], F32)
        b2s = sb("f_b2s", [P, D], F32)
        gamma = sb("f_gamma", [P, D], F32)
        beta = sb("f_beta", [P, D], F32)
        hid = sb("f_hid", [P, 2, CH], F32)
        hid_hi = sb("f_hid_hi", [P, EF, CH], F32R)
        hid_lo = sb("f_hid_lo", [P, EF, CH], F32R)
        y = sb("f_y", [P, GB, D], F32)
        o = sb("f_o", [P, GB, D], F32)
        st = sb("f_st", [P, GB, 6], F32)
        mean3 = sb("f_mean3", [P, GB], F32)
        var3 = sb("f_var3", [P, GB], F32)
        tmp3 = sb("f_tmp3", [P, GB], F32)
        std3 = sb("f_std3", [P, GB], F32)
        rstd3 = sb("f_rstd3", [P, GB], F32)
        psT = ctx.enter_context(nc.psum_tensor("f_psT", [P, 3, 512], F32))
        psO = ctx.enter_context(nc.psum_tensor("f_psO", [P, GB, 512], F32))
        psM = ctx.enter_context(nc.psum_tensor("f_psM", [P, 512], F32))
        consts_here = sem("f_consts_here")
        dve_step = sem("f_dve_step")
        ones_set = sem("f_ones_set")
        var_done = sem("f_var_done")
        std_done = sem("f_std_done")
        xn_done = sem("f_xn_done")
        mean_ready = sem("f_mean_ready")
        mT_done = sem("f_mT_done")
        logits_ready = sem("f_logits_ready")
        ex_need = sem("f_ex_need")
        ex_done = sem("f_ex_done")
        idx_done = sem("f_idx_done")
        top_done = sem("f_top_done")
        wb_ready = sem("f_wb_ready")
        wb_done = sem("f_wb_done")
        xt_done = sem("f_xt_done")
        x_hi_done = sem("f_x_hi_done")
        x_lo_done = sem("f_x_lo_done")
        w_here = [sem(f"f_w_here{k}") for k in range(TOP_K)]
        w1_hi_done = sem("f_w1_hi_done")
        w1_lo_done = sem("f_w1_lo_done")
        w2_scaled = sem("f_w2_scaled")
        w2_hi_done = sem("f_w2_hi_done")
        w2_lo_done = sem("f_w2_lo_done")
        xb_done = sem("f_xb_done")
        x1b_done = sem("f_x1b_done")
        hid_ready = sem("f_hid_ready")
        gelu_done = sem("f_gelu_done")
        h_hi_done = sem("f_h_hi_done")
        h_lo_done = sem("f_h_lo_done")
        out_ready = sem("f_out_ready")
        y_step = sem("f_y_step")
        y_done = sem("f_y_done")
        v3_step = sem("f_v3_step")
        v3_done = sem("f_v3_done")
        s3_done = sem("f_s3_done")
        o_done = sem("f_o_done")
        og_done = sem("f_og_done")
        oo_done = sem("f_oo_done")
        stored = sem("f_stored")
        block = ctx.enter_context(nc.Block())

        def positive(eng, s, v):
            if not isinstance(v, int) or v > 0:
                eng.wait_ge(s, v)

        @block.sync
        def _(sp):
            for dst, src in ((wr, wr_in), (br, br_in), (gamma, gamma_in), (beta, beta_in)):
                sp.dma_start(dst[:], src).then_inc(consts_here, 16)
            sp.wait_ge(idx_done, 1)
            for k in range(TOP_K):
                e = sp.value_load(idx[0:1, k:k + 1], min_val=0, max_val=E - 1)
                sp.dma_start(w1r[:, k], w1_in[e]).then_inc(w_here[k], 16)
                sp.dma_start(w2r[:, k], w2_in[e]).then_inc(w_here[k], 16)
                sp.dma_start(b1[:, k], b1_in[e]).then_inc(w_here[k], 16)
                sp.dma_start(b2[:, k], b2_in[e]).then_inc(w_here[k], 16)

        @block.gpsimd
        def _(pool):
            pool.memset(ones[:], 1.0).then_inc(ones_set, 1)
            pool.wait_ge(consts_here, 64)
            pool.wait_ge(xn_done, NT)
            pool.tensor_tensor(x1[:], x1[:], beta[:].rearrange("p (o d) -> p o d", o=1).to_broadcast([P, NT, D]),
                               ALU.add).then_inc(x1b_done, 1)
            pool.wait_ge(x1b_done, 1)

            def finish(c, tiles):
                pool.wait_ge(o_done, GB * c + tiles)
                g = gamma[:].rearrange("p (o d) -> p o d", o=1).to_broadcast([P, tiles, D])
                pool.tensor_tensor(o[:, 0:tiles], o[:, 0:tiles], g, ALU.mult).then_inc(og_done, 1)
                pool.wait_ge(og_done, c + 1)
                pool.tensor_tensor(o[:, 0:tiles], o[:, 0:tiles], x1[:, bass.ds(GB * c, tiles)],
                                   ALU.add).then_inc(oo_done, 1)
                pool.wait_ge(oo_done, c + 1)
                pool.dma_start(out[bass.ds(GB * c, tiles)].rearrange("t p d -> p t d"),
                               o[:, 0:tiles]).then_inc(stored, 16)
            with pool.Fori(0, LAST) as c:
                finish(c, GB)
            finish(LAST, GSIZE[LAST])
            pool.wait_ge(stored, 16 * NCH)

        @block.scalar
        def _(act):
            act.wait_ge(var_done, 1)
            act.activation(tmp[:], var[:], ACT.Sqrt, bias=eps[:, 0:1]).then_inc(std_done, 1)
            act.wait_ge(mean_ready, 1)
            act.mul(mT[:], psM[:, 0:KD], 1.0 / N).then_inc(mT_done, 1)
            for j, (a, n) in enumerate(((1, E), (5, E), (9, TOP_K))):
                act.wait_ge(ex_need, j + 1)
                act.activation(row[:, a, 0:n], row[:, a - 1, 0:n], ACT.Exp, bias=col[:, 2 * j:2 * j + 1],
                               accum_out=col[:, 2 * j + 1:2 * j + 2]).then_inc(ex_done, 1)
            act.wait_ge(wb_ready, 1)
            act.copy(wb[:], psM[:, 32:32 + TOP_K]).then_inc(wb_done, 1)
            for g in range(NG):
                for k in range(KD):
                    j = KD * g + k
                    n = GSIZE[g] * P
                    act.wait_ge(xt_done, j + 1)
                    act.copy(xT_hi[:, k, g * CH:g * CH + n], psT[:, j % 3, 0:n]).then_inc(x_hi_done, 1)
            for k in range(TOP_K):
                act.wait_ge(w_here[k], 64)
                act.copy(w1_hi[:, k], w1r[:, k]).then_inc(w1_hi_done, 1)
                act.wait_ge(w2_scaled, k + 1)
                act.copy(w2[:, k * FT:(k + 1) * FT, 0:D], w2r[:, k]).then_inc(w2_hi_done, 1)

            def chunk(c, w):
                for e in range(EF):
                    j = EF * c + e
                    act.wait_ge(hid_ready, j + 1)
                    positive(act, h_lo_done, j - 1)
                    act.activation(hid[:, e % 2, 0:w], psT[:, e % 2, 0:w], ACT.Gelu,
                                   bias=b1[:, e // FT, e % FT:e % FT + 1]).then_inc(gelu_done, 1)
                    act.wait_ge(gelu_done, j + 1)
                    positive(act, out_ready, EF * (c - 1) + e + 1)
                    act.copy(hid_hi[:, e, 0:w], hid[:, e % 2, 0:w]).then_inc(h_hi_done, 1)
                act.wait_ge(v3_done, c + 1)
                act.activation(std3[:, 0:w // P], var3[:, 0:w // P], ACT.Sqrt, bias=eps[:, 0:1]).then_inc(s3_done, 1)
            chunk(0, WIDTHS[0])
            with act.Fori(1, LAST) as c:
                chunk(c, CH)
            chunk(LAST, WIDTHS[LAST])

        @block.vector
        def _(dve):
            chain = Chain(dve, dve_step)
            moments(dve, chain, stats, mean[:], var[:], tmp[:])
            dve.nop().then_inc(var_done, 1)
            dve.wait_ge(std_done, 1)
            chain(dve.reciprocal(rstd[:], tmp[:]))
            with dve.Fori(0, NT) as t:
                dve.tensor_scalar(xn[:, t], x1[:, t], mean[:, bass.ds(t, 1)], rstd[:, bass.ds(t, 1)],
                                  ALU.subtract, ALU.mult).then_inc(xn_done, 1)
            dve.wait_ge(consts_here, 64)
            dve.wait_ge(logits_ready, 1)
            lg, e1, rw, sc, e2 = (row[:, a] for a in (0, 1, 2, 3, 5))
            chain(dve.tensor_tensor(lg, psM[0:1, 16:16 + E], br[:], ALU.add))
            chain(dve.tensor_reduce(col[:, 0:1], lg, AX.X, ALU.max))
            dve.tensor_scalar(col[:, 0:1], col[:, 0:1], -1.0, None, ALU.mult).then_inc(ex_need, 1)
            dve.wait_ge(ex_done, 1)
            chain(dve.reciprocal(col[:, 6:7], col[:, 1:2]))
            chain(dve.tensor_scalar(rw, e1, col[:, 6:7], None, ALU.mult))
            chain(dve.tensor_scalar(sc, rw, float(N), 1e-30, ALU.mult, ALU.max))
            chain(dve.reciprocal(row[:, 6], sc))
            chain(dve.tensor_scalar(row[:, 6], row[:, 6], CAPACITY, 1.0, ALU.mult, ALU.min))
            chain(dve.tensor_tensor(row[:, 4], rw, row[:, 6], ALU.mult))
            chain(dve.tensor_reduce(col[:, 2:3], row[:, 4], AX.X, ALU.max))
            dve.tensor_scalar(col[:, 2:3], col[:, 2:3], -1.0, None, ALU.mult).then_inc(ex_need, 1)
            dve.wait_ge(ex_done, 2)
            chain(dve.reciprocal(col[:, 7:8], col[:, 3:4]))
            chain(dve.tensor_scalar(row[:, 7], e2, col[:, 7:8], None, ALU.mult))
            chain(dve.max(row[:, 8], row[:, 7]))
            dve.max_index(idx[:], row[:, 8], row[:, 7]).then_inc(idx_done, 1)
            dve.tensor_scalar(col[:, 4:5], row[:, 8, 0:1], -1.0, None, ALU.mult).then_inc(ex_need, 1)
            dve.wait_ge(ex_done, 3)
            chain(dve.reciprocal(col[:, 8:9], col[:, 5:6]))
            dve.tensor_scalar(row[:, 10, 0:TOP_K], row[:, 9, 0:TOP_K], col[:, 8:9], None, ALU.mult).then_inc(top_done, 1)
            for g in range(NG):
                for k in range(KD):
                    j = KD * g + k
                    n = GSIZE[g] * P
                    dve.wait_ge(x_hi_done, j + 1)
                    dve.tensor_tensor(xT_lo[:, k, g * CH:g * CH + n], psT[:, j % 3, 0:n],
                                      xT_hi[:, k, g * CH:g * CH + n].bitcast(F32), ALU.subtract).then_inc(x_lo_done, 1)
            dve.wait_ge(wb_done, 1)
            for k in range(TOP_K):
                dve.wait_ge(w_here[k], 64)
                dve.tensor_scalar(w2r[:, k], w2r[:, k], wb[:, k:k + 1], None, ALU.mult).then_inc(w2_scaled, 1)
                dve.wait_ge(w1_hi_done, k + 1)
                dve.tensor_tensor(w1_lo[:, k], w1r[:, k], w1_hi[:, k].bitcast(F32), ALU.subtract).then_inc(w1_lo_done, 1)
                dve.wait_ge(w2_hi_done, k + 1)
                dve.tensor_tensor(w2[:, k * FT:(k + 1) * FT, D:2 * D], w2r[:, k],
                                  w2[:, k * FT:(k + 1) * FT, 0:D].bitcast(F32), ALU.subtract).then_inc(w2_lo_done, 1)
            chain(dve.tensor_scalar(b2s[:], b2[:, 0], wb[:, 0:1], None, ALU.mult))
            chain(dve.scalar_tensor_tensor(b2s[:], b2[:, 1], wb[:, 1:2], b2s[:], ALU.mult, ALU.add))

            def chunk(c, w):
                tiles = w // P
                for e in range(EF):
                    j = EF * c + e
                    dve.wait_ge(h_hi_done, j + 1)
                    dve.tensor_tensor(hid_lo[:, e, 0:w], hid[:, e % 2, 0:w], hid_hi[:, e, 0:w].bitcast(F32),
                                      ALU.subtract).then_inc(h_lo_done, 1)
                    if e < tiles:
                        t = GB * c + e
                        dve.tensor_tensor(xn[:, t], xn[:, t], b2s[:], ALU.add).then_inc(xb_done, 1)
                dve.wait_ge(out_ready, EF * (c + 1))
                dve.wait_ge(xb_done, GB * c + tiles)
                for q in range(tiles):
                    t = GB * c + q
                    dve.tensor_tensor(y[:, q], psO[:, q, 0:D], xn[:, t], ALU.add).then_inc(y_step, 1)
                    dve.wait_ge(y_step, t + 1)
                    dve.tensor_tensor(y[:, q], psO[:, q, D:2 * D], y[:, q], ALU.add).then_inc(y_done, 1)
                for q in range(tiles):
                    dve.wait_ge(y_done, GB * c + q + 1)
                    last = dve.bn_stats(st[:, q], y[:, q])
                last.then_inc(v3_step, 1)
                dve.wait_ge(v3_step, 6 * c + 1)
                s_, m_, v_, p_ = st[:, 0:tiles], mean3[:, 0:tiles], var3[:, 0:tiles], tmp3[:, 0:tiles]
                dve.tensor_tensor(m_, s_[:, :, 1], s_[:, :, 4], ALU.add)
                dve.tensor_tensor(p_, s_[:, :, 1], s_[:, :, 4], ALU.subtract)
                dve.tensor_tensor(v_, s_[:, :, 2], s_[:, :, 5], ALU.add).then_inc(v3_step, 1)
                dve.wait_ge(v3_step, 6 * c + 2)
                dve.tensor_scalar(m_, m_, 0.5, None, ALU.mult)
                dve.scalar_tensor_tensor(p_, p_, 0.25, p_, ALU.mult, ALU.mult).then_inc(v3_step, 1)
                dve.wait_ge(v3_step, 6 * c + 3)
                dve.scalar_tensor_tensor(v_, v_, 1.0 / D, p_, ALU.mult, ALU.add).then_inc(v3_done, 1)
                dve.wait_ge(s3_done, c + 1)
                dve.reciprocal(rstd3[:, 0:tiles], std3[:, 0:tiles]).then_inc(v3_step, 1)
                dve.wait_ge(v3_step, 6 * c + 4)
                positive(dve, stored, 16 * c)
                for q in range(tiles):
                    dve.tensor_scalar(o[:, q], y[:, q], mean3[:, q:q + 1], rstd3[:, q:q + 1],
                                      ALU.subtract, ALU.mult).then_inc(o_done, 1)
                dve.wait_ge(o_done, GB * c + tiles)
                dve.nop().then_inc(v3_step, 2)
            chunk(0, WIDTHS[0])
            with dve.Fori(1, LAST) as c:
                chunk(c, CH)
            chunk(LAST, WIDTHS[LAST])

        @block.tensor
        def _(pe):
            pe.wait_ge(ones_set, 1)
            for k in range(KD):
                for t in range(NT):
                    pe.wait_ge(xn_done, t + 1)
                    rows = P if t < NT - 1 else ROWS_LAST
                    last = pe.matmul(psM[:, k:k + 1], xn[0:rows, t, k * P:(k + 1) * P], ones[0:rows, 0:1],
                                     start=(t == 0), stop=(t == NT - 1))
            last.then_inc(mean_ready, 1)
            pe.wait_ge(mT_done, 1)
            pe.wait_ge(consts_here, 64)
            for k in range(KD):
                last = pe.matmul(psM[0:1, 16:16 + E], mT[:, k:k + 1], wr[:, k], start=(k == 0), stop=(k == KD - 1))
            last.then_inc(logits_ready, 1)

            def x_transposes(j):
                g, k = j // KD, j % KD
                if j >= 3:
                    pe.wait_ge(x_lo_done, j - 2)
                for b in range(GSIZE[g]):
                    t = GB * g + b
                    last = pe.transpose(psT[:, j % 3, b * P:(b + 1) * P], xn[:, t, k * P:(k + 1) * P], ident[:])
                last.then_inc(xt_done, 1)
            for j in range(3):
                x_transposes(j)
            pe.wait_ge(top_done, 1)
            pe.matmul(psM[:, 32:32 + TOP_K], ones[0:1, :], row[:, 10, 0:TOP_K], start=True, stop=True).then_inc(wb_ready, 1)
            for j in range(3, KD * NG):
                x_transposes(j)
            pe.wait_ge(x_lo_done, KD * NG)
            pe.wait_ge(w1_lo_done, TOP_K)
            pe.wait_ge(w2_lo_done, TOP_K)

            def hidden(c, e, w):
                j = EF * c + e
                positive(pe, gelu_done, j - 1)
                ps = psT[:, e % 2, 0:w]
                x = e // FT
                cols = slice(e % FT * P, (e % FT + 1) * P)
                terms = [(k, a, v) for k in range(KD) for a, v in ((w1_hi, xT_hi), (w1_hi, xT_lo), (w1_lo, xT_hi))]
                for n, (k, a, v) in enumerate(terms):
                    last = pe.matmul(ps, a[:, x, k, cols], v[:, k, bass.ds(c * CH, w)],
                                     start=(n == 0), stop=(n == len(terms) - 1))
                last.then_inc(hid_ready, 1)

            def output(c, e, w):
                pe.wait_ge(h_lo_done, EF * c + e + 1)
                if e == 0:
                    positive(pe, y_done, GB * c)
                for q in range(w // P):
                    cols = slice(q * P, (q + 1) * P)
                    pe.matmul(psO[:, q, :], hid_hi[:, e, cols], w2[:, e, :], start=(e == 0), stop=False)
                    last = pe.matmul(psO[:, q, 0:D], hid_lo[:, e, cols], w2[:, e, 0:D], start=False,
                                     stop=(e == EF - 1))
                last.then_inc(out_ready, 1)

            def chunk(c, w):
                hidden(c, 0, w)
                hidden(c, 1, w)
                for e in range(EF):
                    output(c, e, w)
                    if e + 2 < EF:
                        hidden(c, e + 2, w)
            chunk(0, WIDTHS[0])
            with pe.Fori(1, LAST) as c:
                chunk(c, CH)
            chunk(LAST, WIDTHS[LAST])


def kernel(x, adj, L0_gnn_gat_W, L0_gnn_gat_a, L0_gnn_edge_Wih, L0_gnn_edge_Whh, L0_gnn_edge_bih, L0_gnn_edge_bhh,
           L0_gnn_node_Wih, L0_gnn_node_Whh, L0_gnn_node_bih, L0_gnn_node_bhh, L0_ffn_Wr, L0_ffn_br, L0_ffn_W1,
           L0_ffn_b1, L0_ffn_W2, L0_ffn_b2, L0_ffn_gamma, L0_ffn_beta):
    import numpy as np
    import concourse.bacc as bacc
    from concourse.bass_utils import run_bass_kernel_spmd

    def rows(a):
        a = np.asarray(a)
        return a.reshape((a.shape[0] // P, P) + a.shape[1:]).swapaxes(0, 1)

    adj = np.asarray(adj)
    xp = np.zeros((NP, D), np.float32)
    xp[:N] = np.asarray(x)
    ap = np.zeros((NP, NP), np.float32)
    ap[:N, :N] = adj
    dg = np.zeros((NP,), np.float32)
    dg[:N] = np.diagonal(adj)
    eye = np.eye(P, dtype=np.float32)
    gw = np.asarray(L0_gnn_gat_W)
    ga = np.asarray(L0_gnn_gat_a)
    gru = (L0_gnn_edge_Wih, L0_gnn_edge_Whh, L0_gnn_node_Wih, L0_gnn_node_Whh)
    gb = (L0_gnn_edge_bih, L0_gnn_edge_bhh, L0_gnn_node_bih, L0_gnn_node_bhh)
    arrays = {
        "x_tiles": xp.reshape(NT, P, D),
        "adj_t": ap.reshape(NT, P, NT, P).transpose(0, 3, 2, 1).reshape(NT, P, NP),
        "adj_n": ap.reshape(NT, P, NP),
        "diag": dg.reshape(NT, P).T,
        "ident": eye,
        "notid": np.ones((P, P), np.float32) - eye,
        "gat_wt": gw.transpose(0, 2, 1).reshape(HEADS, KD, P, D).transpose(2, 0, 1, 3),
        "gat_w": gw.reshape(HEADS, KD, P, D).transpose(2, 0, 1, 3),
        "gat_a": ga.reshape(HEADS, 2, KD, P).transpose(3, 0, 1, 2),
        "gru_w": np.stack([rows(np.asarray(w).T) for w in gru]),
        "gru_b": np.stack([np.asarray(v).reshape(3 * KD, P).T for v in gb], axis=1),
        "wr": rows(L0_ffn_Wr),
        "br": np.asarray(L0_ffn_br).reshape(1, E),
        "w1": np.stack([rows(w) for w in np.asarray(L0_ffn_W1)]),
        "b1": np.asarray(L0_ffn_b1).reshape(E, FT, P).transpose(0, 2, 1),
        "w2": np.stack([rows(w) for w in np.asarray(L0_ffn_W2)]),
        "b2": np.repeat(np.asarray(L0_ffn_b2)[:, None, :], P, axis=1),
        "gamma": np.repeat(np.asarray(L0_ffn_gamma)[None, :], P, axis=0),
        "beta": np.repeat(np.asarray(L0_ffn_beta)[None, :], P, axis=0),
    }
    nc = bacc.Bacc("TRN2", target_bir_lowering=False, num_devices=1)
    sent, args = {}, []
    for name, a in arrays.items():
        a = np.ascontiguousarray(a)
        sent[f"in_{name}"] = a
        args.append(nc.dram_tensor(f"in_{name}", a.shape, mybir.dt.from_np(a.dtype), kind="ExternalInput").ap())
    out = nc.dram_tensor("out_tiles", (NT, P, D), F32, kind="ExternalOutput").ap()
    build(nc, *args, out)
    r = run_bass_kernel_spmd(nc, [sent], core_ids=[0])
    return r.results[0]["out_tiles"].reshape(NP, D)[:N]
```

```python
from contextlib import ExitStack

import concourse.bass as bass
from concourse import mybir

P = 128
N = 2708
D = 256
KD = D // P
NT = (N + P - 1) // P
NP = NT * P
HEADS = 3
NC2 = 2 * HEADS
ALPHA = 0.2
NEG_INF = -9000000000000000.0
LN_EPS = 1e-5
E = 8
F = 512
FT = F // P
TOP_K = 2
CAPACITY = float(-(-N * 5 // (4 * E)))
GB = 4
NG = (NT + GB - 1) // GB
GSIZE = [min(GB, NT - GB * g) for g in range(NG)]
CH = GB * P
NCH = NG
LAST = NCH - 1

F32 = mybir.dt.float32
F32R = mybir.dt.float32r
BF16 = mybir.dt.bfloat16
U32 = mybir.dt.uint32
U8 = mybir.dt.uint8
ALU = mybir.AluOpType
ACT = mybir.ActivationFunctionType
AX = mybir.AxisListType


class Chain:

    def __init__(self, eng, sem):
        self.eng, self.sem, self.n = eng, sem, 0

    def __call__(self, ins):
        self.n += 1
        ins.then_inc(self.sem, 1)
        self.eng.wait_ge(self.sem, self.n)


def build(nc, x_in, adj_t, adj_n, diag_in, ident_in, notid_in, gat_wt_in, gat_w_in, gat_a_in,
          gru_w_in, gru_b_in, wr_in, br_in, w1_in, b1_in, w2_in, b2_in, gamma_in, beta_in, out):
    s_dram = nc.dram_tensor("supportT_scratch", (P, KD, NP), F32, kind="Internal").ap()
    es_dram = nc.dram_tensor("attentionT_scratch", (P, KD, NP), F32, kind="Internal").ap()
    h_dram = nc.dram_tensor("normedT_scratch", (P, KD, NP), F32, kind="Internal").ap()
    eminus_dram = nc.dram_tensor("eminus_scratch", (HEADS, NP), F32, kind="Internal").ap()
    with ExitStack() as keep:
        def sb(name, shape, dt, ctx=keep):
            return ctx.enter_context(nc.sbuf_tensor(name, shape, dt))

        ident = sb("ident", [P, P], F32)
        eps = sb("eps", [P, 1], F32)
        with ExitStack() as graph:
            shared = dict(
                ident=ident, eps=eps,
                notid=sb("notid", [P, P], F32, graph),
                h_mov=sb("h_mov", [P, NT, 2 * D], F32R, graph),
                logit=sb("logit", [P, HEADS, NP], F32, graph),
                a_ring=sb("a_ring", [P, 2, NP], F32, graph),
                neg=sb("neg", [P, NT], F32, graph),
                negtot=sb("negtot", [P, 1], U32, graph),
            )
            with ExitStack() as sums:
                shared["up"] = sb("up", [P, NT, 20], BF16, sums)
                shared["ones"] = sb("ones", [P, P], F32, sums)
                shared["um"] = sb("um", [P, NT, 20], BF16, sums)
                norm_stage(nc, shared, x_in, ident_in, notid_in, gat_wt_in, gat_a_in, h_dram)
                support_stage(nc, shared, adj_t, s_dram, eminus_dram)
            attention_stage(nc, shared, adj_n, gat_w_in, es_dram, eminus_dram)
        x1 = sb("x1", [P, NT, D], F32)
        stats = sb("stats", [P, NT, 6], F32)
        gru_stage(nc, ident, x1, stats, x_in, diag_in, gru_w_in, gru_b_in, s_dram, es_dram, h_dram)
        ffn_stage(nc, ident, eps, x1, stats, wr_in, br_in, w1_in, b1_in, w2_in, b2_in,
                  gamma_in, beta_in, out)


def moments(dve, chain, st, mean, var, tmp):
    chain(dve.tensor_tensor(mean, st[:, :, 1], st[:, :, 4], ALU.add))
    chain(dve.tensor_scalar(mean, mean, 0.5, None, ALU.mult))
    chain(dve.tensor_tensor(tmp, st[:, :, 1], st[:, :, 4], ALU.subtract))
    chain(dve.scalar_tensor_tensor(tmp, tmp, 0.25, tmp, ALU.mult, ALU.mult))
    chain(dve.tensor_tensor(var, st[:, :, 2], st[:, :, 5], ALU.add))
    chain(dve.scalar_tensor_tensor(var, var, 1.0 / D, tmp, ALU.mult, ALU.add))


def norm_stage(nc, sh, x_in, ident_in, notid_in, gat_wt_in, gat_a_in, h_dram):
    ident, h_mov, up, um = sh["ident"], sh["h_mov"], sh["up"], sh["um"]
    XC = [0, 6, 12, 18, NT]
    with ExitStack() as ctx:
        def sb(name, shape, dt):
            return ctx.enter_context(nc.sbuf_tensor(name, shape, dt))

        def sem(name):
            return ctx.enter_context(nc.semaphore(name))

        x = sb("n_x", [P, NT, D], F32)
        st = sb("n_st", [P, NT, 6], F32)
        mean = sb("n_mean", [P, NT], F32)
        var = sb("n_var", [P, NT], F32)
        tmp = sb("n_tmp", [P, NT], F32)
        rstd = sb("n_rstd", [P, NT], F32)
        h = sb("n_h", [P, 2, D], F32)
        hT = sb("n_hT", [P, 2, KD, P], F32)
        gwt = sb("n_gwt", [P, HEADS, KD, D], F32)
        ga = sb("n_ga", [P, HEADS, 2, KD], F32)
        wa = sb("n_wa", [P, KD, 2, HEADS], F32)
        r1 = sb("n_r1", [P, NT, NC2], F32)
        psT = ctx.enter_context(nc.psum_tensor("n_psT", [P, 2, 512], F32))
        psV = ctx.enter_context(nc.psum_tensor("n_psV", [P, KD, 2, HEADS], F32))
        psU = ctx.enter_context(nc.psum_tensor("n_psU", [P, 512], F32))
        x_here = [sem(f"n_x_here{c}") for c in range(len(XC) - 1)]
        consts_here = sem("n_consts_here")
        consts_set = sem("n_consts_set")
        dve_step = sem("n_dve_step")
        stats_done = sem("n_stats_done")
        var_done = sem("n_var_done")
        std_done = sem("n_std_done")
        rstd_done = sem("n_rstd_done")
        h_done = sem("n_h_done")
        hi_done = sem("n_hi_done")
        lo_done = sem("n_lo_done")
        tr_done = sem("n_tr_done")
        hT_done = sem("n_hT_done")
        u_done = sem("n_u_done")
        wa_ready = sem("n_wa_ready")
        wa_copied = sem("n_wa_copied")
        hT_out = sem("n_hT_out")
        block = ctx.enter_context(nc.Block())

        @block.sync
        def _(sp):
            for c in range(len(XC) - 1):
                sp.dma_start(x[:, XC[c]:XC[c + 1], :],
                             x_in[XC[c]:XC[c + 1]].rearrange("t p d -> p t d")).then_inc(x_here[c], 16)
        @block.gpsimd
        def _(pool):
            pool.memset(sh["ones"][:], 1.0).then_inc(consts_set, 1)
            pool.memset(sh["eps"][:], LN_EPS).then_inc(consts_set, 1)
            pool.memset(up[:], 0.0).then_inc(consts_set, 1)
            pool.memset(um[:], 1.0).then_inc(consts_set, 1)

        @block.scalar
        def _(act):
            act.dma_start(ident[:], ident_in).then_inc(consts_here, 16)
            act.dma_start(sh["notid"][:], notid_in).then_inc(consts_here, 16)
            act.dma_start(gwt[:], gat_wt_in).then_inc(consts_here, 16)
            act.dma_start(ga[:], gat_a_in).then_inc(consts_here, 16)
            act.wait_ge(wa_ready, 1)
            act.copy(wa[:], psV[:]).then_inc(wa_copied, 1)
            act.wait_ge(var_done, 1)
            act.wait_ge(consts_set, 4)
            act.activation(tmp[:], var[:], ACT.Sqrt, bias=eps_of(sh)).then_inc(std_done, 1)

            def tile(t):
                act.wait_ge(h_done, t + 1)
                act.copy(h_mov[:, t, 0:D], h[:, t % 2]).then_inc(hi_done, 1)
                act.wait_ge(tr_done, t + 1)
                if not isinstance(t, int):
                    act.wait_ge(u_done, t - 1)
                    act.wait_ge(hT_out, 16 * (t - 1))
                act.copy(hT[:, t % 2], psT[:, t % 2, 0:D].rearrange("p (k n) -> p k n", k=KD)).then_inc(hT_done, 1)
                act.wait_ge(hT_done, t + 1)
                if not isinstance(t, int):
                    act.wait_ge(hT_out, 16 * t)
                elif t:
                    act.wait_ge(hT_out, 16)
                act.dma_start(h_dram[:, :, bass.ds(t * P, P)], hT[:, t % 2]).then_inc(hT_out, 16)
            for t in range(2):
                tile(t)
            with act.Fori(2, NT) as t:
                tile(t)
            act.wait_ge(hT_out, 16 * NT)

        @block.vector
        def _(dve):
            chain = Chain(dve, dve_step)
            for c in range(len(XC) - 1):
                dve.wait_ge(x_here[c], 16)
                with dve.Fori(XC[c], XC[c + 1]) as t:
                    dve.bn_stats(st[:, t], x[:, t]).then_inc(stats_done, 1)
            dve.wait_ge(stats_done, NT)
            moments(dve, chain, st, mean[:], var[:], tmp[:])
            dve.nop().then_inc(var_done, 1)
            dve.wait_ge(std_done, 1)
            dve.reciprocal(rstd[:], tmp[:]).then_inc(rstd_done, 1)
            dve.wait_ge(rstd_done, 1)

            def tile(t):
                if not isinstance(t, int):
                    dve.wait_ge(hi_done, t - 1)
                    dve.wait_ge(tr_done, t - 1)
                dve.tensor_scalar(h[:, t % 2], x[:, t], mean[:, bass.ds(t, 1)], rstd[:, bass.ds(t, 1)],
                                  ALU.subtract, ALU.mult).then_inc(h_done, 1)
                dve.wait_ge(hi_done, t + 1)
                dve.tensor_tensor(h_mov[:, t, D:2 * D], h[:, t % 2], h_mov[:, t, 0:D].bitcast(F32),
                                  ALU.subtract).then_inc(lo_done, 1)
            for t in range(2):
                tile(t)
            with dve.Fori(2, NT) as t:
                tile(t)
            dve.wait_ge(u_done, NT)
            dve.wait_ge(consts_set, 4)
            u = psU[:, 0:NT * NC2].rearrange("p (t c) -> p t c", c=NC2)
            chain(dve.tensor_copy(up[:, :, 0:NC2], u))
            chain(dve.tensor_tensor(r1[:], u, up[:, :, 0:NC2], ALU.subtract))
            chain(dve.tensor_copy(up[:, :, NC2:2 * NC2], r1[:]))
            chain(dve.tensor_tensor(r1[:], r1[:], up[:, :, NC2:2 * NC2], ALU.subtract))
            chain(dve.tensor_copy(up[:, :, 2 * NC2:3 * NC2], r1[:]))
            upv = up[:, :, 0:3 * NC2].rearrange("p t (q s h) -> p t q s h", q=3, s=2)
            umv = um[:, :, 0:3 * NC2].rearrange("p t (q s h) -> p t q s h", q=3, s=2)
            for s in range(2):
                for q in range(3):
                    chain(dve.tensor_copy(umv[:, :, q, s, :], upv[:, :, q, 1 - s, :]))

        @block.tensor
        def _(pe):
            pe.wait_ge(consts_here, 64)
            for hd in range(HEADS):
                for m in range(KD):
                    for k in range(KD):
                        last = pe.matmul(psV[:, m, :, hd], gwt[:, hd, k, m * P:(m + 1) * P], ga[:, hd, :, k],
                                         start=(k == 0), stop=(k == KD - 1))
            last.then_inc(wa_ready, 1)
            pe.wait_ge(wa_copied, 1)

            def transposes(u):
                for k in range(KD):
                    last = pe.transpose(psT[:, u, k * P:(k + 1) * P], h[:, u, k * P:(k + 1) * P], ident[:])
                last.then_inc(tr_done, 1)

            def project(t, u):
                for k in range(KD):
                    last = pe.matmul(psU[:, bass.ds(t * NC2, NC2)], hT[:, u, k, :],
                                     wa[:, k].rearrange("p s h -> p (s h)"), start=(k == 0), stop=(k == KD - 1))
                last.then_inc(u_done, 1)
            def pair(i, first):
                for u in range(2):
                    t = 2 * i + u
                    pe.wait_ge(h_done, t + 1)
                    if not first:
                        pe.wait_ge(hT_done, t - 1)
                    transposes(u)
                    pe.wait_ge(hT_done, t + 1)
                    project(t, u)
            pair(0, True)
            with pe.Fori(1, NT // 2) as i:
                pair(i, False)


def eps_of(sh):
    return sh["eps"][:, 0:1]


def support_stage(nc, sh, adj_t, s_dram, eminus_dram):
    ident, ones, notid, h_mov, logit = sh["ident"], sh["ones"], sh["notid"], sh["h_mov"], sh["logit"]
    a_ring, up, um, neg = sh["a_ring"], sh["up"], sh["um"], sh["neg"]
    with ExitStack() as ctx:
        def sb(name, shape, dt):
            return ctx.enter_context(nc.sbuf_tensor(name, shape, dt))

        def sem(name):
            return ctx.enter_context(nc.semaphore(name))

        hi = sb("s_hi", [P, 2, NP], F32R)
        lo = sb("s_lo", [P, 2, NP], F32R)
        pos = sb("s_pos", [P, 2, NP], BF16)
        ngt = sb("s_neg", [P, 2, NP], BF16)
        half = sb("s_half", [P, D], F32)
        s = sb("s_s", [P, D], F32)
        sT = sb("s_sT", [P, KD, P], F32)
        e0 = sb("s_e0", [P, NC2], F32)
        e1 = sb("s_e1", [P, NC2], F32)
        negsum = sb("s_negsum", [P, 1], F32)
        eminus = sb("s_eminus", [HEADS, NP], F32)
        psS = ctx.enter_context(nc.psum_tensor("s_psS", [P, 2, 512], F32))
        psE = ctx.enter_context(nc.psum_tensor("s_psE", [P, 2, 512], F32))
        psT = ctx.enter_context(nc.psum_tensor("s_psT", [P, 512], F32))
        psB = ctx.enter_context(nc.psum_tensor("s_psB", [P, 2, 512], F32))
        a_here = sem("s_a_here")
        diag_off = sem("s_diag_off")
        hi_done = sem("s_hi_done")
        lo_done = sem("s_lo_done")
        masks_done = sem("s_masks_done")
        mains_done = sem("s_mains_done")
        half_done = sem("s_half_done")
        s_done = sem("s_s_done")
        sum_done = sem("s_sum_done")
        e_done = sem("s_e_done")
        posts_done = sem("s_posts_done")
        sT_done = sem("s_sT_done")
        bcast_done = sem("s_bcast_done")
        sT_out = sem("s_sT_out")
        neg_here = sem("s_neg_here")
        neg_all = sem("s_neg_all")
        eminus_out = sem("s_eminus_out")
        block = ctx.enter_context(nc.Block())

        @block.sync
        def _(sp):
            sp.dma_start(a_ring[:, 0], adj_t[0]).then_inc(a_here, 16)
            sp.wait_ge(a_here, 16)
            sp.dma_start(a_ring[:, 1], adj_t[1]).then_inc(a_here, 16)

        @block.gpsimd
        def _(pool):
            def store(t):
                pool.wait_ge(sT_done, t + 1)
                pool.dma_start(s_dram[:, :, bass.ds(t * P, P)], sT[:]).then_inc(sT_out, 16)
                pool.wait_ge(sT_out, 16 * (t + 1))
            with pool.Fori(0, NT) as t:
                store(t)

        @block.scalar
        def _(act):
            def split(t, u):
                act.wait_ge(diag_off, t + 1)
                if not isinstance(t, int) or t >= 2:
                    act.wait_ge(mains_done, t - 1)
                act.copy(hi[:, u], a_ring[:, u]).then_inc(hi_done, 1)

            def load(t, u):
                act.wait_ge(a_here, 16 * t)
                act.wait_ge(lo_done, t - 1)
                act.wait_ge(masks_done, t - 1)
                act.dma_start(a_ring[:, u], adj_t[t]).then_inc(a_here, 16)

            def halves(t, u):
                act.wait_ge(mains_done, t + 1)
                if not isinstance(t, int) or t:
                    act.wait_ge(s_done, t)
                act.copy(half[:], psS[:, u, D:2 * D]).then_inc(half_done, 1)

            def results(t):
                act.wait_ge(posts_done, t + 1)
                if not isinstance(t, int) or t:
                    act.wait_ge(sT_out, 16 * t)
                act.copy(sT[:], psT[:, 0:D].rearrange("p (k n) -> p k n", k=KD)).then_inc(sT_done, 1)
                act.copy(eminus[:, bass.ds(t * P, P)], psB[0:HEADS, 1, 0:P])
                act.copy(logit[:, :, bass.ds(t * P, P)],
                         psB[:, 0, 0:HEADS * P].rearrange("p (c n) -> p c n", c=HEADS)).then_inc(bcast_done, 1)

            def turn(t, u, more, load_more):
                halves(t - 1, 1 - u)
                if more:
                    split(t + 1, 1 - u)
                if load_more:
                    load(t + 2, u)
                results(t - 1)
            split(0, 0)
            split(1, 1)
            load(2, 0)
            for t in (1, 2):
                turn(t, t % 2, True, True)
            with act.Fori(1, NT // 2 - 2) as i:
                turn(2 * i + 1, 1, True, True)
                turn(2 * i + 2, 0, True, True)
            turn(NT - 3, 1, True, True)
            turn(NT - 2, 0, True, False)
            turn(NT - 1, 1, False, False)
            halves(NT - 1, 1)
            results(NT - 1)
            act.wait_ge(bcast_done, NT)
            act.dma_start(eminus_dram, eminus[:]).then_inc(eminus_out, 16)
            act.wait_ge(eminus_out, 16)

        @block.vector
        def _(dve):
            def prepare(t, u):
                dve.wait_ge(a_here, 16 * (t + 1))
                d = a_ring[:, u, bass.ds(t * P, P)]
                dve.tensor_tensor(d, d, notid[:], ALU.mult).then_inc(diag_off, 1)
                dve.wait_ge(diag_off, t + 1)
                if not isinstance(t, int) or t >= 2:
                    dve.wait_ge(mains_done, t - 1)
                dve.tensor_scalar(pos[:, u], a_ring[:, u], 0.0, None, ALU.is_gt)
                dve.tensor_scalar(ngt[:, u], a_ring[:, u], 0.0, None, ALU.is_lt).then_inc(masks_done, 1)
                dve.wait_ge(hi_done, t + 1)
                dve.tensor_tensor(lo[:, u], a_ring[:, u], hi[:, u].bitcast(F32), ALU.subtract).then_inc(lo_done, 1)

            def post(t, u):
                dve.wait_ge(mains_done, t + 1)
                if not isinstance(t, int) or t:
                    dve.wait_ge(posts_done, t)
                dve.tensor_reduce(e0[:], psE[:, u, 0:3 * NC2].rearrange("p (q c) -> p c q", q=3), AX.X,
                                  ALU.add).then_inc(sum_done, 1)
                dve.tensor_copy(neg[:, bass.ds(t, 1)], psE[:, u, 3 * NC2:3 * NC2 + 1])
                dve.wait_ge(sum_done, t + 1)
                dve.scalar_tensor_tensor(e1[:], e0[:], ALPHA, e0[:], ALU.mult, ALU.max).then_inc(e_done, 1)
                dve.wait_ge(half_done, t + 1)
                dve.tensor_tensor(s[:], psS[:, u, 0:D], half[:], ALU.add).then_inc(s_done, 1)

            def turn(t, u):
                post(t - 1, 1 - u)
                prepare(t + 1, 1 - u)
            prepare(0, 0)
            prepare(1, 1)
            for t in (1, 2):
                turn(t, t % 2)
            with dve.Fori(1, NT // 2 - 1) as i:
                turn(2 * i + 1, 1)
                turn(2 * i + 2, 0)
            post(NT - 2, 0)
            post(NT - 1, 1)
            dve.wait_ge(e_done, NT)
            dve.tensor_reduce(negsum[:], neg[:], AX.X, ALU.add).then_inc(neg_here, 1)
            dve.wait_ge(neg_all, 1)
            dve.tensor_copy(sh["negtot"][:], psT[:, 256:257])

        @block.tensor
        def _(pe):
            def main(t, u, between):
                pe.wait_ge(masks_done, t + 1)
                for j in range(NT):
                    b = slice(j * P, (j + 1) * P)
                    pe.matmul(psE[:, u, 0:19], pos[:, u, b], up[:, j, 0:19], start=(j == 0), stop=False)
                    pe.matmul(psE[:, u, 0:19], ngt[:, u, b], um[:, j, 0:19], start=False, stop=(j == NT - 1))
                pe.wait_ge(hi_done, t + 1)
                pe.wait_ge(lo_done, t + 1)
                for j in range(NT):
                    if j == NT // 4:
                        between()
                    b = slice(j * P, (j + 1) * P)
                    pe.matmul(psS[:, u, :], hi[:, u, b], h_mov[:, j, :], start=(j == 0), stop=False)
                    last = pe.matmul(psS[:, u, 0:D], lo[:, u, b], h_mov[:, j, 0:D], start=False,
                                     stop=(j == NT - 1))
                last.then_inc(mains_done, 1)

            def post(t):
                pe.wait_ge(e_done, t + 1)
                if not isinstance(t, int) or t:
                    pe.wait_ge(bcast_done, t)
                for c in range(HEADS):
                    pe.matmul(psB[:, 0, c * P:(c + 1) * P],
                              e1[:, c:c + 1].to_broadcast([P, P]), ident[:], start=True, stop=True)
                pe.matmul(psB[0:HEADS, 1, 0:P], e1[:, HEADS:NC2], ident[:], start=True, stop=True)
                pe.wait_ge(s_done, t + 1)
                for k in range(KD):
                    last = pe.transpose(psT[:, k * P:(k + 1) * P], s[:, k * P:(k + 1) * P], ident[:])
                last.then_inc(posts_done, 1)
            main(0, 0, lambda: None)
            main(1, 1, lambda: post(0))
            main(2, 0, lambda: post(1))
            with pe.Fori(1, NT // 2 - 1) as i:
                main(2 * i + 1, 1, lambda: post(2 * i))
                main(2 * i + 2, 0, lambda: post(2 * i + 1))
            main(NT - 1, 1, lambda: post(NT - 2))
            post(NT - 1)
            pe.wait_ge(neg_here, 1)
            pe.wait_ge(bcast_done, NT)
            pe.matmul(psT[:, 256:257], ones[:], negsum[:], start=True, stop=True).then_inc(neg_all, 1)


def attention_stage(nc, sh, adj_n, gat_w_in, es_dram, eminus_dram):
    ident, notid, h_mov, logit, a_ring = sh["ident"], sh["notid"], sh["h_mov"], sh["logit"], sh["a_ring"]
    LT = 3
    WR = 4
    TR = 3
    SPI = 2 * HEADS
    LE = 3
    EE = 2
    GPI = SPI * NG
    STEPS = NT * HEADS
    ITERS = NT // 2
    HALF = NP // 2
    assert GPI % WR == 0 and GPI % TR == 0
    with ExitStack() as ctx:
        def sb(name, shape, dt):
            return ctx.enter_context(nc.sbuf_tensor(name, shape, dt))

        def sem(name):
            return ctx.enter_context(nc.semaphore(name))

        w_nat = sb("a_w", [P, SPI, NP], F32)
        mask = sb("a_mask", [P, NP], BF16)
        isneg = sb("a_isneg", [P, NP], U8)
        wt_hi = sb("a_wt_hi", [P, WR, GB * P], F32R)
        wt_lo = sb("a_wt_lo", [P, WR, GB * P], F32R)
        gw = sb("a_gw", [P, HEADS, KD, 2 * D], F32R)
        gw_raw = w_nat[:, SPI - 1, 0:HEADS * KD * D].rearrange("p (h k d) -> p h k d", h=HEADS, k=KD)
        mx = sb("a_mx", [P, SPI, 2], F32)
        carrier = sb("a_carrier", [P, SPI], F32)
        nmx = sb("a_nmx", [P, SPI], F32)
        ssum = sb("a_ssum", [P, SPI, 2], F32)
        s3 = sb("a_s3", [P, SPI], F32)
        rs = sb("a_rs", [P, SPI], F32)
        ghalf = sb("a_ghalf", [P, D], F32)
        g = sb("a_g", [P, D], F32)
        gT_hi = sb("a_gT_hi", [P, D], F32R)
        gT_lo = sb("a_gT_lo", [P, D], F32R)
        esT = sb("a_esT", [P, KD, P], F32)
        psW = ctx.enter_context(nc.psum_tensor("a_psW", [P, TR, 512], F32))
        psO = ctx.enter_context(nc.psum_tensor("a_psO", [P, 2, 512], F32))
        psG = ctx.enter_context(nc.psum_tensor("a_psG", [P, 512], F32))
        psX = ctx.enter_context(nc.psum_tensor("a_psX", [P, 512], F32))
        a_here = sem("a_a_here")
        gw_here = sem("a_gw_here")
        gw_hi = sem("a_gw_hi")
        gw_lo = sem("a_gw_lo")
        diag_off = sem("a_diag_off")
        mask_done = sem("a_mask_done")
        logits_done = sem("a_logits_done")
        nmx_done = sem("a_nmx_done")
        exp_done = sem("a_exp_done")
        w_pool = sem("a_w_pool")
        w_dve = sem("a_w_dve")
        tr_done = sem("a_tr_done")
        hi_done = sem("a_hi_done")
        lo_done = sem("a_lo_done")
        mm_done = sem("a_mm_done")
        rs_step = sem("a_rs_step")
        rs_done = sem("a_rs_done")
        ghalf_done = sem("a_ghalf_done")
        g_done = sem("a_g_done")
        gt_done = sem("a_gt_done")
        gT_hi_done = sem("a_gT_hi_done")
        gT_lo_done = sem("a_gT_lo_done")
        proj_done = sem("a_proj_done")
        ehalf_done = sem("a_ehalf_done")
        es_done = sem("a_es_done")
        est_done = sem("a_est_done")
        esT_done = sem("a_esT_done")
        esT_out = sem("a_esT_out")
        rare_here = sem("a_rare_here")
        block = ctx.enter_context(nc.Block())

        def at_least(eng, s, v):
            if not isinstance(v, int) or v > 0:
                eng.wait_ge(s, v)

        def later(i, k, by):
            return i + (k + by) // SPI, (k + by) % SPI

        def loop(eng, body):
            body(0, False)
            with eng.Fori(1, ITERS - 1) as i:
                body(i, False)
            body(ITERS - 1, True)

        @block.sync
        def _(sp):
            sp.dma_start(a_ring[:, 0], adj_n[0]).then_inc(a_here, 16)
            sp.wait_ge(a_here, 16)
            sp.dma_start(a_ring[:, 1], adj_n[1]).then_inc(a_here, 16)

        @block.gpsimd
        def _(pool):
            def weights(i, k):
                if k % HEADS == HEADS - 1:
                    return
                pool.wait_ge(exp_done, SPI * i + k + 1)
                w = w_nat[:, k]
                pool.tensor_tensor(w, w, a_ring[:, k // HEADS], ALU.mult).then_inc(w_pool, 1)

            def store(t):
                pool.wait_ge(esT_done, t + 1)
                pool.dma_start(es_dram[:, :, bass.ds(t * P, P)], esT[:]).then_inc(esT_out, 16)

            def body(i, last):
                for k in range(SPI):
                    if not (last and k + EE >= SPI):
                        weights(*later(i, k, EE))
                    if k % HEADS == HEADS - 1 and (k > HEADS or not isinstance(i, int) or i):
                        store(2 * i + k // HEADS - 1)
            for k in range(EE):
                weights(0, k)
            loop(pool, body)
            store(NT - 1)
            pool.wait_ge(esT_out, 16 * NT)

        @block.scalar
        def _(act):
            act.dma_start(gw_raw, gat_w_in).then_inc(gw_here, 16)
            has_negatives = act.value_load(sh["negtot"][0:1, 0:1])
            act.wait_ge(gw_here, 16)
            act.copy(gw[:, :, :, 0:D], gw_raw).then_inc(gw_hi, 1)
            act.wait_ge(gw_lo, 1)

            def rare(i, k):
                s = SPI * i + k
                with act.If(has_negatives > 0):
                    at_least(act, rare_here, 16 * s)
                    at_least(act, tr_done, NG * (s - SPI + 2))
                    act.dma_start(w_nat[:, (k + 1) % SPI],
                                  eminus_dram[k % HEADS:k % HEADS + 1, :].to_broadcast([P, NP])).then_inc(rare_here, 16)

            def exps(i, k, half):
                s = SPI * i + k
                if half == 0:
                    act.wait_ge(nmx_done, s + 1)
                    at_least(act, rs_done, s - SPI + 1)
                w = w_nat[:, k, half * HALF:(half + 1) * HALF]
                ins = act.activation(w, w, ACT.Exp, bias=nmx[:, k:k + 1], accum_out=ssum[:, k, half:half + 1])
                if half:
                    ins.then_inc(exp_done, 1)

            def hi_group(i, k, gi):
                q = GPI * i + k * NG + gi
                n = GSIZE[gi] * P
                act.wait_ge(tr_done, q + 1)
                at_least(act, mm_done, q - WR + 1)
                act.copy(wt_hi[:, (k * NG + gi) % WR, 0:n],
                         psW[:, (k * NG + gi) % TR, 0:n]).then_inc(hi_done, 1)

            def scaled_half(s, k, i=None):
                act.wait_ge(rs_done, s + 1)
                act.wait_ge(mm_done, NG * (s + 1))
                at_least(act, g_done, s)
                if k % HEADS == 0:
                    at_least(act, es_done, 2 * i + k // HEADS)
                act.mul(ghalf[:], psO[:, k % 2, D:2 * D], rs[:, k:k + 1]).then_inc(ghalf_done, 1)

            def gT_half(s):
                act.wait_ge(gt_done, s + 1)
                at_least(act, proj_done, s)
                act.copy(gT_hi[:], psG[:, 0:D]).then_inc(gT_hi_done, 1)

            def es_half(t):
                act.wait_ge(proj_done, HEADS * (t + 1))
                act.wait_ge(g_done, HEADS * (t + 1))
                act.copy(ghalf[:], psX[:, D:2 * D]).then_inc(ehalf_done, 1)

            def esT_copy(t):
                act.wait_ge(est_done, t + 1)
                at_least(act, esT_out, 16 * t)
                act.copy(esT[:], psG[:, 0:D].rearrange("p (k n) -> p k n", k=KD)).then_inc(esT_done, 1)

            def load(t, u):
                act.wait_ge(a_here, 16 * t)
                act.wait_ge(w_pool, 2 * (t - 1))
                act.wait_ge(w_dve, t - 1)
                act.dma_start(a_ring[:, u], adj_n[t]).then_inc(a_here, 16)

            def body(i, last):
                for k in range(SPI):
                    s = SPI * i + k
                    before = k > 0 or not isinstance(i, int) or i > 0
                    tile_before = k >= HEADS or not isinstance(i, int) or i > 0
                    ahead = not (last and k + EE >= SPI)
                    if not (last and k + LE + 1 >= SPI):
                        rare(*later(i, k, LE + 1))
                    hi_group(i, k, 0)
                    if ahead:
                        exps(*later(i, k, EE), 0)
                    hi_group(i, k, 1)
                    if k % HEADS == 1 and tile_before:
                        esT_copy(2 * i + k // HEADS - 1)
                    if ahead:
                        exps(*later(i, k, EE), 1)
                    hi_group(i, k, 2)
                    if before:
                        scaled_half(s - 1, (k - 1) % SPI, i)
                    hi_group(i, k, 3)
                    if before:
                        gT_half(s - 1)
                    hi_group(i, k, 4)
                    if k % HEADS == 1 and not last:
                        load(2 * i + k // HEADS + 2, k // HEADS)
                    hi_group(i, k, 5)
                    if k % HEADS == 0 and tile_before:
                        es_half(2 * i + k // HEADS - 1)
            for k in range(LE + 1):
                rare(0, k)
            for k in range(EE):
                exps(0, k, 0)
                exps(0, k, 1)
            loop(act, body)
            scaled_half(STEPS - 1, SPI - 1)
            gT_half(STEPS - 1)
            es_half(NT - 1)
            esT_copy(NT - 1)

        @block.vector
        def _(dve):
            has_negatives = dve.value_load(sh["negtot"][0:1, 0:1])
            dve.wait_ge(gw_hi, 1)
            dve.tensor_tensor(gw[:, :, :, D:2 * D], gw_raw, gw[:, :, :, 0:D].bitcast(F32),
                              ALU.subtract).then_inc(gw_lo, 1)
            dve.wait_ge(gw_lo, 1)

            def diagonal(i, u):
                t = 2 * i + u
                dve.wait_ge(a_here, 16 * (t + 1))
                d = a_ring[:, u, bass.ds(t * P, P)]
                dve.tensor_tensor(d, d, notid[:], ALU.mult).then_inc(diag_off, 1)

            def masks(i, u):
                t = 2 * i + u
                dve.wait_ge(diag_off, t + 1)
                at_least(dve, logits_done, HEADS * t)
                dve.tensor_scalar(mask[:], a_ring[:, u], 0.0, NEG_INF, ALU.is_equal, ALU.mult).then_inc(mask_done, 1)

            def logits(i, k, half):
                s = SPI * i + k
                c = slice(half * HALF, (half + 1) * HALF)
                if half == 0:
                    dve.wait_ge(mask_done, 2 * i + k // HEADS + 1)
                    at_least(dve, tr_done, NG * (s - SPI + 1))
                    at_least(dve, exp_done, s - SPI + 1)
                    dve.memset(carrier[:, k:k + 1], 0.0)
                ins = dve.tensor_tensor_reduce(w_nat[:, k, c], mask[:, c], logit[:, k % HEADS, c], 1.0, -3.0e38,
                                               ALU.add, ALU.max, mx[:, k, half:half + 1])
                if half:
                    ins.then_inc(logits_done, 1)

            def maximum(i, k):
                s = SPI * i + k
                with dve.If(has_negatives > 0):
                    dve.wait_ge(rare_here, 16 * (s + 1))
                    dve.tensor_scalar(isneg[:], a_ring[:, k // HEADS], 0.0, None, ALU.is_lt)
                    dve.drain()
                    dve.copy_predicated(w_nat[:, k], isneg[:], w_nat[:, (k + 1) % SPI])
                    dve.drain()
                    for half in range(2):
                        dve.tensor_reduce(mx[:, k, half:half + 1], w_nat[:, k, half * HALF:(half + 1) * HALF],
                                          AX.X, ALU.max)
                    dve.drain()
                dve.wait_ge(logits_done, s + 1)
                dve.tensor_scalar(nmx[:, k:k + 1], mx[:, k, 0:1], mx[:, k, 1:2], -1.0, ALU.max,
                                  ALU.mult).then_inc(nmx_done, 1)

            def weights(i, k, half):
                if half == 0:
                    dve.wait_ge(exp_done, SPI * i + k + 1)
                c = slice(half * HALF, (half + 1) * HALF)
                w = w_nat[:, k, c]
                ins = dve.tensor_tensor(w, w, a_ring[:, k // HEADS, c], ALU.mult)
                if half:
                    ins.then_inc(w_dve, 1)

            def lo_group(i, k, gi):
                q = GPI * i + k * NG + gi
                n = GSIZE[gi] * P
                slot = (k * NG + gi) % WR
                dve.wait_ge(hi_done, q + 1)
                dve.tensor_tensor(wt_lo[:, slot, 0:n], psW[:, (k * NG + gi) % TR, 0:n],
                                  wt_hi[:, slot, 0:n].bitcast(F32), ALU.subtract).then_inc(lo_done, 1)

            def scale(i, k):
                s = SPI * i + k
                dve.wait_ge(exp_done, s + 1)
                at_least(dve, g_done, s - SPI + 1)
                dve.tensor_scalar(s3[:, k:k + 1], ssum[:, k, 0:1], ssum[:, k, 1:2], float(HEADS), ALU.add,
                                  ALU.mult).then_inc(rs_step, 1)
                dve.wait_ge(rs_step, s + 1)
                dve.reciprocal(rs[:, k:k + 1], s3[:, k:k + 1]).then_inc(rs_done, 1)

            def gather(s, k, i=None):
                dve.wait_ge(ghalf_done, s + 1)
                at_least(dve, gt_done, s)
                if k % HEADS == 0:
                    at_least(dve, est_done, 2 * i + k // HEADS)
                dve.scalar_tensor_tensor(g[:], psO[:, k % 2, 0:D], rs[:, k:k + 1], ghalf[:],
                                         ALU.mult, ALU.add).then_inc(g_done, 1)

            def gT_half(s):
                dve.wait_ge(gT_hi_done, s + 1)
                dve.tensor_tensor(gT_lo[:], psG[:, 0:D], gT_hi[:].bitcast(F32), ALU.subtract).then_inc(gT_lo_done, 1)

            def es_sum(t):
                dve.wait_ge(ehalf_done, t + 1)
                dve.tensor_tensor(g[:], psX[:, 0:D], ghalf[:], ALU.add).then_inc(es_done, 1)

            def body(i, last):
                for k in range(SPI):
                    s = SPI * i + k
                    before = k > 0 or not isinstance(i, int) or i > 0
                    tile_before = k >= HEADS or not isinstance(i, int) or i > 0
                    more_logits = not (last and k + LE >= SPI)
                    dve_weights = k % HEADS == 0
                    lo_group(i, k, 0)
                    if more_logits:
                        logits(*later(i, k, LE), 0)
                    lo_group(i, k, 1)
                    if more_logits:
                        logits(*later(i, k, LE), 1)
                        maximum(*later(i, k, LE))
                    lo_group(i, k, 2)
                    if before:
                        gather(s - 1, (k - 1) % SPI, i)
                    lo_group(i, k, 3)
                    scale(i, k)
                    if dve_weights:
                        weights(*later(i, k, EE), 0)
                    elif k % HEADS == HEADS - 1 and not last:
                        diagonal(i + 1, k // HEADS)
                    if before:
                        gT_half(s - 1)
                    lo_group(i, k, 4)
                    if dve_weights:
                        weights(*later(i, k, EE), 1)
                    elif k % HEADS == HEADS - 1 and not last:
                        masks(i + 1, k // HEADS)
                    lo_group(i, k, 5)
                    if k % HEADS == 0 and tile_before:
                        es_sum(2 * i + k // HEADS - 1)
            diagonal(0, 0)
            masks(0, 0)
            for k in range(LE):
                logits(0, k, 0)
                logits(0, k, 1)
                maximum(0, k)
            diagonal(0, 1)
            masks(0, 1)
            loop(dve, body)
            gather(STEPS - 1, SPI - 1)
            gT_half(STEPS - 1)
            es_sum(NT - 1)

        @block.tensor
        def _(pe):
            def transposes(i, k, gi):
                if gi == 0:
                    t = 2 * i + k // HEADS
                    if k % HEADS == HEADS - 1:
                        pe.wait_ge(w_dve, t + 1)
                    else:
                        pe.wait_ge(w_pool, 2 * t + k % HEADS + 1)
                bank = (k * NG + gi) % TR
                for b in range(GSIZE[gi]):
                    j = gi * GB + b
                    last = pe.transpose(psW[:, bank, b * P:(b + 1) * P], w_nat[:, k, j * P:(j + 1) * P], ident[:])
                last.then_inc(tr_done, 1)

            def products(i, k, gi):
                slot = (k * NG + gi) % WR
                pe.wait_ge(lo_done, GPI * i + k * NG + gi + 1)
                if gi == 0:
                    at_least(pe, g_done, SPI * i + k - 1)
                for b in range(GSIZE[gi]):
                    j = gi * GB + b
                    c = slice(b * P, (b + 1) * P)
                    pe.matmul(psO[:, k % 2, :], wt_hi[:, slot, c], h_mov[:, j, :], start=(j == 0), stop=False)
                    last = pe.matmul(psO[:, k % 2, 0:D], wt_lo[:, slot, c], h_mov[:, j, 0:D], start=False,
                                     stop=(j == NT - 1))
                last.then_inc(mm_done, 1)

            def g_transposes(s, k, i=None):
                pe.wait_ge(g_done, s + 1)
                at_least(pe, gT_lo_done, s)
                if k % HEADS == 0:
                    at_least(pe, esT_done, 2 * i + k // HEADS)
                for c in range(KD):
                    last = pe.transpose(psG[:, c * P:(c + 1) * P], g[:, c * P:(c + 1) * P], ident[:])
                last.then_inc(gt_done, 1)

            def project(s, k, i=None):
                hd = k % HEADS
                pe.wait_ge(gT_lo_done, s + 1)
                if hd == 0:
                    at_least(pe, es_done, 2 * i + k // HEADS)
                for c in range(KD):
                    pe.matmul(psX[:], gT_hi[:, c * P:(c + 1) * P], gw[:, hd, c, :],
                              start=(hd == 0 and c == 0), stop=False)
                    last = pe.matmul(psX[:, 0:D], gT_lo[:, c * P:(c + 1) * P], gw[:, hd, c, 0:D],
                                     start=False, stop=(hd == HEADS - 1 and c == KD - 1))
                last.then_inc(proj_done, 1)

            def es_transposes(t):
                pe.wait_ge(es_done, t + 1)
                for c in range(KD):
                    last = pe.transpose(psG[:, c * P:(c + 1) * P], g[:, c * P:(c + 1) * P], ident[:])
                last.then_inc(est_done, 1)

            def body(i, last):
                for k in range(SPI):
                    s = SPI * i + k
                    before = k > 0 or not isinstance(i, int) or i > 0
                    tile_before = k >= HEADS or not isinstance(i, int) or i > 0
                    for gi in range(NG):
                        products(i, k, gi)
                        ahead = k * NG + gi + LT
                        if not (last and ahead >= GPI):
                            transposes(i + ahead // GPI, ahead % GPI // NG, ahead % NG)
                        if gi == 0 and k % HEADS == 1 and tile_before:
                            es_transposes(2 * i + k // HEADS - 1)
                        if gi == 2 and before:
                            g_transposes(s - 1, (k - 1) % SPI, i)
                        if gi == 4 and before:
                            project(s - 1, (k - 1) % SPI, i)
            pe.wait_ge(gw_lo, 1)
            for gi in range(LT):
                transposes(0, 0, gi)
            loop(pe, body)
            g_transposes(STEPS - 1, SPI - 1)
            project(STEPS - 1, SPI - 1)
            es_transposes(NT - 1)


def gru_stage(nc, ident, x1, stats, x_in, diag_in, gru_w_in, gru_b_in, s_dram, es_dram, h_dram):
    WIDTHS = [CH] * (NCH - 1) + [GSIZE[LAST] * P]
    UNITS = 4
    with ExitStack() as ctx:
        def sb(name, shape, dt):
            return ctx.enter_context(nc.sbuf_tensor(name, shape, dt))

        def sem(name):
            return ctx.enter_context(nc.semaphore(name))

        x = sb("r_x", [P, NT, D], F32)
        diag = sb("r_diag", [P, NT], F32)
        w_raw = sb("r_w_raw", [P, 2, KD, 3 * D], F32)
        w_hi = sb("r_w_hi", [P, 4, KD, 3 * D], F32R)
        w_lo = sb("r_w_lo", [P, 4, KD, 3 * D], F32R)
        b = sb("r_b", [P, 4, 3 * KD], F32)
        brz = sb("r_brz", [P, 2, 2 * KD], F32)
        raw = sb("r_raw", [P, 2, 3, KD, CH], F32)
        v_hi = sb("r_hi", [P, 2, 3, KD, CH], F32R)
        v_lo = sb("r_lo", [P, 2, 3, KD, CH], F32R)
        r = sb("r_r", [P, 2, CH], F32)
        z = sb("r_z", [P, 2, CH], F32)
        t1 = sb("r_t1", [P, CH], F32)
        t2 = sb("r_t2", [P, CH], F32)
        n = sb("r_n", [P, CH], F32)
        t3 = sb("r_t3", [P, CH], F32)
        t4 = sb("r_t4", [P, CH], F32)
        total = sb("r_total", [P, KD, CH], F32)
        psR = ctx.enter_context(nc.psum_tensor("r_psR", [P, 2, 512], F32))
        psZ = ctx.enter_context(nc.psum_tensor("r_psZ", [P, 2, 512], F32))
        psH = ctx.enter_context(nc.psum_tensor("r_psH", [P, 512], F32))
        psN = ctx.enter_context(nc.psum_tensor("r_psN", [P, 512], F32))
        psX = ctx.enter_context(nc.psum_tensor("r_psX", [P, 2, 512], F32))
        consts_here = sem("r_consts_here")
        x_here = sem("r_x_here")
        w_here = [sem(f"r_w_here{g}") for g in range(4)]
        w_hi_done = sem("r_w_hi_done")
        w_lo_done = sem("r_w_lo_done")
        brz_done = sem("r_brz_done")
        raw_here = sem("r_raw_here")
        v_hi_done = sem("r_v_hi_done")
        v_lo_done = sem("r_v_lo_done")
        r_ready = sem("r_r_ready")
        z_ready = sem("r_z_ready")
        h_ready = sem("r_h_ready")
        n_ready = sem("r_n_ready")
        r_done = sem("r_r_done")
        z_done = sem("r_z_done")
        t_step = sem("r_t_step")
        t2_done = sem("r_t2_done")
        n_done = sem("r_n_done")
        mix_step = sem("r_mix_step")
        mix_done = sem("r_mix_done")
        tr_done = sem("r_tr_done")
        x1_done = sem("r_x1_done")
        st_done = sem("r_st_done")
        block = ctx.enter_context(nc.Block())

        def positive(eng, s, v):
            if not isinstance(v, int) or v > 0:
                eng.wait_ge(s, v)

        def chunks(eng, body):
            body(0, WIDTHS[0])
            with eng.Fori(1, LAST) as c:
                body(c, CH)
            body(LAST, WIDTHS[LAST])

        @block.sync
        def _(sp):
            for g in range(4):
                if g >= 2:
                    sp.wait_ge(w_lo_done, g - 1)
                sp.dma_start(w_raw[:, g % 2], gru_w_in[g]).then_inc(w_here[g], 16)
                if g == 1:
                    sp.dma_start(b[:], gru_b_in).then_inc(consts_here, 16)
                    sp.dma_start(diag[:], diag_in).then_inc(consts_here, 16)
                    sp.dma_start(x[:], x_in.rearrange("t p d -> p t d")).then_inc(x_here, 16)

        @block.scalar
        def _(act):
            def load(c, w):
                positive(act, raw_here, 48 * c)
                positive(act, mix_done, UNITS * (c - 1))
                for m, src in enumerate((s_dram, es_dram, h_dram)):
                    act.dma_start(raw[:, c % 2, m, :, 0:w], src[:, :, bass.ds(c * CH, w)]).then_inc(raw_here, 16)

            def split(c, w):
                act.wait_ge(raw_here, 48 * (c + 1))
                positive(act, n_ready, UNITS * (c - 1))
                for m in range(3):
                    act.copy(v_hi[:, c % 2, m, :, 0:w], raw[:, c % 2, m, :, 0:w]).then_inc(v_hi_done, 1)

            def unit(c, u, w):
                g, f = u // KD, u % KD
                k = UNITS * c + u
                act.wait_ge(r_ready, k + 1)
                positive(act, mix_done, k - 1)
                act.activation(r[:, u % 2, 0:w], psR[:, u % 2, 0:w], ACT.Sigmoid,
                               bias=brz[:, g, f:f + 1]).then_inc(r_done, 1)
                act.wait_ge(z_ready, k + 1)
                act.activation(z[:, u % 2, 0:w], psZ[:, u % 2, 0:w], ACT.Sigmoid,
                               bias=brz[:, g, KD + f:KD + f + 1]).then_inc(z_done, 1)
                act.wait_ge(t2_done, k + 1)
                positive(act, mix_done, k)
                act.activation(n[:, 0:w], t2[:, 0:w], ACT.Tanh,
                               bias=b[:, 2 * g, 2 * KD + f:2 * KD + f + 1]).then_inc(n_done, 1)

            load(0, WIDTHS[0])
            for g in range(4):
                act.wait_ge(w_here[g], 16)
                act.copy(w_hi[:, g], w_raw[:, g % 2]).then_inc(w_hi_done, 1)
            load(1, WIDTHS[1])
            act.wait_ge(brz_done, 1)
            split(0, WIDTHS[0])

            def body(c, w):
                first = isinstance(c, int) and c == 0
                last = isinstance(c, int) and c == LAST
                for u in range(UNITS):
                    unit(c, u, w)
                    if u == 1 and not last:
                        split_next(c)
                if not last:
                    load_after(c)

            def split_next(c):
                if isinstance(c, int):
                    split(c + 1, WIDTHS[c + 1])
                else:
                    split(c + 1, CH)

            def load_after(c):
                if isinstance(c, int):
                    load(c + 2, WIDTHS[c + 2])
                else:
                    load(c + 2, CH)
            body(0, WIDTHS[0])
            with act.Fori(1, LAST - 2) as c:
                body(c, CH)
            for c in (LAST - 2, LAST - 1, LAST):
                for u in range(UNITS):
                    unit(c, u, WIDTHS[c])
                    if u == 1 and c < LAST:
                        split(c + 1, WIDTHS[c + 1])
                if c + 2 <= LAST:
                    load(c + 2, WIDTHS[c + 2])

        @block.vector
        def _(dve):
            dve.wait_ge(consts_here, 32)
            for g in range(2):
                last = dve.tensor_tensor(brz[:, g], b[:, 2 * g, 0:2 * KD], b[:, 2 * g + 1, 0:2 * KD], ALU.add)
            last.then_inc(brz_done, 1)
            for g in range(4):
                dve.wait_ge(w_hi_done, g + 1)
                dve.tensor_tensor(w_lo[:, g], w_raw[:, g % 2], w_hi[:, g].bitcast(F32),
                                  ALU.subtract).then_inc(w_lo_done, 1)

            def split(c, w):
                for m in range(3):
                    dve.wait_ge(v_hi_done, 3 * c + m + 1)
                    dve.tensor_tensor(v_lo[:, c % 2, m, :, 0:w], raw[:, c % 2, m, :, 0:w],
                                      v_hi[:, c % 2, m, :, 0:w].bitcast(F32), ALU.subtract).then_inc(v_lo_done, 1)

            def unit(c, u, w):
                g, f = u // KD, u % KD
                k = UNITS * c + u
                dve.wait_ge(r_done, k + 1)
                dve.wait_ge(h_ready, k + 1)
                dve.scalar_tensor_tensor(t1[:, 0:w], psH[:, 0:w], b[:, 2 * g + 1, 2 * KD + f:2 * KD + f + 1],
                                         r[:, u % 2, 0:w], ALU.add, ALU.mult).then_inc(t_step, 1)
                dve.wait_ge(t_step, k + 1)
                dve.wait_ge(n_ready, k + 1)
                positive(dve, n_done, k)
                dve.tensor_tensor(t2[:, 0:w], psN[:, 0:w], t1[:, 0:w], ALU.add).then_inc(t2_done, 1)
                dve.wait_ge(n_done, k + 1)
                dve.wait_ge(z_done, k + 1)
                hraw = raw[:, c % 2, 2, f, 0:w]
                dve.tensor_tensor(t3[:, 0:w], hraw, n[:, 0:w], ALU.subtract).then_inc(mix_step, 1)
                dve.wait_ge(mix_step, 3 * k + 1)
                dve.tensor_tensor(t4[:, 0:w], t3[:, 0:w], z[:, u % 2, 0:w], ALU.mult).then_inc(mix_step, 1)
                dve.wait_ge(mix_step, 3 * k + 2)
                if g == 0:
                    dve.tensor_tensor(total[:, f, 0:w], n[:, 0:w], t4[:, 0:w], ALU.add).then_inc(mix_step, 1)
                    dve.wait_ge(mix_step, 3 * k + 3)
                    dve.nop().then_inc(mix_done, 1)
                else:
                    dve.tensor_tensor(t3[:, 0:w], n[:, 0:w], t4[:, 0:w], ALU.add).then_inc(mix_step, 1)
                    dve.wait_ge(mix_step, 3 * k + 3)
                    dve.tensor_tensor(total[:, f, 0:w], total[:, f, 0:w], t3[:, 0:w], ALU.add).then_inc(mix_done, 1)

            def finish(c, tiles):
                for q in range(tiles):
                    t = GB * c + q
                    dve.wait_ge(tr_done, t + 1)
                    dve.scalar_tensor_tensor(x1[:, t], psX[:, q % 2, 0:D], diag[:, bass.ds(t, 1)], x[:, t],
                                             ALU.mult, ALU.add).then_inc(x1_done, 1)
                    dve.wait_ge(x1_done, t + 1)
                    dve.bn_stats(stats[:, t], x1[:, t]).then_inc(st_done, 1)

            split(0, WIDTHS[0])
            dve.wait_ge(x_here, 16)

            def body(c, w, nxt):
                if not (isinstance(c, int) and c == 0):
                    finish(c - 1, GB)
                for u in range(UNITS):
                    unit(c, u, w)
                    if u == 1 and nxt:
                        split(c + 1, nxt)
            body(0, WIDTHS[0], WIDTHS[1])
            with dve.Fori(1, LAST - 1) as c:
                body(c, CH, CH)
            body(LAST - 1, WIDTHS[LAST - 1], WIDTHS[LAST])
            body(LAST, WIDTHS[LAST], 0)
            finish(LAST, GSIZE[LAST])

        @block.tensor
        def _(pe):
            pe.wait_ge(w_lo_done, 4)

            def gate(ps, col, sources, c, w):
                terms = [(g, m, k, a, v) for g, m in sources for k in range(KD)
                         for a, v in ((w_hi, v_hi), (w_hi, v_lo), (w_lo, v_hi))]
                for j, (g, m, k, a, v) in enumerate(terms):
                    last = pe.matmul(ps[:, 0:w], a[:, g, k, col:col + P], v[:, c % 2, m, k, 0:w],
                                     start=(j == 0), stop=(j == len(terms) - 1))
                return last

            def unit(c, u, w):
                g, f = u // KD, u % KD
                k = UNITS * c + u
                ih, hh = (2 * g, g), (2 * g + 1, 2)
                positive(pe, r_done, k - 1)
                gate(psR[:, u % 2], f * P, (ih, hh), c, w).then_inc(r_ready, 1)
                positive(pe, z_done, k - 1)
                gate(psZ[:, u % 2], D + f * P, (ih, hh), c, w).then_inc(z_ready, 1)
                positive(pe, t_step, k)
                gate(psH, 2 * D + f * P, (hh,), c, w).then_inc(h_ready, 1)
                positive(pe, t2_done, k)
                gate(psN, 2 * D + f * P, (ih,), c, w).then_inc(n_ready, 1)

            def natural(c, tiles):
                pe.wait_ge(mix_done, UNITS * (c + 1))
                for q in range(tiles):
                    t = GB * c + q
                    if q >= 2:
                        pe.wait_ge(x1_done, t - 1)
                    for f in range(KD):
                        last = pe.transpose(psX[:, q % 2, f * P:(f + 1) * P], total[:, f, q * P:(q + 1) * P], ident[:])
                    last.then_inc(tr_done, 1)

            def body(c, w):
                pe.wait_ge(v_lo_done, 3 * (c + 1))
                unit(c, 0, w)
                if not (isinstance(c, int) and c == 0):
                    natural(c - 1, GB)
                for u in range(1, UNITS):
                    unit(c, u, w)
            chunks(pe, body)
            natural(LAST, GSIZE[LAST])


def ffn_stage(nc, ident, eps, x1, stats, wr_in, br_in, w1_in, b1_in, w2_in, b2_in,
              gamma_in, beta_in, out):
    WIDTHS = [CH] * (NCH - 1) + [GSIZE[LAST] * P]
    ROWS_LAST = N - (NT - 1) * P
    EF = TOP_K * FT
    with ExitStack() as ctx:
        def sb(name, shape, dt):
            return ctx.enter_context(nc.sbuf_tensor(name, shape, dt))

        def sem(name):
            return ctx.enter_context(nc.semaphore(name))

        mean = sb("f_mean", [P, NT], F32)
        var = sb("f_var", [P, NT], F32)
        tmp = sb("f_tmp", [P, NT], F32)
        rstd = sb("f_rstd", [P, NT], F32)
        xn = sb("f_xn", [P, NT, D], F32)
        xT_hi = sb("f_xT_hi", [P, KD, NP], F32R)
        xT_lo = sb("f_xT_lo", [P, KD, NP], F32R)
        ones = sb("f_ones", [P, P], F32)
        mT = sb("f_mT", [P, KD], F32)
        wr = sb("f_wr", [P, KD, E], F32)
        br = sb("f_br", [1, E], F32)
        row = sb("f_row", [1, 16, E], F32)
        col = sb("f_col", [1, 16], F32)
        idx = sb("f_idx", [1, E], U32)
        wb = sb("f_wb", [P, TOP_K], F32)
        w1r = sb("f_w1r", [P, TOP_K, KD, F], F32)
        w1_hi = sb("f_w1_hi", [P, TOP_K, KD, F], F32R)
        w1_lo = sb("f_w1_lo", [P, TOP_K, KD, F], F32R)
        w2r = sb("f_w2r", [P, TOP_K, FT, D], F32)
        w2 = sb("f_w2", [P, EF, 2 * D], F32R)
        b1 = sb("f_b1", [P, TOP_K, FT], F32)
        b2 = sb("f_b2", [P, TOP_K, D], F32)
        b2s = sb("f_b2s", [P, D], F32)
        gamma = sb("f_gamma", [P, D], F32)
        beta = sb("f_beta", [P, D], F32)
        hid = sb("f_hid", [P, 2, CH], F32)
        hid_hi = sb("f_hid_hi", [P, EF, CH], F32R)
        hid_lo = sb("f_hid_lo", [P, EF, CH], F32R)
        y = sb("f_y", [P, GB, D], F32)
        o = sb("f_o", [P, GB, D], F32)
        st = sb("f_st", [P, GB, 6], F32)
        mean3 = sb("f_mean3", [P, GB], F32)
        var3 = sb("f_var3", [P, GB], F32)
        tmp3 = sb("f_tmp3", [P, GB], F32)
        std3 = sb("f_std3", [P, GB], F32)
        rstd3 = sb("f_rstd3", [P, GB], F32)
        psT = ctx.enter_context(nc.psum_tensor("f_psT", [P, 3, 512], F32))
        psO = ctx.enter_context(nc.psum_tensor("f_psO", [P, GB, 512], F32))
        psM = ctx.enter_context(nc.psum_tensor("f_psM", [P, 512], F32))
        consts_here = sem("f_consts_here")
        dve_step = sem("f_dve_step")
        ones_set = sem("f_ones_set")
        var_done = sem("f_var_done")
        std_done = sem("f_std_done")
        xn_done = sem("f_xn_done")
        mean_ready = sem("f_mean_ready")
        mT_done = sem("f_mT_done")
        logits_ready = sem("f_logits_ready")
        ex_need = sem("f_ex_need")
        ex_done = sem("f_ex_done")
        idx_done = sem("f_idx_done")
        top_done = sem("f_top_done")
        wb_ready = sem("f_wb_ready")
        wb_done = sem("f_wb_done")
        xt_done = sem("f_xt_done")
        x_hi_done = sem("f_x_hi_done")
        x_lo_done = sem("f_x_lo_done")
        w_here = [sem(f"f_w_here{k}") for k in range(TOP_K)]
        w1_hi_done = sem("f_w1_hi_done")
        w1_lo_done = sem("f_w1_lo_done")
        w2_scaled = sem("f_w2_scaled")
        w2_hi_done = sem("f_w2_hi_done")
        w2_lo_done = sem("f_w2_lo_done")
        xb_done = sem("f_xb_done")
        x1b_done = sem("f_x1b_done")
        hid_ready = sem("f_hid_ready")
        gelu_done = sem("f_gelu_done")
        h_hi_done = sem("f_h_hi_done")
        h_lo_done = sem("f_h_lo_done")
        out_ready = sem("f_out_ready")
        y_step = sem("f_y_step")
        y_done = sem("f_y_done")
        v3_step = sem("f_v3_step")
        v3_done = sem("f_v3_done")
        s3_done = sem("f_s3_done")
        o_done = sem("f_o_done")
        og_done = sem("f_og_done")
        oo_done = sem("f_oo_done")
        stored = sem("f_stored")
        block = ctx.enter_context(nc.Block())

        def positive(eng, s, v):
            if not isinstance(v, int) or v > 0:
                eng.wait_ge(s, v)

        @block.sync
        def _(sp):
            for dst, src in ((wr, wr_in), (br, br_in), (gamma, gamma_in), (beta, beta_in)):
                sp.dma_start(dst[:], src).then_inc(consts_here, 16)
            sp.wait_ge(idx_done, 1)
            for k in range(TOP_K):
                e = sp.value_load(idx[0:1, k:k + 1], min_val=0, max_val=E - 1)
                sp.dma_start(w1r[:, k], w1_in[e]).then_inc(w_here[k], 16)
                sp.dma_start(w2r[:, k], w2_in[e]).then_inc(w_here[k], 16)
                sp.dma_start(b1[:, k], b1_in[e]).then_inc(w_here[k], 16)
                sp.dma_start(b2[:, k], b2_in[e]).then_inc(w_here[k], 16)

        @block.gpsimd
        def _(pool):
            pool.memset(ones[:], 1.0).then_inc(ones_set, 1)
            pool.wait_ge(consts_here, 64)
            pool.wait_ge(xn_done, NT)
            pool.tensor_tensor(x1[:], x1[:], beta[:].rearrange("p (o d) -> p o d", o=1).to_broadcast([P, NT, D]),
                               ALU.add).then_inc(x1b_done, 1)
            pool.wait_ge(x1b_done, 1)

            def finish(c, tiles):
                pool.wait_ge(o_done, GB * c + tiles)
                g = gamma[:].rearrange("p (o d) -> p o d", o=1).to_broadcast([P, tiles, D])
                pool.tensor_tensor(o[:, 0:tiles], o[:, 0:tiles], g, ALU.mult).then_inc(og_done, 1)
                pool.wait_ge(og_done, c + 1)
                pool.tensor_tensor(o[:, 0:tiles], o[:, 0:tiles], x1[:, bass.ds(GB * c, tiles)],
                                   ALU.add).then_inc(oo_done, 1)
                pool.wait_ge(oo_done, c + 1)
                pool.dma_start(out[bass.ds(GB * c, tiles)].rearrange("t p d -> p t d"),
                               o[:, 0:tiles]).then_inc(stored, 16)
            with pool.Fori(0, LAST) as c:
                finish(c, GB)
            finish(LAST, GSIZE[LAST])
            pool.wait_ge(stored, 16 * NCH)

        @block.scalar
        def _(act):
            act.wait_ge(var_done, 1)
            act.activation(tmp[:], var[:], ACT.Sqrt, bias=eps[:, 0:1]).then_inc(std_done, 1)
            act.wait_ge(mean_ready, 1)
            act.mul(mT[:], psM[:, 0:KD], 1.0 / N).then_inc(mT_done, 1)
            for j, (a, n) in enumerate(((1, E), (5, E), (9, TOP_K))):
                act.wait_ge(ex_need, j + 1)
                act.activation(row[:, a, 0:n], row[:, a - 1, 0:n], ACT.Exp, bias=col[:, 2 * j:2 * j + 1],
                               accum_out=col[:, 2 * j + 1:2 * j + 2]).then_inc(ex_done, 1)
            act.wait_ge(wb_ready, 1)
            act.copy(wb[:], psM[:, 32:32 + TOP_K]).then_inc(wb_done, 1)
            for g in range(NG):
                for k in range(KD):
                    j = KD * g + k
                    n = GSIZE[g] * P
                    act.wait_ge(xt_done, j + 1)
                    act.copy(xT_hi[:, k, g * CH:g * CH + n], psT[:, j % 3, 0:n]).then_inc(x_hi_done, 1)
            for k in range(TOP_K):
                act.wait_ge(w_here[k], 64)
                act.copy(w1_hi[:, k], w1r[:, k]).then_inc(w1_hi_done, 1)
                act.wait_ge(w2_scaled, k + 1)
                act.copy(w2[:, k * FT:(k + 1) * FT, 0:D], w2r[:, k]).then_inc(w2_hi_done, 1)

            def chunk(c, w):
                for e in range(EF):
                    j = EF * c + e
                    act.wait_ge(hid_ready, j + 1)
                    positive(act, h_lo_done, j - 1)
                    act.activation(hid[:, e % 2, 0:w], psT[:, e % 2, 0:w], ACT.Gelu,
                                   bias=b1[:, e // FT, e % FT:e % FT + 1]).then_inc(gelu_done, 1)
                    act.wait_ge(gelu_done, j + 1)
                    positive(act, out_ready, EF * (c - 1) + e + 1)
                    act.copy(hid_hi[:, e, 0:w], hid[:, e % 2, 0:w]).then_inc(h_hi_done, 1)
                act.wait_ge(v3_done, c + 1)
                act.activation(std3[:, 0:w // P], var3[:, 0:w // P], ACT.Sqrt, bias=eps[:, 0:1]).then_inc(s3_done, 1)
            chunk(0, WIDTHS[0])
            with act.Fori(1, LAST) as c:
                chunk(c, CH)
            chunk(LAST, WIDTHS[LAST])

        @block.vector
        def _(dve):
            chain = Chain(dve, dve_step)
            moments(dve, chain, stats, mean[:], var[:], tmp[:])
            dve.nop().then_inc(var_done, 1)
            dve.wait_ge(std_done, 1)
            chain(dve.reciprocal(rstd[:], tmp[:]))
            with dve.Fori(0, NT) as t:
                dve.tensor_scalar(xn[:, t], x1[:, t], mean[:, bass.ds(t, 1)], rstd[:, bass.ds(t, 1)],
                                  ALU.subtract, ALU.mult).then_inc(xn_done, 1)
            dve.wait_ge(consts_here, 64)
            dve.wait_ge(logits_ready, 1)
            lg, e1, rw, sc, e2 = (row[:, a] for a in (0, 1, 2, 3, 5))
            chain(dve.tensor_tensor(lg, psM[0:1, 16:16 + E], br[:], ALU.add))
            chain(dve.tensor_reduce(col[:, 0:1], lg, AX.X, ALU.max))
            dve.tensor_scalar(col[:, 0:1], col[:, 0:1], -1.0, None, ALU.mult).then_inc(ex_need, 1)
            dve.wait_ge(ex_done, 1)
            chain(dve.reciprocal(col[:, 6:7], col[:, 1:2]))
            chain(dve.tensor_scalar(rw, e1, col[:, 6:7], None, ALU.mult))
            chain(dve.tensor_scalar(sc, rw, float(N), 1e-30, ALU.mult, ALU.max))
            chain(dve.reciprocal(row[:, 6], sc))
            chain(dve.tensor_scalar(row[:, 6], row[:, 6], CAPACITY, 1.0, ALU.mult, ALU.min))
            chain(dve.tensor_tensor(row[:, 4], rw, row[:, 6], ALU.mult))
            chain(dve.tensor_reduce(col[:, 2:3], row[:, 4], AX.X, ALU.max))
            dve.tensor_scalar(col[:, 2:3], col[:, 2:3], -1.0, None, ALU.mult).then_inc(ex_need, 1)
            dve.wait_ge(ex_done, 2)
            chain(dve.reciprocal(col[:, 7:8], col[:, 3:4]))
            chain(dve.tensor_scalar(row[:, 7], e2, col[:, 7:8], None, ALU.mult))
            chain(dve.max(row[:, 8], row[:, 7]))
            dve.max_index(idx[:], row[:, 8], row[:, 7]).then_inc(idx_done, 1)
            dve.tensor_scalar(col[:, 4:5], row[:, 8, 0:1], -1.0, None, ALU.mult).then_inc(ex_need, 1)
            dve.wait_ge(ex_done, 3)
            chain(dve.reciprocal(col[:, 8:9], col[:, 5:6]))
            dve.tensor_scalar(row[:, 10, 0:TOP_K], row[:, 9, 0:TOP_K], col[:, 8:9], None, ALU.mult).then_inc(top_done, 1)
            for g in range(NG):
                for k in range(KD):
                    j = KD * g + k
                    n = GSIZE[g] * P
                    dve.wait_ge(x_hi_done, j + 1)
                    dve.tensor_tensor(xT_lo[:, k, g * CH:g * CH + n], psT[:, j % 3, 0:n],
                                      xT_hi[:, k, g * CH:g * CH + n].bitcast(F32), ALU.subtract).then_inc(x_lo_done, 1)
            dve.wait_ge(wb_done, 1)
            for k in range(TOP_K):
                dve.wait_ge(w_here[k], 64)
                dve.tensor_scalar(w2r[:, k], w2r[:, k], wb[:, k:k + 1], None, ALU.mult).then_inc(w2_scaled, 1)
                dve.wait_ge(w1_hi_done, k + 1)
                dve.tensor_tensor(w1_lo[:, k], w1r[:, k], w1_hi[:, k].bitcast(F32), ALU.subtract).then_inc(w1_lo_done, 1)
                dve.wait_ge(w2_hi_done, k + 1)
                dve.tensor_tensor(w2[:, k * FT:(k + 1) * FT, D:2 * D], w2r[:, k],
                                  w2[:, k * FT:(k + 1) * FT, 0:D].bitcast(F32), ALU.subtract).then_inc(w2_lo_done, 1)
            chain(dve.tensor_scalar(b2s[:], b2[:, 0], wb[:, 0:1], None, ALU.mult))
            chain(dve.scalar_tensor_tensor(b2s[:], b2[:, 1], wb[:, 1:2], b2s[:], ALU.mult, ALU.add))

            def chunk(c, w):
                tiles = w // P
                for e in range(EF):
                    j = EF * c + e
                    dve.wait_ge(h_hi_done, j + 1)
                    dve.tensor_tensor(hid_lo[:, e, 0:w], hid[:, e % 2, 0:w], hid_hi[:, e, 0:w].bitcast(F32),
                                      ALU.subtract).then_inc(h_lo_done, 1)
                    if e < tiles:
                        t = GB * c + e
                        dve.tensor_tensor(xn[:, t], xn[:, t], b2s[:], ALU.add).then_inc(xb_done, 1)
                dve.wait_ge(out_ready, EF * (c + 1))
                dve.wait_ge(xb_done, GB * c + tiles)
                for q in range(tiles):
                    t = GB * c + q
                    dve.tensor_tensor(y[:, q], psO[:, q, 0:D], xn[:, t], ALU.add).then_inc(y_step, 1)
                    dve.wait_ge(y_step, t + 1)
                    dve.tensor_tensor(y[:, q], psO[:, q, D:2 * D], y[:, q], ALU.add).then_inc(y_done, 1)
                for q in range(tiles):
                    dve.wait_ge(y_done, GB * c + q + 1)
                    last = dve.bn_stats(st[:, q], y[:, q])
                last.then_inc(v3_step, 1)
                dve.wait_ge(v3_step, 6 * c + 1)
                s_, m_, v_, p_ = st[:, 0:tiles], mean3[:, 0:tiles], var3[:, 0:tiles], tmp3[:, 0:tiles]
                dve.tensor_tensor(m_, s_[:, :, 1], s_[:, :, 4], ALU.add)
                dve.tensor_tensor(p_, s_[:, :, 1], s_[:, :, 4], ALU.subtract)
                dve.tensor_tensor(v_, s_[:, :, 2], s_[:, :, 5], ALU.add).then_inc(v3_step, 1)
                dve.wait_ge(v3_step, 6 * c + 2)
                dve.tensor_scalar(m_, m_, 0.5, None, ALU.mult)
                dve.scalar_tensor_tensor(p_, p_, 0.25, p_, ALU.mult, ALU.mult).then_inc(v3_step, 1)
                dve.wait_ge(v3_step, 6 * c + 3)
                dve.scalar_tensor_tensor(v_, v_, 1.0 / D, p_, ALU.mult, ALU.add).then_inc(v3_done, 1)
                dve.wait_ge(s3_done, c + 1)
                dve.reciprocal(rstd3[:, 0:tiles], std3[:, 0:tiles]).then_inc(v3_step, 1)
                dve.wait_ge(v3_step, 6 * c + 4)
                positive(dve, stored, 16 * c)
                for q in range(tiles):
                    dve.tensor_scalar(o[:, q], y[:, q], mean3[:, q:q + 1], rstd3[:, q:q + 1],
                                      ALU.subtract, ALU.mult).then_inc(o_done, 1)
                dve.wait_ge(o_done, GB * c + tiles)
                dve.nop().then_inc(v3_step, 2)
            chunk(0, WIDTHS[0])
            with dve.Fori(1, LAST) as c:
                chunk(c, CH)
            chunk(LAST, WIDTHS[LAST])

        @block.tensor
        def _(pe):
            pe.wait_ge(ones_set, 1)
            for k in range(KD):
                for t in range(NT):
                    pe.wait_ge(xn_done, t + 1)
                    rows = P if t < NT - 1 else ROWS_LAST
                    last = pe.matmul(psM[:, k:k + 1], xn[0:rows, t, k * P:(k + 1) * P], ones[0:rows, 0:1],
                                     start=(t == 0), stop=(t == NT - 1))
            last.then_inc(mean_ready, 1)
            pe.wait_ge(mT_done, 1)
            pe.wait_ge(consts_here, 64)
            for k in range(KD):
                last = pe.matmul(psM[0:1, 16:16 + E], mT[:, k:k + 1], wr[:, k], start=(k == 0), stop=(k == KD - 1))
            last.then_inc(logits_ready, 1)

            def x_transposes(j):
                g, k = j // KD, j % KD
                if j >= 3:
                    pe.wait_ge(x_lo_done, j - 2)
                for b in range(GSIZE[g]):
                    t = GB * g + b
                    last = pe.transpose(psT[:, j % 3, b * P:(b + 1) * P], xn[:, t, k * P:(k + 1) * P], ident[:])
                last.then_inc(xt_done, 1)
            for j in range(3):
                x_transposes(j)
            pe.wait_ge(top_done, 1)
            pe.matmul(psM[:, 32:32 + TOP_K], ones[0:1, :], row[:, 10, 0:TOP_K], start=True, stop=True).then_inc(wb_ready, 1)
            for j in range(3, KD * NG):
                x_transposes(j)
            pe.wait_ge(x_lo_done, KD * NG)
            pe.wait_ge(w1_lo_done, TOP_K)
            pe.wait_ge(w2_lo_done, TOP_K)

            def hidden(c, e, w):
                j = EF * c + e
                positive(pe, gelu_done, j - 1)
                ps = psT[:, e % 2, 0:w]
                x = e // FT
                cols = slice(e % FT * P, (e % FT + 1) * P)
                terms = [(k, a, v) for k in range(KD) for a, v in ((w1_hi, xT_hi), (w1_hi, xT_lo), (w1_lo, xT_hi))]
                for n, (k, a, v) in enumerate(terms):
                    last = pe.matmul(ps, a[:, x, k, cols], v[:, k, bass.ds(c * CH, w)],
                                     start=(n == 0), stop=(n == len(terms) - 1))
                last.then_inc(hid_ready, 1)

            def output(c, e, w):
                pe.wait_ge(h_lo_done, EF * c + e + 1)
                if e == 0:
                    positive(pe, y_done, GB * c)
                for q in range(w // P):
                    cols = slice(q * P, (q + 1) * P)
                    pe.matmul(psO[:, q, :], hid_hi[:, e, cols], w2[:, e, :], start=(e == 0), stop=False)
                    last = pe.matmul(psO[:, q, 0:D], hid_lo[:, e, cols], w2[:, e, 0:D], start=False,
                                     stop=(e == EF - 1))
                last.then_inc(out_ready, 1)

            def chunk(c, w):
                hidden(c, 0, w)
                hidden(c, 1, w)
                for e in range(EF):
                    output(c, e, w)
                    if e + 2 < EF:
                        hidden(c, e + 2, w)
            chunk(0, WIDTHS[0])
            with pe.Fori(1, LAST) as c:
                chunk(c, CH)
            chunk(LAST, WIDTHS[LAST])


def kernel(x, adj, L0_gnn_gat_W, L0_gnn_gat_a, L0_gnn_edge_Wih, L0_gnn_edge_Whh, L0_gnn_edge_bih, L0_gnn_edge_bhh,
           L0_gnn_node_Wih, L0_gnn_node_Whh, L0_gnn_node_bih, L0_gnn_node_bhh, L0_ffn_Wr, L0_ffn_br, L0_ffn_W1,
           L0_ffn_b1, L0_ffn_W2, L0_ffn_b2, L0_ffn_gamma, L0_ffn_beta):
    import numpy as np
    import concourse.bacc as bacc
    from concourse.bass_utils import run_bass_kernel_spmd

    def rows(a):
        a = np.asarray(a)
        return a.reshape((a.shape[0] // P, P) + a.shape[1:]).swapaxes(0, 1)

    adj = np.asarray(adj)
    xp = np.zeros((NP, D), np.float32)
    xp[:N] = np.asarray(x)
    ap = np.zeros((NP, NP), np.float32)
    ap[:N, :N] = adj
    dg = np.zeros((NP,), np.float32)
    dg[:N] = np.diagonal(adj)
    eye = np.eye(P, dtype=np.float32)
    gw = np.asarray(L0_gnn_gat_W)
    ga = np.asarray(L0_gnn_gat_a)
    gru = (L0_gnn_edge_Wih, L0_gnn_edge_Whh, L0_gnn_node_Wih, L0_gnn_node_Whh)
    gb = (L0_gnn_edge_bih, L0_gnn_edge_bhh, L0_gnn_node_bih, L0_gnn_node_bhh)
    arrays = {
        "x_tiles": xp.reshape(NT, P, D),
        "adj_t": ap.reshape(NT, P, NT, P).transpose(0, 3, 2, 1).reshape(NT, P, NP),
        "adj_n": ap.reshape(NT, P, NP),
        "diag": dg.reshape(NT, P).T,
        "ident": eye,
        "notid": np.ones((P, P), np.float32) - eye,
        "gat_wt": gw.transpose(0, 2, 1).reshape(HEADS, KD, P, D).transpose(2, 0, 1, 3),
        "gat_w": gw.reshape(HEADS, KD, P, D).transpose(2, 0, 1, 3),
        "gat_a": ga.reshape(HEADS, 2, KD, P).transpose(3, 0, 1, 2),
        "gru_w": np.stack([rows(np.asarray(w).T) for w in gru]),
        "gru_b": np.stack([np.asarray(v).reshape(3 * KD, P).T for v in gb], axis=1),
        "wr": rows(L0_ffn_Wr),
        "br": np.asarray(L0_ffn_br).reshape(1, E),
        "w1": np.stack([rows(w) for w in np.asarray(L0_ffn_W1)]),
        "b1": np.asarray(L0_ffn_b1).reshape(E, FT, P).transpose(0, 2, 1),
        "w2": np.stack([rows(w) for w in np.asarray(L0_ffn_W2)]),
        "b2": np.repeat(np.asarray(L0_ffn_b2)[:, None, :], P, axis=1),
        "gamma": np.repeat(np.asarray(L0_ffn_gamma)[None, :], P, axis=0),
        "beta": np.repeat(np.asarray(L0_ffn_beta)[None, :], P, axis=0),
    }
    nc = bacc.Bacc("TRN2", target_bir_lowering=False, num_devices=1)
    sent, args = {}, []
    for name, a in arrays.items():
        a = np.ascontiguousarray(a)
        sent[f"in_{name}"] = a
        args.append(nc.dram_tensor(f"in_{name}", a.shape, mybir.dt.from_np(a.dtype), kind="ExternalInput").ap())
    out = nc.dram_tensor("out_tiles", (NT, P, D), F32, kind="ExternalOutput").ap()
    build(nc, *args, out)
    r = run_bass_kernel_spmd(nc, [sent], core_ids=[0])
    return r.results[0]["out_tiles"].reshape(NP, D)[:N]
```

```python
from contextlib import ExitStack

import concourse.bass as bass
from concourse import mybir

P = 128
N = 2708
D = 256
KD = D // P
NT = (N + P - 1) // P
NP = NT * P
HEADS = 3
NC2 = 2 * HEADS
ALPHA = 0.2
NEG_INF = -9000000000000000.0
LN_EPS = 1e-5
E = 8
F = 512
FT = F // P
TOP_K = 2
CAPACITY = float(-(-N * 5 // (4 * E)))
GB = 4
NG = (NT + GB - 1) // GB
GSIZE = [min(GB, NT - GB * g) for g in range(NG)]
CH = GB * P
NCH = NG
LAST = NCH - 1
CROWS = 32
COPIES = 3
TAIL = (NT - 1) * P
assert N - TAIL <= CROWS and COPIES * CROWS <= P and COPIES == HEADS

F32 = mybir.dt.float32
F32R = mybir.dt.float32r
BF16 = mybir.dt.bfloat16
U32 = mybir.dt.uint32
U8 = mybir.dt.uint8
ALU = mybir.AluOpType
ACT = mybir.ActivationFunctionType
AX = mybir.AxisListType


class Chain:

    def __init__(self, eng, sem):
        self.eng, self.sem, self.n = eng, sem, 0

    def __call__(self, ins):
        self.n += 1
        ins.then_inc(self.sem, 1)
        self.eng.wait_ge(self.sem, self.n)


def build(nc, x_in, adj_t, adj_n, diag_in, ident_in, notid_in, gat_wt_in, gat_w_in, gat_a_in,
          gru_w_in, gru_b_in, wr_in, br_in, w1_in, b1_in, w2_in, b2_in, gamma_in, beta_in, out):
    s_dram = nc.dram_tensor("supportT_scratch", (P, KD, NP), F32, kind="Internal").ap()
    es_dram = nc.dram_tensor("attentionT_scratch", (P, KD, NP), F32, kind="Internal").ap()
    h_dram = nc.dram_tensor("normedT_scratch", (P, KD, NP), F32, kind="Internal").ap()
    eminus_dram = nc.dram_tensor("eminus_scratch", (HEADS, NP), F32, kind="Internal").ap()
    with ExitStack() as keep:
        def sb(name, shape, dt, ctx=keep):
            return ctx.enter_context(nc.sbuf_tensor(name, shape, dt))

        ident = sb("ident", [P, P], F32)
        eps = sb("eps", [P, 1], F32)
        a_ring = sb("a_ring", [P, 2, NP], F32)
        adj_t_here = keep.enter_context(nc.semaphore("adj_t_here"))
        adj_here = keep.enter_context(nc.semaphore("adj_here"))
        chunk0_here = keep.enter_context(nc.semaphore("chunk0_here"))
        gru_w_here = [keep.enter_context(nc.semaphore(f"gru_w_here{g}")) for g in range(4)]
        with ExitStack() as graph:
            shared = dict(
                ident=ident, eps=eps,
                notid=sb("notid", [P, 2, P], F32, graph),
                h_mov=sb("h_mov", [P, NT, 2 * D], F32R, graph),
                logit=sb("logit", [P, HEADS, NP], F32, graph),
                a_ring=a_ring,
                mask=sb("mask", [P, NP], BF16, graph),
                diag_off=graph.enter_context(nc.semaphore("diag_off")),
                mask_done=graph.enter_context(nc.semaphore("mask_done")),
                neg=sb("neg", [P, NT], F32, graph),
                negtot=sb("negtot", [P, 1], U32, graph),
            )
            with ExitStack() as sums:
                shared["up"] = sb("up", [P, NT, 20], BF16, sums)
                shared["ones"] = sb("ones", [P, P], F32, sums)
                shared["um"] = sb("um", [P, NT, 20], BF16, sums)
                norm_stage(nc, shared, x_in, ident_in, notid_in, gat_wt_in, gat_a_in, h_dram, adj_t,
                           adj_t_here)
                support_stage(nc, shared, adj_t, adj_t_here, s_dram, adj_n, adj_here)
                signed_stage(nc, shared, adj_t, eminus_dram)
            attention_stage(nc, shared, adj_n, adj_here, gat_w_in, es_dram, eminus_dram, gru_w_in,
                            gru_w_here, s_dram, h_dram, chunk0_here)
        x1 = sb("x1", [P, NT, D], F32)
        stats = sb("stats", [P, NT, 6], F32)
        gru_stage(nc, ident, a_ring, x1, stats, x_in, diag_in, gru_w_in, gru_w_here, chunk0_here, gru_b_in,
                  s_dram, es_dram, h_dram)
        ffn_stage(nc, ident, eps, a_ring, x1, stats, wr_in, br_in, w1_in, b1_in, w2_in, b2_in,
                  gamma_in, beta_in, out)


def moments(dve, chain, st, mean, var, tmp):
    chain(dve.tensor_tensor(mean, st[:, :, 1], st[:, :, 4], ALU.add))
    chain(dve.tensor_scalar(mean, mean, 0.5, None, ALU.mult))
    chain(dve.tensor_tensor(tmp, st[:, :, 1], st[:, :, 4], ALU.subtract))
    chain(dve.scalar_tensor_tensor(tmp, tmp, 0.25, tmp, ALU.mult, ALU.mult))
    chain(dve.tensor_tensor(var, st[:, :, 2], st[:, :, 5], ALU.add))
    chain(dve.scalar_tensor_tensor(var, var, 1.0 / D, tmp, ALU.mult, ALU.add))


def norm_stage(nc, sh, x_in, ident_in, notid_in, gat_wt_in, gat_a_in, h_dram, adj_t, adj_t_here):
    ident, h_mov, up, um = sh["ident"], sh["h_mov"], sh["up"], sh["um"]
    XC = [0, 6, 12, 18, NT]
    PAIRS = NT // 2
    with ExitStack() as ctx:
        def sb(name, shape, dt):
            return ctx.enter_context(nc.sbuf_tensor(name, shape, dt))

        def sem(name):
            return ctx.enter_context(nc.semaphore(name))

        x = sb("n_x", [P, NT, D], F32)
        st = sb("n_st", [P, NT, 6], F32)
        mean = sb("n_mean", [P, NT], F32)
        var = sb("n_var", [P, NT], F32)
        tmp = sb("n_tmp", [P, NT], F32)
        rstd = sb("n_rstd", [P, NT], F32)
        h = sb("n_h", [P, 2, 2, D], F32)
        hT = sb("n_hT", [P, 2, KD, 2 * P], F32)
        gwt = sb("n_gwt", [P, HEADS, KD, D], F32)
        ga = sb("n_ga", [P, HEADS, 2, KD], F32)
        wa = sb("n_wa", [P, KD, 2, HEADS], F32)
        r1 = sb("n_r1", [P, NT, NC2], F32)
        psT = ctx.enter_context(nc.psum_tensor("n_psT", [P, 2, 512], F32))
        psV = ctx.enter_context(nc.psum_tensor("n_psV", [P, KD, 2, HEADS], F32))
        psU = ctx.enter_context(nc.psum_tensor("n_psU", [P, 512], F32))
        x_here = [sem(f"n_x_here{c}") for c in range(len(XC) - 1)]
        consts_here = sem("n_consts_here")
        consts_set = sem("n_consts_set")
        dve_step = sem("n_dve_step")
        stats_done = sem("n_stats_done")
        var_done = sem("n_var_done")
        std_done = sem("n_std_done")
        rstd_done = sem("n_rstd_done")
        h_done = sem("n_h_done")
        hi_done = sem("n_hi_done")
        lo_done = sem("n_lo_done")
        tr_done = sem("n_tr_done")
        hT_done = sem("n_hT_done")
        u_done = sem("n_u_done")
        wa_ready = sem("n_wa_ready")
        wa_copied = sem("n_wa_copied")
        hT_out = [sem(f"n_hT_out{u}") for u in range(2)]
        block = ctx.enter_context(nc.Block())

        @block.sync
        def _(sp):
            for c in range(len(XC) - 1):
                sp.dma_start(x[:, XC[c]:XC[c + 1], :],
                             x_in[XC[c]:XC[c + 1]].rearrange("t p d -> p t d")).then_inc(x_here[c], 16)
            sp.wait_ge(x_here[-1], 16)
            sp.dma_start(sh["a_ring"][:, 0], adj_t[0]).then_inc(adj_t_here, 16)
            sp.wait_ge(adj_t_here, 16)
            sp.dma_start(sh["a_ring"][:, 1], adj_t[1]).then_inc(adj_t_here, 16)

        @block.gpsimd
        def _(pool):
            pool.memset(sh["ones"][:], 1.0).then_inc(consts_set, 1)
            pool.memset(sh["eps"][:], LN_EPS).then_inc(consts_set, 1)
            pool.memset(up[:], 0.0).then_inc(consts_set, 1)
            pool.memset(um[:], 0.0).then_inc(consts_set, 1)

            def store(p, u):
                pool.wait_ge(hT_done, p + 1)
                pool.dma_start(h_dram[:, :, bass.ds(p * 2 * P, 2 * P)], hT[:, u]).then_inc(hT_out[u], 16)
            with pool.Fori(0, PAIRS // 2) as i:
                store(2 * i, 0)
                store(2 * i + 1, 1)
            store(PAIRS - 1, 0)
            pool.wait_ge(hT_out[0], 16 * (PAIRS // 2 + 1))
            pool.wait_ge(hT_out[1], 16 * (PAIRS // 2))

        @block.scalar
        def _(act):
            act.dma_start(ident[:], ident_in).then_inc(consts_here, 16)
            act.dma_start(sh["notid"][:], notid_in).then_inc(consts_here, 16)
            act.dma_start(gwt[:], gat_wt_in).then_inc(consts_here, 16)
            act.dma_start(ga[:], gat_a_in).then_inc(consts_here, 16)
            act.wait_ge(var_done, 1)
            act.wait_ge(consts_set, 4)
            act.activation(tmp[:], var[:], ACT.Sqrt, bias=eps_of(sh)).then_inc(std_done, 1)
            act.wait_ge(wa_ready, 1)
            act.copy(wa[:], psV[:]).then_inc(wa_copied, 1)

            def high(p, u):
                act.wait_ge(h_done, p + 1)
                act.copy(h_mov[:, bass.ds(2 * p, 2), 0:D], h[:, u]).then_inc(hi_done, 1)

            def hT_copy(p, u, i):
                act.wait_ge(tr_done, p + 1)
                if not isinstance(i, int) or i:
                    act.wait_ge(u_done, p - 1)
                    act.wait_ge(hT_out[u], 16 * i)
                act.copy(hT[:, u], psT[:, u].rearrange("p (t k n) -> p k t n", t=2, k=KD)).then_inc(hT_done, 1)

            def turns(i):
                hT_copy(2 * i, 0, i)
                high(2 * i + 1, 1)
                hT_copy(2 * i + 1, 1, i)
                high(2 * i + 2, 0)
            high(0, 0)
            turns(0)
            with act.Fori(1, PAIRS // 2) as i:
                turns(i)
            hT_copy(PAIRS - 1, 0, PAIRS // 2)

        @block.vector
        def _(dve):
            chain = Chain(dve, dve_step)
            for c in range(len(XC) - 1):
                dve.wait_ge(x_here[c], 16)
                for t in range(XC[c], XC[c + 1]):
                    dve.bn_stats(st[:, t], x[:, t]).then_inc(stats_done, 1)
            dve.wait_ge(stats_done, NT)
            moments(dve, chain, st, mean[:], var[:], tmp[:])
            dve.nop().then_inc(var_done, 1)
            dve.wait_ge(std_done, 1)
            dve.reciprocal(rstd[:], tmp[:]).then_inc(rstd_done, 1)
            dve.wait_ge(rstd_done, 1)

            def normalise(p, u, started=True):
                if started:
                    dve.wait_ge(tr_done, p - 1)
                    dve.wait_ge(lo_done, p - 1)
                for q in range(2):
                    t = 2 * p + q
                    last = dve.tensor_scalar(h[:, u, q], x[:, t], mean[:, bass.ds(t, 1)], rstd[:, bass.ds(t, 1)],
                                             ALU.subtract, ALU.mult)
                last.then_inc(h_done, 1)

            def low(p, u):
                dve.wait_ge(hi_done, p + 1)
                dve.tensor_tensor(h_mov[:, bass.ds(2 * p, 2), D:2 * D], h[:, u],
                                  h_mov[:, bass.ds(2 * p, 2), 0:D].bitcast(F32), ALU.subtract).then_inc(lo_done, 1)

            def turn(p, u, started=True):
                normalise(p, u, started)
                low(p - 1, 1 - u)
            normalise(0, 0, False)
            turn(1, 1, False)
            turn(2, 0)
            with dve.Fori(1, PAIRS // 2) as i:
                turn(2 * i + 1, 1)
                turn(2 * i + 2, 0)
            low(PAIRS - 1, 0)
            dve.wait_ge(lo_done, PAIRS)
            dve.tensor_copy(h_mov[CROWS:2 * CROWS, NT - 1, 0:D], h_mov[CROWS:2 * CROWS, NT - 1, D:2 * D].bitcast(F32))
            dve.wait_ge(u_done, PAIRS)
            dve.wait_ge(consts_set, 4)
            u = psU[:, 0:NT * NC2].rearrange("p (t c) -> p t c", c=NC2)
            chain(dve.tensor_copy(up[:, :, 0:NC2], u))
            chain(dve.tensor_tensor(r1[:], u, up[:, :, 0:NC2], ALU.subtract))
            chain(dve.tensor_copy(up[:, :, NC2:2 * NC2], r1[:]))
            chain(dve.tensor_tensor(r1[:], r1[:], up[:, :, NC2:2 * NC2], ALU.subtract))
            chain(dve.tensor_copy(up[:, :, 2 * NC2:3 * NC2], r1[:]))
            upv = up[:, :, 0:3 * NC2].rearrange("p t (q s h) -> p t q s h", q=3, s=2)
            umv = um[:, :, 0:3 * NC2].rearrange("p t (q s h) -> p t q s h", q=3, s=2)
            for s in range(2):
                dve.tensor_copy(umv[:, :, :, s, :], upv[:, :, :, 1 - s, :])

        @block.tensor
        def _(pe):
            pe.wait_ge(consts_here, 64)
            for hd in range(HEADS):
                for m in range(KD):
                    for k in range(KD):
                        last = pe.matmul(psV[:, m, :, hd], gwt[:, hd, k, m * P:(m + 1) * P], ga[:, hd, :, k],
                                         start=(k == 0), stop=(k == KD - 1))
            last.then_inc(wa_ready, 1)
            pe.wait_ge(wa_copied, 1)

            def transposes(p, u, started=True):
                pe.wait_ge(h_done, p + 1)
                if started:
                    pe.wait_ge(hT_done, p - 1)
                for q in range(2):
                    for k in range(KD):
                        last = pe.transpose(psT[:, u, (KD * q + k) * P:(KD * q + k + 1) * P],
                                            h[:, u, q, k * P:(k + 1) * P], ident[:])
                last.then_inc(tr_done, 1)

            def project(p, u):
                pe.wait_ge(hT_done, p + 1)
                for q in range(2):
                    for k in range(KD):
                        last = pe.matmul(psU[:, bass.ds((2 * p + q) * NC2, NC2)], hT[:, u, k, q * P:(q + 1) * P],
                                         wa[:, k].rearrange("p s h -> p (s h)"), start=(k == 0), stop=(k == KD - 1))
                last.then_inc(u_done, 1)

            def turn(p, u, started=True):
                transposes(p, u, started)
                project(p - 1, 1 - u)
            transposes(0, 0, False)
            turn(1, 1, False)
            turn(2, 0)
            with pe.Fori(1, PAIRS // 2) as i:
                turn(2 * i + 1, 1)
                turn(2 * i + 2, 0)
            project(PAIRS - 1, 0)


def copy_tail_logits(act, logit):
    for copy in range(1, COPIES):
        c = slice(TAIL + CROWS * copy, TAIL + CROWS * (copy + 1))
        act.copy(logit[:, :, c], logit[:, :, TAIL:TAIL + CROWS])


def eps_of(sh):
    return sh["eps"][:, 0:1]


def support_stage(nc, sh, adj_t, a_here, s_dram, adj_n, adj_here):
    ident, ones, notid, h_mov, logit = sh["ident"], sh["ones"], sh["notid"], sh["h_mov"], sh["logit"]
    a_ring, up, um, neg = sh["a_ring"], sh["up"], sh["um"], sh["neg"]
    with ExitStack() as ctx:
        def sb(name, shape, dt):
            return ctx.enter_context(nc.sbuf_tensor(name, shape, dt))

        def sem(name):
            return ctx.enter_context(nc.semaphore(name))

        hi = sb("s_hi", [P, 2, NP], F32R)
        lo = sb("s_lo", [P, 2, TAIL], F32R)
        pos = sb("s_pos", [P, 2, NP], BF16)
        negpart = sb("s_negpart", [P, NP], BF16)
        half = sb("s_half", [P, D], F32)
        s = sb("s_s", [P, D], F32)
        sT = sb("s_sT", [P, KD, P], F32)
        e0 = sb("s_e0", [P, NC2], F32)
        e1 = sb("s_e1", [P, NC2], F32)
        negsum = sb("s_negsum", [P, 1], F32)
        anyneg = sb("s_anyneg", [P, 1], F32)
        psS = ctx.enter_context(nc.psum_tensor("s_psS", [P, 2, 512], F32))
        psE = ctx.enter_context(nc.psum_tensor("s_psE", [P, 2, 512], F32))
        psT = ctx.enter_context(nc.psum_tensor("s_psT", [P, 512], F32))
        psB = ctx.enter_context(nc.psum_tensor("s_psB", [P, 512], F32))
        diag_off = sem("s_diag_off")
        hi_done = sem("s_hi_done")
        lo_done = sem("s_lo_done")
        masks_done = sem("s_masks_done")
        mains_done = sem("s_mains_done")
        half_done = sem("s_half_done")
        s_done = sem("s_s_done")
        sum_done = sem("s_sum_done")
        e_done = sem("s_e_done")
        posts_done = sem("s_posts_done")
        sT_done = sem("s_sT_done")
        bcast_done = sem("s_bcast_done")
        sT_out = sem("s_sT_out")
        neg_here = sem("s_neg_here")
        neg_all = sem("s_neg_all")
        last_out = sem("s_last_out")
        neg_done = sem("s_neg_done")
        negsum_done = sem("s_negsum_done")
        block = ctx.enter_context(nc.Block())

        @block.sync
        def _(sp):
            for u in range(2):
                sp.wait_ge(masks_done, NT - 1 + u)
                sp.wait_ge(lo_done, NT - 1 + u)
                sp.wait_ge(neg_done, NT - 1 + u)
                if u:
                    sp.wait_ge(adj_here, 16)
                sp.dma_start(a_ring[:, u], adj_n[u]).then_inc(adj_here, 16)
            sp.wait_ge(sT_done, NT)
            sp.dma_start(s_dram[:, :, TAIL:NP], sT[:]).then_inc(last_out, 16)
            sp.wait_ge(last_out, 16)

        @block.gpsimd
        def _(pool):
            def store(t):
                pool.wait_ge(sT_done, t + 1)
                pool.dma_start(s_dram[:, :, bass.ds(t * P, P)], sT[:]).then_inc(sT_out, 16)
                pool.wait_ge(sT_out, 16 * (t + 1))
            with pool.Fori(0, NT - 1) as t:
                store(t)
            pool.wait_ge(sT_out, 16 * (NT - 1))

        @block.scalar
        def _(act):
            def split(t, u):
                act.wait_ge(diag_off, t + 1)
                if not isinstance(t, int) or t >= 2:
                    act.wait_ge(mains_done, t - 1)
                act.copy(hi[:, u], a_ring[:, u]).then_inc(hi_done, 1)
                if not isinstance(t, int) or t:
                    act.wait_ge(neg_done, t)
                act.activation(negpart[:], a_ring[:, u], ACT.Relu, scale=-1.0,
                               accum_out=neg[:, bass.ds(t, 1)]).then_inc(neg_done, 1)

            def load(t, u):
                act.wait_ge(a_here, 16 * t)
                act.wait_ge(lo_done, t - 1)
                act.wait_ge(masks_done, t - 1)
                act.wait_ge(neg_done, t - 1)
                act.dma_start(a_ring[:, u], adj_t[t]).then_inc(a_here, 16)

            def halves(t, u):
                act.wait_ge(mains_done, t + 1)
                if not isinstance(t, int) or t:
                    act.wait_ge(s_done, t)
                act.copy(half[:], psS[:, u, D:2 * D]).then_inc(half_done, 1)

            def results(t):
                act.wait_ge(posts_done, t + 1)
                if not isinstance(t, int) or t:
                    act.wait_ge(sT_out, 16 * t)
                act.copy(sT[:], psT[:, 0:D].rearrange("p (k n) -> p k n", k=KD)).then_inc(sT_done, 1)
                act.copy(logit[:, :, bass.ds(t * P, P)],
                         psB[:, 0:HEADS * P].rearrange("p (c n) -> p c n", c=HEADS)).then_inc(bcast_done, 1)

            def turn(t, u, more, load_more):
                halves(t - 1, 1 - u)
                if more:
                    split(t + 1, 1 - u)
                if load_more:
                    load(t + 2, u)
                results(t - 1)
            split(0, 0)
            split(1, 1)
            load(2, 0)
            for t in (1, 2):
                turn(t, t % 2, True, True)
            with act.Fori(1, NT // 2 - 2) as i:
                turn(2 * i + 1, 1, True, True)
                turn(2 * i + 2, 0, True, True)
            turn(NT - 3, 1, True, True)
            turn(NT - 2, 0, True, False)
            turn(NT - 1, 1, False, False)
            halves(NT - 1, 1)
            results(NT - 1)
            act.wait_ge(bcast_done, NT)
            copy_tail_logits(act, logit)

        @block.vector
        def _(dve):
            def prepare(t, u):
                dve.wait_ge(a_here, 16 * (t + 1))
                d = a_ring[:, u, bass.ds(t * P, P)]
                dve.tensor_tensor(d, d, notid[:, t // (NT - 1)], ALU.mult).then_inc(diag_off, 1)
                dve.wait_ge(diag_off, t + 1)
                if not isinstance(t, int) or t >= 2:
                    dve.wait_ge(mains_done, t - 1)
                dve.tensor_scalar(pos[:, u], a_ring[:, u], 0.0, None, ALU.is_gt).then_inc(masks_done, 1)
                dve.wait_ge(hi_done, t + 1)
                dve.tensor_tensor(lo[:, u, 0:TAIL], a_ring[:, u, 0:TAIL], hi[:, u, 0:TAIL].bitcast(F32), ALU.subtract)
                c3 = slice(2 * CROWS, 3 * CROWS)
                dve.tensor_tensor(hi[c3, u, TAIL:NP], a_ring[c3, u, TAIL:NP], hi[c3, u, TAIL:NP].bitcast(F32),
                                  ALU.subtract).then_inc(lo_done, 1)

            def post(t, u):
                dve.wait_ge(mains_done, t + 1)
                if not isinstance(t, int) or t:
                    dve.wait_ge(posts_done, t)
                dve.tensor_reduce(e0[:], psE[:, u, 0:3 * NC2].rearrange("p (q c) -> p c q", q=3), AX.X,
                                  ALU.add).then_inc(sum_done, 1)
                dve.wait_ge(sum_done, t + 1)
                dve.scalar_tensor_tensor(e1[:], e0[:], ALPHA, e0[:], ALU.mult, ALU.max).then_inc(e_done, 1)
                dve.wait_ge(half_done, t + 1)
                dve.tensor_tensor(s[:], psS[:, u, 0:D], half[:], ALU.add).then_inc(s_done, 1)

            def turn(t, u):
                post(t - 1, 1 - u)
                prepare(t + 1, 1 - u)
            prepare(0, 0)
            prepare(1, 1)
            for t in (1, 2):
                turn(t, t % 2)
            with dve.Fori(1, NT // 2 - 1) as i:
                turn(2 * i + 1, 1)
                turn(2 * i + 2, 0)
            post(NT - 2, 0)
            dve.wait_ge(adj_here, 16)
            first = a_ring[:, 0, 0:P]
            dve.tensor_tensor(first, first, notid[:, 0], ALU.mult).then_inc(sh["diag_off"], 1)
            dve.wait_ge(sh["diag_off"], 1)
            dve.tensor_scalar(sh["mask"][:], a_ring[:, 0], 0.0, NEG_INF, ALU.is_equal,
                              ALU.mult).then_inc(sh["mask_done"], 1)
            post(NT - 1, 1)
            dve.wait_ge(e_done, NT)
            dve.wait_ge(neg_done, NT)
            dve.tensor_reduce(negsum[:], neg[:], AX.X, ALU.add).then_inc(negsum_done, 1)
            dve.wait_ge(negsum_done, 1)
            dve.tensor_scalar(anyneg[:], negsum[:], 0.0, None, ALU.is_gt).then_inc(neg_here, 1)
            dve.wait_ge(neg_all, 1)
            dve.tensor_copy(sh["negtot"][:], psT[:, 256:257])

        @block.tensor
        def _(pe):
            def main(t, u, between):
                pe.wait_ge(masks_done, t + 1)
                for j in range(NT):
                    b = slice(j * P, (j + 1) * P)
                    r = slice(0, P if j < NT - 1 else CROWS)
                    pe.matmul(psE[:, u, 0:3 * NC2], pos[r, u, b], up[r, j, 0:3 * NC2], start=(j == 0), stop=(j == NT - 1))
                pe.wait_ge(hi_done, t + 1)
                pe.wait_ge(lo_done, t + 1)
                for j in range(NT - 1):
                    if j == NT // 4:
                        between()
                    b = slice(j * P, (j + 1) * P)
                    pe.matmul(psS[:, u, :], hi[:, u, b], h_mov[:, j, :], start=(j == 0), stop=False)
                    pe.matmul(psS[:, u, 0:D], lo[:, u, b], h_mov[:, j, 0:D], start=False, stop=False)
                pe.matmul(psS[:, u, 0:D], hi[:, u, TAIL:NP], h_mov[:, NT - 1, 0:D], start=False,
                          stop=True).then_inc(mains_done, 1)

            def post(t):
                pe.wait_ge(e_done, t + 1)
                if not isinstance(t, int) or t:
                    pe.wait_ge(bcast_done, t)
                for c in range(HEADS):
                    pe.matmul(psB[:, c * P:(c + 1) * P],
                              e1[:, c:c + 1].to_broadcast([P, P]), ident[:], start=True, stop=True)
                pe.wait_ge(s_done, t + 1)
                for k in range(KD):
                    last = pe.transpose(psT[:, k * P:(k + 1) * P], s[:, k * P:(k + 1) * P], ident[:])
                last.then_inc(posts_done, 1)
            main(0, 0, lambda: None)
            main(1, 1, lambda: post(0))
            main(2, 0, lambda: post(1))
            with pe.Fori(1, NT // 2 - 1) as i:
                main(2 * i + 1, 1, lambda: post(2 * i))
                main(2 * i + 2, 0, lambda: post(2 * i + 1))
            main(NT - 1, 1, lambda: post(NT - 2))
            post(NT - 1)
            pe.wait_ge(neg_here, 1)
            pe.wait_ge(bcast_done, NT)
            pe.matmul(psT[:, 256:257], ones[:], anyneg[:], start=True, stop=True).then_inc(neg_all, 1)


def signed_stage(nc, sh, adj_t, eminus_dram):
    ident, notid, logit, up, um = sh["ident"], sh["notid"], sh["logit"], sh["up"], sh["um"]
    with ExitStack() as ctx:
        def sb(name, shape, dt):
            return ctx.enter_context(nc.sbuf_tensor(name, shape, dt))

        def sem(name):
            return ctx.enter_context(nc.semaphore(name))

        raw = sb("g_raw", [P, NP], F32)
        pos = sb("g_pos", [P, NP], BF16)
        ngt = sb("g_neg", [P, NP], BF16)
        e0 = sb("g_e0", [P, NC2], F32)
        e1 = sb("g_e1", [P, NC2], F32)
        eminus = sb("g_eminus", [HEADS, NP], F32)
        psE = ctx.enter_context(nc.psum_tensor("g_psE", [P, 512], F32))
        psB = ctx.enter_context(nc.psum_tensor("g_psB", [P, 2, 512], F32))
        raw_here = sem("g_raw_here")
        diag_off = sem("g_diag_off")
        masks_done = sem("g_masks_done")
        sums_done = sem("g_sums_done")
        sum_step = sem("g_sum_step")
        e_done = sem("g_e_done")
        bcast_ready = sem("g_bcast_ready")
        bcast_done = sem("g_bcast_done")
        copies_done = sem("g_copies_done")
        eminus_out = sem("g_eminus_out")
        block = ctx.enter_context(nc.Block())

        def tiles(eng, tile):
            tile(0)
            with eng.Fori(1, NT) as t:
                tile(t)

        @block.scalar
        def _(act):
            has_negatives = act.value_load(sh["negtot"][0:1, 0:1])

            def tile(t):
                if not isinstance(t, int):
                    act.wait_ge(masks_done, t)
                act.dma_start(raw[:], adj_t[t]).then_inc(raw_here, 16)
                act.wait_ge(bcast_ready, t + 1)
                act.copy(eminus[:, bass.ds(t * P, P)], psB[0:HEADS, 1, 0:P])
                act.copy(logit[:, :, bass.ds(t * P, P)],
                         psB[:, 0, 0:HEADS * P].rearrange("p (c n) -> p c n", c=HEADS)).then_inc(bcast_done, 1)
            with act.If(has_negatives > 0):
                tiles(act, tile)
                act.wait_ge(bcast_done, NT)
                copy_tail_logits(act, logit)
                for copy in range(1, COPIES):
                    last = act.copy(eminus[:, TAIL + CROWS * copy:TAIL + CROWS * (copy + 1)],
                                    eminus[:, TAIL:TAIL + CROWS])
                last.then_inc(copies_done, 1)
                act.wait_ge(copies_done, 1)
                act.dma_start(eminus_dram, eminus[:]).then_inc(eminus_out, 16)
                act.wait_ge(eminus_out, 16)

        @block.vector
        def _(dve):
            has_negatives = dve.value_load(sh["negtot"][0:1, 0:1])

            def tile(t):
                dve.wait_ge(raw_here, 16 * (t + 1))
                d = raw[:, bass.ds(t * P, P)]
                dve.tensor_tensor(d, d, notid[:, t // (NT - 1)], ALU.mult).then_inc(diag_off, 1)
                dve.wait_ge(diag_off, t + 1)
                dve.tensor_scalar(pos[:], raw[:], 0.0, None, ALU.is_gt)
                dve.tensor_scalar(ngt[:], raw[:], 0.0, None, ALU.is_lt).then_inc(masks_done, 1)
                dve.wait_ge(sums_done, t + 1)
                if not isinstance(t, int):
                    dve.wait_ge(bcast_ready, t)
                dve.tensor_reduce(e0[:], psE[:, 0:3 * NC2].rearrange("p (q c) -> p c q", q=3), AX.X,
                                  ALU.add).then_inc(sum_step, 1)
                dve.wait_ge(sum_step, t + 1)
                dve.scalar_tensor_tensor(e1[:], e0[:], ALPHA, e0[:], ALU.mult, ALU.max).then_inc(e_done, 1)
            with dve.If(has_negatives > 0):
                tiles(dve, tile)

        @block.tensor
        def _(pe):
            has_negatives = pe.value_load(sh["negtot"][0:1, 0:1])

            def tile(t):
                pe.wait_ge(masks_done, t + 1)
                if not isinstance(t, int):
                    pe.wait_ge(e_done, t)
                for j in range(NT):
                    b = slice(j * P, (j + 1) * P)
                    r = slice(0, P if j < NT - 1 else CROWS)
                    pe.matmul(psE[:, 0:3 * NC2], pos[r, b], up[r, j, 0:3 * NC2], start=(j == 0), stop=False)
                    last = pe.matmul(psE[:, 0:3 * NC2], ngt[r, b], um[r, j, 0:3 * NC2], start=False, stop=(j == NT - 1))
                last.then_inc(sums_done, 1)
                pe.wait_ge(e_done, t + 1)
                if not isinstance(t, int):
                    pe.wait_ge(bcast_done, t)
                for c in range(HEADS):
                    pe.matmul(psB[:, 0, c * P:(c + 1) * P],
                              e1[:, c:c + 1].to_broadcast([P, P]), ident[:], start=True, stop=True)
                pe.matmul(psB[0:HEADS, 1, 0:P], e1[:, HEADS:NC2], ident[:], start=True, stop=True).then_inc(bcast_ready, 1)
            with pe.If(has_negatives > 0):
                tiles(pe, tile)


def attention_stage(nc, sh, adj_n, a_here, gat_w_in, es_dram, eminus_dram, gru_w_in, gru_w_here,
                    s_dram, h_dram, chunk0_here):
    ident, notid, h_mov, logit, a_ring = sh["ident"], sh["notid"], sh["h_mov"], sh["logit"], sh["a_ring"]
    LT = 3
    WR = 4
    TR = 3
    SPI = 2 * HEADS
    LE = 3
    EE = 2
    GPI = SPI * NG
    MERGED = HEADS
    STEPS = (NT - 1) * HEADS + 1
    ITERS = NT // 2
    HALF = NP // 2
    assert GPI % WR == 0 and GPI % TR == 0
    with ExitStack() as ctx:
        def sb(name, shape, dt):
            return ctx.enter_context(nc.sbuf_tensor(name, shape, dt))

        def sem(name):
            return ctx.enter_context(nc.semaphore(name))

        w_nat = sb("a_w", [P, SPI, NP], F32)
        mask, diag_off, mask_done = sh["mask"], sh["diag_off"], sh["mask_done"]
        isneg = sb("a_isneg", [P, HALF], U8)
        wt_hi = sb("a_wt_hi", [P, WR, GB * P], F32R)
        wt_lo = sb("a_wt_lo", [P, WR, GB * P], F32R)
        gw = sb("a_gw", [P, HEADS, KD, 2 * D], F32R)
        gw_raw = w_nat[:, SPI - 1, 0:HEADS * KD * D].rearrange("p (h k d) -> p h k d", h=HEADS, k=KD)
        mx = sb("a_mx", [P, SPI, 2], F32)
        carrier = sb("a_carrier", [P, SPI], F32)
        nmx = sb("a_nmx", [P, SPI], F32)
        ssum = sb("a_ssum", [P, SPI, 2], F32)
        s3 = sb("a_s3", [P, SPI], F32)
        rs = sb("a_rs", [P, SPI], F32)
        g_warm = sb("a_g_warm", [P, 1], F32)
        ghalf = sb("a_ghalf", [P, D], F32)
        g = sb("a_g", [P, D], F32)
        es = sb("a_es", [P, D], F32)
        gT_hi = sb("a_gT_hi", [P, D], F32R)
        gT_lo = sb("a_gT_lo", [P, D], F32R)
        esT = sb("a_esT", [P, KD, P], F32)
        psW = ctx.enter_context(nc.psum_tensor("a_psW", [P, TR, 512], F32))
        psO = ctx.enter_context(nc.psum_tensor("a_psO", [P, 2, 512], F32))
        psG = ctx.enter_context(nc.psum_tensor("a_psG", [P, 512], F32))
        psE = ctx.enter_context(nc.psum_tensor("a_psE", [P, D], F32))
        psX = ctx.enter_context(nc.psum_tensor("a_psX", [P, 512], F32))
        gw_here = sem("a_gw_here")
        gw_hi = sem("a_gw_hi")
        gw_lo = sem("a_gw_lo")
        logits_done = sem("a_logits_done")
        nmx_done = sem("a_nmx_done")
        exp_done = sem("a_exp_done")
        w_pool = sem("a_w_pool")
        w_dve = sem("a_w_dve")
        tr_done = sem("a_tr_done")
        hi_done = sem("a_hi_done")
        lo_done = sem("a_lo_done")
        mm_done = sem("a_mm_done")
        rs_step = sem("a_rs_step")
        rs_done = sem("a_rs_done")
        ghalf_done = sem("a_ghalf_done")
        g_done = sem("a_g_done")
        gt_done = sem("a_gt_done")
        gT_hi_done = sem("a_gT_hi_done")
        gT_lo_done = sem("a_gT_lo_done")
        proj_done = sem("a_proj_done")
        ehalf_done = sem("a_ehalf_done")
        es_done = sem("a_es_done")
        est_done = sem("a_est_done")
        esT_done = sem("a_esT_done")
        esT_out = sem("a_esT_out")
        last_out = sem("a_last_out")
        rare_here = sem("a_rare_here")
        block = ctx.enter_context(nc.Block())

        def at_least(eng, s, v):
            if not isinstance(v, int) or v > 0:
                eng.wait_ge(s, v)

        def later(i, k, by):
            return i + (k + by) // SPI, (k + by) % SPI

        def loop(eng, body):
            body(0, False)
            with eng.Fori(1, ITERS - 1) as i:
                body(i, False)
            body(ITERS - 1, True)

        def steps_of(last):
            return MERGED + 1 if last else SPI

        @block.sync
        def _(sp):
            sp.wait_ge(w_pool, 2 * (NT - 1) + 1)
            sp.wait_ge(w_dve, NT - 1)
            for g in range(2):
                sp.dma_start(landing(a_ring, g, 0, KD, 3 * D), gru_w_in[g]).then_inc(gru_w_here[g], 16)
            for m, src in enumerate((s_dram, h_dram)):
                sp.dma_start(landing(a_ring, m, KD * 3 * D, KD, CH), src[:, :, 0:CH]).then_inc(chunk0_here, 16)
            sp.wait_ge(esT_done, NT)
            sp.dma_start(es_dram[:, :, TAIL:NP], esT[:]).then_inc(last_out, 16)
            sp.wait_ge(last_out, 16)
            sp.wait_ge(esT_out, 16 * (NT - 1))

        @block.gpsimd
        def _(pool):
            def weights(i, k):
                if k % HEADS == HEADS - 1:
                    return
                pool.wait_ge(exp_done, SPI * i + k + 1)
                w = w_nat[:, k]
                pool.tensor_tensor(w, w, a_ring[:, k // HEADS], ALU.mult).then_inc(w_pool, 1)

            def store(t):
                pool.wait_ge(esT_done, t + 1)
                pool.dma_start(es_dram[:, :, bass.ds(t * P, P)], esT[:]).then_inc(esT_out, 16)

            def body(i, last):
                for k in range(steps_of(last)):
                    if not (last and k + EE >= MERGED):
                        weights(*later(i, k, EE))
                    if k % HEADS == HEADS - 1 and (k > HEADS or not isinstance(i, int) or i):
                        store(2 * i + k // HEADS - 1)
            pool.wait_ge(gw_hi, 1)
            pool.tensor_tensor(gw[:, :, :, D:2 * D], gw_raw, gw[:, :, :, 0:D].bitcast(F32),
                               ALU.subtract).then_inc(gw_lo, 1)
            pool.wait_ge(w_pool, 1)
            weights(0, 1)
            loop(pool, body)
            store(NT - 2)

        @block.scalar
        def _(act):
            act.dma_start(gw_raw, gat_w_in).then_inc(gw_here, 16)
            has_negatives = act.value_load(sh["negtot"][0:1, 0:1])

            def rare(i, k):
                s = SPI * i + k
                with act.If(has_negatives > 0):
                    at_least(act, rare_here, 16 * s)
                    if isinstance(s, int) and s == SPI - 2:
                        act.wait_ge(gw_lo, 1)
                    at_least(act, tr_done, NG * (s - SPI + 2))
                    act.dma_start(w_nat[:, (k + 1) % SPI],
                                  eminus_dram[k % HEADS:k % HEADS + 1, :].to_broadcast([P, NP])).then_inc(rare_here, 16)

            def exps(i, k, half):
                s = SPI * i + k
                if half == 0:
                    act.wait_ge(nmx_done, s + 1)
                    at_least(act, rs_done, s - SPI + 1)
                w = w_nat[:, k, half * HALF:HALF if half == 0 else TAIL + CROWS]
                ins = act.activation(w, w, ACT.Exp, bias=nmx[:, k:k + 1], accum_out=ssum[:, k, half:half + 1])
                if half:
                    w = w_nat[:, k, TAIL + CROWS:NP]
                    act.activation(w, w, ACT.Exp, bias=nmx[:, k:k + 1]).then_inc(exp_done, 1)

            def hi_group(i, k, gi):
                q = GPI * i + k * NG + gi
                n = GSIZE[gi] * P
                act.wait_ge(tr_done, q + 1)
                at_least(act, mm_done, q - WR + 1)
                act.copy(wt_hi[:, (k * NG + gi) % WR, 0:n],
                         psW[:, (k * NG + gi) % TR, 0:n]).then_inc(hi_done, 1)

            def scaled_half(s, k, i=None):
                act.wait_ge(rs_done, s + 1)
                act.wait_ge(mm_done, NG * (s + 1))
                at_least(act, g_done, s)
                if k % HEADS == 0:
                    at_least(act, es_done, 2 * i + k // HEADS)
                act.mul(ghalf[:], psO[:, k % 2, D:2 * D], rs[:, k:k + 1]).then_inc(ghalf_done, 1)

            def gT_half(s):
                act.wait_ge(gt_done, s + 1)
                at_least(act, proj_done, s)
                act.copy(gT_hi[:], psG[:, 0:D]).then_inc(gT_hi_done, 1)

            def es_half(t, steps=None):
                steps = HEADS * (t + 1) if steps is None else steps
                act.wait_ge(proj_done, steps)
                act.wait_ge(g_done, steps)
                act.copy(ghalf[:], psX[:, D:2 * D]).then_inc(ehalf_done, 1)

            def esT_copy(t):
                act.wait_ge(est_done, t + 1)
                at_least(act, esT_out, 16 * t)
                act.copy(esT[:], psE[:].rearrange("p (k n) -> p k n", k=KD)).then_inc(esT_done, 1)

            def load(t, u):
                act.wait_ge(a_here, 16 * t)
                act.wait_ge(w_pool, 2 * (t - 1))
                act.wait_ge(w_dve, t - 1)
                act.dma_start(a_ring[:, u], adj_n[t]).then_inc(a_here, 16)

            def rare_merged():
                with act.If(has_negatives > 0):
                    act.wait_ge(rare_here, 16 * STEPS)
                    for hd in range(1, HEADS):
                        rows = slice(CROWS * hd, CROWS * (hd + 1))
                        act.dma_start(w_nat[rows, MERGED + 1],
                                      eminus_dram[hd:hd + 1, :].to_broadcast([CROWS, NP])).then_inc(rare_here, 16)

            def body(i, last):
                for k in range(steps_of(last)):
                    s = SPI * i + k
                    before = k > 0 or not isinstance(i, int) or i > 0
                    tile_before = k >= HEADS or not isinstance(i, int) or i > 0
                    ahead = not (last and k + EE >= MERGED)
                    if not last:
                        rare(*later(i, k, LE + 1))
                    elif k == 0:
                        rare_merged()
                    hi_group(i, k, 0)
                    if ahead:
                        exps(*later(i, k, EE), 0)
                    hi_group(i, k, 1)
                    if k % HEADS == 1 and tile_before:
                        es_half(2 * i + k // HEADS - 1)
                    if ahead:
                        exps(*later(i, k, EE), 1)
                    hi_group(i, k, 2)
                    hi_group(i, k, 3)
                    if before:
                        scaled_half(s - 1, (k - 1) % SPI, i)
                    hi_group(i, k, 4)
                    if k % HEADS == 1 and not last:
                        load(2 * i + k // HEADS + 2, k // HEADS)
                    hi_group(i, k, 5)
                    if last and k == 1:
                        exps(i, MERGED, 0)
                        exps(i, MERGED, 1)
                    if before:
                        gT_half(s - 1)
                    if k % HEADS == 1 and tile_before:
                        esT_copy(2 * i + k // HEADS - 1)
            for k in range(LE + 1):
                rare(0, k)
            act.activation(g_warm[:], sh["eps"][:], ACT.Exp)
            for k in range(EE):
                exps(0, k, 0)
                exps(0, k, 1)
                if k == 0:
                    act.wait_ge(gw_here, 16)
                    act.copy(gw[:, :, :, 0:D], gw_raw).then_inc(gw_hi, 1)
            loop(act, body)
            es_half(NT - 2)
            scaled_half(STEPS - 1, MERGED, ITERS - 1)
            gT_half(STEPS - 1)
            esT_copy(NT - 2)
            es_half(NT - 1, STEPS)
            esT_copy(NT - 1)

        @block.vector
        def _(dve):
            has_negatives = dve.value_load(sh["negtot"][0:1, 0:1])

            def diagonal(i, u):
                t = 2 * i + u
                dve.wait_ge(a_here, 16 * (t + 1))
                d = a_ring[:, u, bass.ds(t * P, P)]
                dve.tensor_tensor(d, d, notid[:, t // (NT - 1)], ALU.mult).then_inc(diag_off, 1)

            def masks(i, u):
                t = 2 * i + u
                dve.wait_ge(diag_off, t + 1)
                at_least(dve, logits_done, HEADS * t)
                dve.tensor_scalar(mask[:], a_ring[:, u], 0.0, NEG_INF, ALU.is_equal, ALU.mult).then_inc(mask_done, 1)

            def logits(i, k, half):
                s = SPI * i + k
                c = slice(half * HALF, (half + 1) * HALF)
                if half == 0:
                    dve.wait_ge(mask_done, 2 * i + k // HEADS + 1)
                    at_least(dve, tr_done, NG * (s - SPI + 1))
                    at_least(dve, exp_done, s - SPI + 1)
                    if isinstance(s, int) and s == SPI - 1:
                        dve.wait_ge(gw_lo, 1)
                    dve.memset(carrier[:, k:k + 1], 0.0)
                ins = dve.tensor_tensor_reduce(w_nat[:, k, c], mask[:, c], logit[:, k % HEADS, c], 1.0, -3.0e38,
                                               ALU.add, ALU.max, mx[:, k, half:half + 1])
                if half:
                    ins.then_inc(logits_done, 1)

            def merged_logits(hd, half):
                k = MERGED
                if (hd, half) == (0, 0):
                    dve.wait_ge(mask_done, NT)
                    dve.wait_ge(tr_done, NG * (STEPS - SPI))
                    dve.wait_ge(exp_done, STEPS - SPI)
                rows = slice(CROWS * hd, P if hd == HEADS - 1 else CROWS * (hd + 1))
                c = slice(half * HALF, (half + 1) * HALF)
                ins = dve.tensor_tensor_reduce(w_nat[rows, k, c], mask[rows, c], logit[rows, hd, c], 1.0, -3.0e38,
                                               ALU.add, ALU.max, mx[rows, k, half:half + 1])
                if (hd, half) == (HEADS - 1, 1):
                    ins.then_inc(logits_done, 1)

            def maximum(i, k, loads=None):
                s = SPI * i + k
                with dve.If(has_negatives > 0):
                    dve.wait_ge(rare_here, 16 * (s + 1 if loads is None else loads))
                    for half in range(2):
                        c = slice(half * HALF, (half + 1) * HALF)
                        dve.tensor_scalar(isneg[:], a_ring[:, k // HEADS, c], 0.0, None, ALU.is_lt)
                        dve.drain()
                        dve.copy_predicated(w_nat[:, k, c], isneg[:], w_nat[:, (k + 1) % SPI, c])
                        dve.drain()
                        dve.tensor_reduce(mx[:, k, half:half + 1], w_nat[:, k, c], AX.X, ALU.max)
                    dve.drain()
                dve.wait_ge(logits_done, s + 1)
                dve.tensor_scalar(nmx[:, k:k + 1], mx[:, k, 0:1], mx[:, k, 1:2], -1.0, ALU.max,
                                  ALU.mult).then_inc(nmx_done, 1)

            def weights(i, k, half, done=w_dve):
                if half == 0:
                    dve.wait_ge(exp_done, SPI * i + k + 1)
                c = slice(half * HALF, (half + 1) * HALF)
                w = w_nat[:, k, c]
                ins = dve.tensor_tensor(w, w, a_ring[:, k // HEADS, c], ALU.mult)
                if half:
                    ins.then_inc(done, 1)

            def lo_group(i, k, gi):
                q = GPI * i + k * NG + gi
                n = GSIZE[gi] * P
                slot = (k * NG + gi) % WR
                dve.wait_ge(hi_done, q + 1)
                if gi == NG - 1:
                    c3, b = slice(2 * CROWS, 3 * CROWS), slice(n - P, n)
                    dve.tensor_tensor(wt_hi[c3, slot, b], psW[c3, (k * NG + gi) % TR, b], wt_hi[c3, slot, b].bitcast(F32),
                                      ALU.subtract)
                    n -= P
                dve.tensor_tensor(wt_lo[:, slot, 0:n], psW[:, (k * NG + gi) % TR, 0:n],
                                  wt_hi[:, slot, 0:n].bitcast(F32), ALU.subtract).then_inc(lo_done, 1)

            def scale(i, k):
                s = SPI * i + k
                dve.wait_ge(exp_done, s + 1)
                at_least(dve, g_done, s - SPI + 1)
                dve.tensor_scalar(s3[:, k:k + 1], ssum[:, k, 0:1], ssum[:, k, 1:2], float(HEADS), ALU.add,
                                  ALU.mult).then_inc(rs_step, 1)
                dve.wait_ge(rs_step, s + 1)
                dve.reciprocal(rs[:, k:k + 1], s3[:, k:k + 1]).then_inc(rs_done, 1)

            def gather(s, k):
                dve.wait_ge(ghalf_done, s + 1)
                at_least(dve, gt_done, s)
                dve.scalar_tensor_tensor(g[:], psO[:, k % 2, 0:D], rs[:, k:k + 1], ghalf[:],
                                         ALU.mult, ALU.add).then_inc(g_done, 1)

            def gT_half(s):
                dve.wait_ge(gT_hi_done, s + 1)
                dve.tensor_tensor(gT_lo[:], psG[:, 0:D], gT_hi[:].bitcast(F32), ALU.subtract).then_inc(gT_lo_done, 1)

            def es_sum(t):
                dve.wait_ge(ehalf_done, t + 1)
                at_least(dve, est_done, t)
                dve.tensor_tensor(es[:], psX[:, 0:D], ghalf[:], ALU.add).then_inc(es_done, 1)

            def body(i, last):
                for k in range(steps_of(last)):
                    s = SPI * i + k
                    before = k > 0 or not isinstance(i, int) or i > 0
                    tile_before = k >= HEADS or not isinstance(i, int) or i > 0
                    more_logits = not last
                    dve_weights = k % HEADS == 0 and not (last and k == MERGED)
                    lo_group(i, k, 0)
                    if more_logits:
                        logits(*later(i, k, LE), 0)
                    elif k == 1:
                        merged_logits(1, 0)
                    elif k == 2:
                        weights(i, MERGED, 0, w_pool)
                    lo_group(i, k, 1)
                    if k % HEADS == 1 and tile_before:
                        es_sum(2 * i + k // HEADS - 1)
                    if more_logits:
                        logits(*later(i, k, LE), 1)
                        maximum(*later(i, k, LE))
                    elif k == 0:
                        merged_logits(0, 0)
                    elif k == 1:
                        merged_logits(1, 1)
                    elif k == 2:
                        weights(i, MERGED, 1, w_pool)
                    lo_group(i, k, 2)
                    if last and k == 0:
                        merged_logits(0, 1)
                    if last and k == 1:
                        merged_logits(2, 0)
                    lo_group(i, k, 3)
                    if before:
                        gather(s - 1, (k - 1) % SPI)
                    scale(i, k)
                    if dve_weights:
                        weights(*later(i, k, EE), 0)
                    elif k % HEADS == HEADS - 1 and not last:
                        diagonal(i + 1, k // HEADS)
                    lo_group(i, k, 4)
                    if dve_weights:
                        weights(*later(i, k, EE), 1)
                    elif k % HEADS == HEADS - 1 and not last:
                        masks(i + 1, k // HEADS)
                    elif last and k == 1:
                        merged_logits(2, 1)
                        maximum(i, MERGED, STEPS + HEADS - 1)
                    lo_group(i, k, 5)
                    if before:
                        gT_half(s - 1)
            for k in range(LE):
                logits(0, k, 0)
                if k == 1:
                    dve.wait_ge(exp_done, 1)
                    dve.tensor_tensor(w_nat[:, 0], w_nat[:, 0], a_ring[:, 0], ALU.mult).then_inc(w_pool, 1)
                logits(0, k, 1)
                maximum(0, k)
            diagonal(0, 1)
            masks(0, 1)
            loop(dve, body)
            es_sum(NT - 2)
            gather(STEPS - 1, MERGED)
            gT_half(STEPS - 1)
            es_sum(NT - 1)

        @block.tensor
        def _(pe):
            def transposes(i, k, gi):
                if gi == 0:
                    t = 2 * i + k // HEADS
                    if k % HEADS == HEADS - 1:
                        pe.wait_ge(w_dve, t + 1)
                    else:
                        pe.wait_ge(w_pool, 2 * t + k % HEADS + 1)
                bank = (k * NG + gi) % TR
                for b in range(GSIZE[gi]):
                    j = gi * GB + b
                    last = pe.transpose(psW[:, bank, b * P:(b + 1) * P], w_nat[:, k, j * P:(j + 1) * P], ident[:])
                last.then_inc(tr_done, 1)

            def products(i, k, gi):
                slot = (k * NG + gi) % WR
                pe.wait_ge(lo_done, GPI * i + k * NG + gi + 1)
                if gi == 0:
                    at_least(pe, g_done, SPI * i + k - 1)
                for b in range(GSIZE[gi]):
                    j = gi * GB + b
                    c = slice(b * P, (b + 1) * P)
                    if j == NT - 1:
                        last = pe.matmul(psO[:, k % 2, 0:D], wt_hi[:, slot, c], h_mov[:, j, 0:D], start=False, stop=True)
                        continue
                    pe.matmul(psO[:, k % 2, :], wt_hi[:, slot, c], h_mov[:, j, :], start=(j == 0), stop=False)
                    last = pe.matmul(psO[:, k % 2, 0:D], wt_lo[:, slot, c], h_mov[:, j, 0:D], start=False, stop=False)
                last.then_inc(mm_done, 1)

            def g_transposes(s):
                pe.wait_ge(g_done, s + 1)
                at_least(pe, gT_lo_done, s)
                for c in range(KD):
                    last = pe.transpose(psG[:, c * P:(c + 1) * P], g[:, c * P:(c + 1) * P], ident[:])
                last.then_inc(gt_done, 1)

            def project_merged():
                pe.wait_ge(gT_lo_done, STEPS)
                pe.wait_ge(es_done, NT - 1)
                for hd in range(HEADS):
                    for c in range(KD):
                        cols = slice(c * P + CROWS * hd, c * P + CROWS * (hd + 1))
                        pe.matmul(psX[0:CROWS], gT_hi[:, cols], gw[:, hd, c, :],
                                  start=(hd == 0 and c == 0), stop=False)
                        last = pe.matmul(psX[0:CROWS, 0:D], gT_lo[:, cols], gw[:, hd, c, 0:D],
                                         start=False, stop=(hd == HEADS - 1 and c == KD - 1))
                last.then_inc(proj_done, 1)

            def project(s, k, i=None):
                hd = k % HEADS
                pe.wait_ge(gT_lo_done, s + 1)
                if isinstance(s, int) and s == 0:
                    pe.wait_ge(gw_lo, 1)
                if hd == 0:
                    at_least(pe, es_done, 2 * i + k // HEADS)
                for c in range(KD):
                    pe.matmul(psX[:], gT_hi[:, c * P:(c + 1) * P], gw[:, hd, c, :],
                              start=(hd == 0 and c == 0), stop=False)
                    last = pe.matmul(psX[:, 0:D], gT_lo[:, c * P:(c + 1) * P], gw[:, hd, c, 0:D],
                                     start=False, stop=(hd == HEADS - 1 and c == KD - 1))
                last.then_inc(proj_done, 1)

            def es_transposes(t):
                pe.wait_ge(es_done, t + 1)
                at_least(pe, esT_done, t)
                for c in range(KD):
                    last = pe.transpose(psE[:, c * P:(c + 1) * P], es[:, c * P:(c + 1) * P], ident[:])
                last.then_inc(est_done, 1)

            def body(i, last):
                for k in range(steps_of(last)):
                    s = SPI * i + k
                    before = k > 0 or not isinstance(i, int) or i > 0
                    tile_before = k >= HEADS or not isinstance(i, int) or i > 0
                    for gi in range(NG):
                        products(i, k, gi)
                        ahead = k * NG + gi + LT
                        if not (last and ahead >= NG * (MERGED + 1)):
                            transposes(i + ahead // GPI, ahead % GPI // NG, ahead % NG)
                        if gi == 1 and k % HEADS == 1 and tile_before:
                            es_transposes(2 * i + k // HEADS - 1)
                        if gi == 2 and before:
                            g_transposes(s - 1)
                        if gi == 4 and before:
                            project(s - 1, (k - 1) % SPI, i)
            for gi in range(LT):
                transposes(0, 0, gi)
            loop(pe, body)
            es_transposes(NT - 2)
            g_transposes(STEPS - 1)
            project_merged()
            es_transposes(NT - 1)


def landing(a_ring, u, start, k, m):
    return a_ring[:, u, start:start + k * m].rearrange("p (k m) -> p k m", k=k)


def gru_stage(nc, ident, a_ring, x1, stats, x_in, diag_in, gru_w_in, w_here, chunk0_here, gru_b_in,
              s_dram, es_dram, h_dram):
    WIDTHS = [CH] * (NCH - 1) + [GSIZE[LAST] * P]
    UNITS = 4
    with ExitStack() as ctx:
        def sb(name, shape, dt):
            return ctx.enter_context(nc.sbuf_tensor(name, shape, dt))

        def sem(name):
            return ctx.enter_context(nc.semaphore(name))

        x = sb("r_x", [P, NT, D], F32)
        diag = sb("r_diag", [P, NT], F32)
        w_raw = [landing(a_ring, g, 0, KD, 3 * D) for g in range(2)]
        w_hi = sb("r_w_hi", [P, 4, KD, 3 * D], F32R)
        w_lo = sb("r_w_lo", [P, 4, KD, 3 * D], F32R)
        b = sb("r_b", [P, 4, 3 * KD], F32)
        brz = sb("r_brz", [P, 2, 2 * KD], F32)
        raw = sb("r_raw", [P, 2, 3, KD, CH], F32)
        v_hi = sb("r_hi", [P, 2, 3, KD, CH], F32R)
        v_lo = sb("r_lo", [P, 2, 3, KD, CH], F32R)
        r = sb("r_r", [P, 2, CH], F32)
        z = sb("r_z", [P, 2, CH], F32)
        raw0 = [landing(a_ring, m, KD * 3 * D, KD, CH) for m in range(2)]
        t1 = sb("r_t1", [P, CH], F32)
        t2 = sb("r_t2", [P, CH], F32)
        n = sb("r_n", [P, CH], F32)
        t3, t4 = t2, t1
        total = sb("r_total", [P, KD, CH], F32)
        psR = ctx.enter_context(nc.psum_tensor("r_psR", [P, 2, 512], F32))
        psZ = ctx.enter_context(nc.psum_tensor("r_psZ", [P, 2, 512], F32))
        psH = ctx.enter_context(nc.psum_tensor("r_psH", [P, 512], F32))
        psN = ctx.enter_context(nc.psum_tensor("r_psN", [P, 512], F32))
        psX = ctx.enter_context(nc.psum_tensor("r_psX", [P, 2, 512], F32))
        consts_here = sem("r_consts_here")
        x_here = sem("r_x_here")
        w_hi_done = sem("r_w_hi_done")
        w_lo_done = sem("r_w_lo_done")
        brz_done = sem("r_brz_done")
        raw_here = sem("r_raw_here")
        att_here = sem("r_att_here")
        v_hi_done = sem("r_v_hi_done")
        v_lo_done = sem("r_v_lo_done")
        r_ready = sem("r_r_ready")
        z_ready = sem("r_z_ready")
        h_ready = sem("r_h_ready")
        n_ready = sem("r_n_ready")
        r_done = sem("r_r_done")
        z_done = sem("r_z_done")
        t_step = sem("r_t_step")
        t2_done = sem("r_t2_done")
        n_done = sem("r_n_done")
        mix_step = sem("r_mix_step")
        mix_done = sem("r_mix_done")
        tr_done = sem("r_tr_done")
        x1_done = sem("r_x1_done")
        st_done = sem("r_st_done")
        block = ctx.enter_context(nc.Block())

        def positive(eng, s, v):
            if not isinstance(v, int) or v > 0:
                eng.wait_ge(s, v)

        def source(c, m, w):
            if isinstance(c, int) and c == 0 and m < 2:
                return raw0[m]
            return raw[:, c % 2, m, :, 0:w]

        def chunks(eng, body):
            body(0, WIDTHS[0])
            with eng.Fori(1, LAST) as c:
                body(c, CH)
            body(LAST, WIDTHS[LAST])

        @block.sync
        def _(sp):
            sp.dma_start(b[:], gru_b_in).then_inc(consts_here, 16)
            sp.dma_start(diag[:], diag_in).then_inc(consts_here, 16)
            sp.dma_start(raw[:, 0, 2], es_dram[:, :, 0:CH]).then_inc(att_here, 16)
            for g in range(2, 4):
                sp.wait_ge(w_lo_done, g - 1)
                sp.dma_start(w_raw[g % 2], gru_w_in[g]).then_inc(w_here[g], 16)
            sp.wait_ge(w_here[3], 16)
            sp.dma_start(x[:], x_in.rearrange("t p d -> p t d")).then_inc(x_here, 16)

        @block.scalar
        def _(act):
            def load(c, w):
                positive(act, raw_here, 32 * (c - 1))
                positive(act, att_here, 16 * c)
                positive(act, mix_done, UNITS * (c - 1))
                for m, (src, here) in enumerate(((s_dram, raw_here), (h_dram, raw_here), (es_dram, att_here))):
                    act.dma_start(raw[:, c % 2, m, :, 0:w], src[:, :, bass.ds(c * CH, w)]).then_inc(here, 16)

            def split(c, w, sources=range(3)):
                positive(act, n_ready, UNITS * (c - 1))
                for m in sources:
                    chunk0 = isinstance(c, int) and c == 0
                    if m == 0:
                        if chunk0:
                            act.wait_ge(chunk0_here, 32)
                        else:
                            act.wait_ge(raw_here, 32 * c)
                    if m == 2:
                        act.wait_ge(att_here, 16 * (c + 1))
                    act.copy(v_hi[:, c % 2, m, :, 0:w], source(c, m, w)).then_inc(v_hi_done, 1)

            def unit(c, u, w):
                g, f = u // KD, u % KD
                k = UNITS * c + u
                act.wait_ge(r_ready, k + 1)
                positive(act, mix_done, k - 1)
                act.activation(r[:, u % 2, 0:w], psR[:, u % 2, 0:w], ACT.Sigmoid,
                               bias=brz[:, g, f:f + 1]).then_inc(r_done, 1)
                act.wait_ge(z_ready, k + 1)
                act.activation(z[:, u % 2, 0:w], psZ[:, u % 2, 0:w], ACT.Sigmoid,
                               bias=brz[:, g, KD + f:KD + f + 1]).then_inc(z_done, 1)
                act.wait_ge(t2_done, k + 1)
                positive(act, mix_done, k)
                act.activation(n[:, 0:w], t2[:, 0:w], ACT.Tanh,
                               bias=b[:, 2 * g, 2 * KD + f:2 * KD + f + 1]).then_inc(n_done, 1)

            def split_weights(g):
                act.wait_ge(w_here[g], 16)
                act.copy(w_hi[:, g], w_raw[g % 2]).then_inc(w_hi_done, 1)
            split_weights(0)
            split_weights(1)
            split(0, WIDTHS[0], (0, 1))
            act.wait_ge(brz_done, 1)

            def body(c, w):
                first = isinstance(c, int) and c == 0
                last = isinstance(c, int) and c == LAST
                for u in range(UNITS):
                    unit(c, u, w)
                    if u == 0 and first:
                        split_weights(2)
                        split_weights(3)
                        split(0, WIDTHS[0], (2,))
                        load(1, WIDTHS[1])
                    if u == 1 and not last:
                        split_next(c)
                if not last:
                    load_after(c)

            def split_next(c):
                if isinstance(c, int):
                    split(c + 1, WIDTHS[c + 1])
                else:
                    split(c + 1, CH)

            def load_after(c):
                if isinstance(c, int):
                    load(c + 2, WIDTHS[c + 2])
                else:
                    load(c + 2, CH)
            body(0, WIDTHS[0])
            with act.Fori(1, LAST - 2) as c:
                body(c, CH)
            for c in (LAST - 2, LAST - 1, LAST):
                for u in range(UNITS):
                    unit(c, u, WIDTHS[c])
                    if u == 1 and c < LAST:
                        split(c + 1, WIDTHS[c + 1])
                if c + 2 <= LAST:
                    load(c + 2, WIDTHS[c + 2])

        @block.vector
        def _(dve):

            def split_weights(g):
                dve.wait_ge(w_hi_done, g + 1)
                dve.tensor_tensor(w_lo[:, g], w_raw[g % 2], w_hi[:, g].bitcast(F32),
                                  ALU.subtract).then_inc(w_lo_done, 1)

            def split(c, w, sources=range(3)):
                for m in sources:
                    dve.wait_ge(v_hi_done, 3 * c + m + 1)
                    dve.tensor_tensor(v_lo[:, c % 2, m, :, 0:w], source(c, m, w),
                                      v_hi[:, c % 2, m, :, 0:w].bitcast(F32), ALU.subtract).then_inc(v_lo_done, 1)

            def unit(c, u, w):
                g, f = u // KD, u % KD
                k = UNITS * c + u
                dve.wait_ge(r_done, k + 1)
                dve.wait_ge(h_ready, k + 1)
                positive(dve, mix_done, k)
                dve.scalar_tensor_tensor(t1[:, 0:w], psH[:, 0:w], b[:, 2 * g + 1, 2 * KD + f:2 * KD + f + 1],
                                         r[:, u % 2, 0:w], ALU.add, ALU.mult).then_inc(t_step, 1)
                dve.wait_ge(t_step, k + 1)
                dve.wait_ge(n_ready, k + 1)
                dve.tensor_tensor(t2[:, 0:w], psN[:, 0:w], t1[:, 0:w], ALU.add).then_inc(t2_done, 1)
                dve.wait_ge(n_done, k + 1)
                dve.wait_ge(z_done, k + 1)
                hraw = source(c, 1, w)[:, f]
                dve.tensor_tensor(t3[:, 0:w], hraw, n[:, 0:w], ALU.subtract).then_inc(mix_step, 1)
                dve.wait_ge(mix_step, 3 * k + 1)
                dve.tensor_tensor(t4[:, 0:w], t3[:, 0:w], z[:, u % 2, 0:w], ALU.mult).then_inc(mix_step, 1)
                dve.wait_ge(mix_step, 3 * k + 2)
                if g == 0:
                    dve.tensor_tensor(total[:, f, 0:w], n[:, 0:w], t4[:, 0:w], ALU.add).then_inc(mix_step, 1)
                    dve.wait_ge(mix_step, 3 * k + 3)
                    dve.nop().then_inc(mix_done, 1)
                else:
                    dve.tensor_tensor(t3[:, 0:w], n[:, 0:w], t4[:, 0:w], ALU.add).then_inc(mix_step, 1)
                    dve.wait_ge(mix_step, 3 * k + 3)
                    dve.tensor_tensor(total[:, f, 0:w], total[:, f, 0:w], t3[:, 0:w], ALU.add).then_inc(mix_done, 1)

            def finish(c, tiles):
                for q in range(tiles):
                    t = GB * c + q
                    if q % 2 == 0:
                        dve.wait_ge(tr_done, t + 2)
                    dve.scalar_tensor_tensor(x1[:, t], psX[:, q // 2, (q % 2) * D:(q % 2 + 1) * D], diag[:, bass.ds(t, 1)], x[:, t],
                                             ALU.mult, ALU.add).then_inc(x1_done, 1)
                    dve.wait_ge(x1_done, t + 1)
                    dve.bn_stats(stats[:, t], x1[:, t]).then_inc(st_done, 1)

            split_weights(0)
            split_weights(1)
            split(0, WIDTHS[0], (0, 1))
            dve.wait_ge(consts_here, 32)
            for g in range(2):
                last = dve.tensor_tensor(brz[:, g], b[:, 2 * g, 0:2 * KD], b[:, 2 * g + 1, 0:2 * KD], ALU.add)
            last.then_inc(brz_done, 1)

            def body(c, w, nxt):
                first = isinstance(c, int) and c == 0
                if not first:
                    finish(c - 1, GB)
                for u in range(UNITS):
                    unit(c, u, w)
                    if u == 0 and first:
                        split_weights(2)
                        split_weights(3)
                        split(0, WIDTHS[0], (2,))
                    if u == 1 and nxt:
                        split(c + 1, nxt)
            body(0, WIDTHS[0], WIDTHS[1])
            dve.wait_ge(x_here, 16)
            with dve.Fori(1, LAST - 1) as c:
                body(c, CH, CH)
            body(LAST - 1, WIDTHS[LAST - 1], WIDTHS[LAST])
            body(LAST, WIDTHS[LAST], 0)
            finish(LAST, GSIZE[LAST])

        @block.tensor
        def _(pe):
            def gate(ps, col, sources, c, w):
                terms = [(g, m, k, a, v) for g, m in sources for k in range(KD)
                         for a, v in ((w_hi, v_hi), (w_hi, v_lo), (w_lo, v_hi))]
                for j, (g, m, k, a, v) in enumerate(terms):
                    last = pe.matmul(ps[:, 0:w], a[:, g, k, col:col + P], v[:, c % 2, m, k, 0:w],
                                     start=(j == 0), stop=(j == len(terms) - 1))
                return last

            def unit(c, u, w):
                g, f = u // KD, u % KD
                k = UNITS * c + u
                ih, hh = (2 * g, 2 * g), (2 * g + 1, 1)
                positive(pe, r_done, k - 1)
                gate(psR[:, u % 2], f * P, (ih, hh), c, w).then_inc(r_ready, 1)
                positive(pe, z_done, k - 1)
                gate(psZ[:, u % 2], D + f * P, (ih, hh), c, w).then_inc(z_ready, 1)
                positive(pe, t_step, k)
                gate(psH, 2 * D + f * P, (hh,), c, w).then_inc(h_ready, 1)
                positive(pe, t2_done, k)
                gate(psN, 2 * D + f * P, (ih,), c, w).then_inc(n_ready, 1)

            def natural(c, tiles):
                pe.wait_ge(mix_done, UNITS * (c + 1))
                for q in range(tiles):
                    for f in range(KD):
                        last = pe.transpose(psX[:, q // 2, (KD * (q % 2) + f) * P:(KD * (q % 2) + f + 1) * P],
                                            total[:, f, q * P:(q + 1) * P], ident[:])
                    last.then_inc(tr_done, 1)

            def body(c, w):
                first = isinstance(c, int) and c == 0
                if first:
                    pe.wait_ge(w_lo_done, 2)
                pe.wait_ge(v_lo_done, 3 * c + 2)
                unit(c, 0, w)
                if not first:
                    natural(c - 1, GB)
                unit(c, 1, w)
                if first:
                    pe.wait_ge(w_lo_done, 4)
                pe.wait_ge(v_lo_done, 3 * (c + 1))
                for u in range(KD, UNITS):
                    unit(c, u, w)
            chunks(pe, body)
            natural(LAST, GSIZE[LAST])


def ffn_stage(nc, ident, eps, a_ring, x1, stats, wr_in, br_in, w1_in, b1_in, w2_in, b2_in,
              gamma_in, beta_in, out):
    WIDTHS = [CH] * (NCH - 1) + [GSIZE[LAST] * P]
    ROWS_LAST = N - (NT - 1) * P
    EF = TOP_K * FT
    BANK = [e % 3 for e in range(EF)]
    AFTER = {0: (3,), 1: (4,), 2: (5,), 3: (6,), 4: (7,)}
    AFTER_NEXT = {5: (0,), 7: (1, 2)}
    with ExitStack() as ctx:
        def sb(name, shape, dt):
            return ctx.enter_context(nc.sbuf_tensor(name, shape, dt))

        def sem(name):
            return ctx.enter_context(nc.semaphore(name))

        mean = sb("f_mean", [P, NT], F32)
        var = sb("f_var", [P, NT], F32)
        tmp = sb("f_tmp", [P, NT], F32)
        rstd = sb("f_rstd", [P, NT], F32)
        xn = sb("f_xn", [P, NT, D], F32)
        xT_hi = sb("f_xT_hi", [P, KD, NP], F32R)
        xT_lo = sb("f_xT_lo", [P, KD, NP], F32R)
        ones = sb("f_ones", [P, P], F32)
        total = sb("f_total", [1, D], F32)
        mT = sb("f_mT", [P, KD], F32)
        warm = sb("f_warm", [P, 3], F32)
        wr = sb("f_wr", [P, KD, E], F32)
        br = sb("f_br", [1, E], F32)
        row = sb("f_row", [1, 16, E], F32)
        col = sb("f_col", [1, 16], F32)
        idx = sb("f_idx", [1, E], U32)
        wb = sb("f_wb", [P, TOP_K], F32)
        w1r = [landing(a_ring, k, 0, KD, F) for k in range(TOP_K)]
        w1_hi = sb("f_w1_hi", [P, TOP_K, KD, F], F32R)
        w1_lo = sb("f_w1_lo", [P, TOP_K, KD, F], F32R)
        w2r = [landing(a_ring, k, KD * F, FT, D) for k in range(TOP_K)]
        w2 = sb("f_w2", [P, EF, 2 * D], F32R)
        b1 = sb("f_b1", [P, TOP_K, FT], F32)
        b2 = sb("f_b2", [P, TOP_K, D], F32)
        b2s = sb("f_b2s", [P, D], F32)
        gamma = sb("f_gamma", [P, D], F32)
        beta = sb("f_beta", [P, D], F32)
        hid = sb("f_hid", [P, 2, CH], F32)
        hid_hi = sb("f_hid_hi", [P, EF, CH], F32R)
        hid_lo = sb("f_hid_lo", [P, EF, CH], F32R)
        y = sb("f_y", [P, GB, D], F32)
        y_low = sb("f_y_low", [P, GB, D], F32)
        o = sb("f_o", [P, GB, D], F32)
        st = sb("f_st", [P, GB, 6], F32)
        mean3 = sb("f_mean3", [P, GB], F32)
        var3 = sb("f_var3", [P, GB], F32)
        tmp3 = sb("f_tmp3", [P, GB], F32)
        std3 = sb("f_std3", [P, GB], F32)
        rstd3 = sb("f_rstd3", [P, GB], F32)
        psT = ctx.enter_context(nc.psum_tensor("f_psT", [P, 3, 512], F32))
        psO = ctx.enter_context(nc.psum_tensor("f_psO", [P, GB, 512], F32))
        psM = ctx.enter_context(nc.psum_tensor("f_psM", [P, 512], F32))
        consts_here = sem("f_consts_here")
        dve_step = sem("f_dve_step")
        ones_set = sem("f_ones_set")
        var_done = sem("f_var_done")
        std_done = sem("f_std_done")
        xn_done = sem("f_xn_done")
        sum_ready = sem("f_sum_ready")
        sum_done = sem("f_sum_done")
        mean_ready = sem("f_mean_ready")
        mT_done = sem("f_mT_done")
        logits_ready = sem("f_logits_ready")
        ex_need = sem("f_ex_need")
        ex_done = sem("f_ex_done")
        idx_done = sem("f_idx_done")
        top_done = sem("f_top_done")
        wb_ready = sem("f_wb_ready")
        wb_done = sem("f_wb_done")
        xt_done = sem("f_xt_done")
        x_hi_done = sem("f_x_hi_done")
        x_lo_done = sem("f_x_lo_done")
        w1_here = [sem(f"f_w1_here{k}") for k in range(TOP_K)]
        w2_here = [sem(f"f_w2_here{k}") for k in range(TOP_K)]
        b1_here = sem("f_b1_here")
        b2_here = sem("f_b2_here")
        w1_hi_done = sem("f_w1_hi_done")
        w1_lo_done = sem("f_w1_lo_done")
        w2_scaled = sem("f_w2_scaled")
        w2_hi_done = sem("f_w2_hi_done")
        w2_lo_done = sem("f_w2_lo_done")
        xb_done = sem("f_xb_done")
        x1b_done = sem("f_x1b_done")
        hid_ready = sem("f_hid_ready")
        gelu_done = sem("f_gelu_done")
        h_hi_done = sem("f_h_hi_done")
        h_lo_done = sem("f_h_lo_done")
        out_ready = sem("f_out_ready")
        y_high_done = sem("f_y_high_done")
        y_low_done = sem("f_y_low_done")
        y_done = sem("f_y_done")
        v3_step = sem("f_v3_step")
        v3_done = sem("f_v3_done")
        s3_done = sem("f_s3_done")
        o_done = sem("f_o_done")
        og_done = sem("f_og_done")
        oo_done = sem("f_oo_done")
        stored = sem("f_stored")
        last_stored = sem("f_last_stored")
        block = ctx.enter_context(nc.Block())

        def positive(eng, s, v):
            if not isinstance(v, int) or v > 0:
                eng.wait_ge(s, v)

        @block.sync
        def _(sp):
            for dst, src in ((wr, wr_in), (br, br_in), (gamma, gamma_in), (beta, beta_in)):
                sp.dma_start(dst[:], src).then_inc(consts_here, 16)
            sp.wait_ge(idx_done, 1)
            chosen = [sp.value_load(idx[0:1, k:k + 1], min_val=0, max_val=E - 1) for k in range(TOP_K)]
            for k, e in enumerate(chosen):
                sp.dma_start(b1[:, k], b1_in[e]).then_inc(b1_here, 16)
                sp.dma_start(w1r[k], w1_in[e]).then_inc(w1_here[k], 16)
                sp.dma_start(w2r[k], w2_in[e]).then_inc(w2_here[k], 16)
            for k, e in enumerate(chosen):
                sp.dma_start(b2[:, k], b2_in[e]).then_inc(b2_here, 16)
            sp.wait_ge(oo_done, NCH)
            sp.dma_start(out[GB * LAST:NT].rearrange("t p d -> p t d"), o[:, 0:GSIZE[LAST]]).then_inc(last_stored, 16)
            sp.wait_ge(last_stored, 16)
            sp.wait_ge(stored, 16 * LAST)

        @block.gpsimd
        def _(pool):
            pool.memset(ones[:], 1.0).then_inc(ones_set, 1)
            pool.wait_ge(consts_here, 64)
            pool.wait_ge(xn_done, NT)
            pool.tensor_tensor(x1[:], x1[:], beta[:].rearrange("p (o d) -> p o d", o=1).to_broadcast([P, NT, D]),
                               ALU.add).then_inc(x1b_done, 1)
            pool.wait_ge(x1b_done, 1)

            def finish(c, tiles):
                pool.wait_ge(o_done, GB * c + tiles)
                g = gamma[:].rearrange("p (o d) -> p o d", o=1).to_broadcast([P, tiles, D])
                pool.tensor_tensor(o[:, 0:tiles], o[:, 0:tiles], g, ALU.mult).then_inc(og_done, 1)
                pool.wait_ge(og_done, c + 1)
                pool.tensor_tensor(o[:, 0:tiles], o[:, 0:tiles], x1[:, bass.ds(GB * c, tiles)],
                                   ALU.add).then_inc(oo_done, 1)
                pool.wait_ge(oo_done, c + 1)
                pool.dma_start(out[bass.ds(GB * c, tiles)].rearrange("t p d -> p t d"),
                               o[:, 0:tiles]).then_inc(stored, 16)
            with pool.Fori(0, LAST) as c:
                finish(c, GB)

        @block.scalar
        def _(act):
            act.activation(warm[:, 0:1], eps[:], ACT.Sqrt)
            act.wait_ge(var_done, 1)
            act.activation(tmp[:], var[:], ACT.Sqrt, bias=eps[:, 0:1]).then_inc(std_done, 1)
            act.activation(warm[:, 1:2], eps[:], ACT.Exp)
            act.wait_ge(sum_ready, 1)
            act.copy(total[:], psM[0:1, D:2 * D]).then_inc(sum_done, 1)
            act.wait_ge(mean_ready, 1)
            act.mul(mT[:], psM[:, 0:KD], 1.0 / N).then_inc(mT_done, 1)
            for j, (a, n) in enumerate(((1, E), (5, E), (9, TOP_K))):
                act.wait_ge(ex_need, j + 1)
                act.activation(row[:, a, 0:n], row[:, a - 1, 0:n], ACT.Exp, bias=col[:, 2 * j:2 * j + 1],
                               accum_out=col[:, 2 * j + 1:2 * j + 2]).then_inc(ex_done, 1)
            act.wait_ge(wb_ready, 1)
            act.copy(wb[:], psM[:, 32:32 + TOP_K]).then_inc(wb_done, 1)
            for g in range(NG):
                for k in range(KD):
                    j = KD * g + k
                    n = GSIZE[g] * P
                    act.wait_ge(xt_done, j + 1)
                    act.copy(xT_hi[:, k, g * CH:g * CH + n], psT[:, j % 3, 0:n]).then_inc(x_hi_done, 1)

            def weights(k):
                act.wait_ge(w1_here[k], 16)
                act.copy(w1_hi[:, k], w1r[k]).then_inc(w1_hi_done, 1)
                act.wait_ge(w2_scaled, k + 1)
                act.copy(w2[:, k * FT:(k + 1) * FT, 0:D], w2r[k]).then_inc(w2_hi_done, 1)
            act.activation(warm[:, 2:3], eps[:], ACT.Gelu)
            weights(0)
            act.wait_ge(b1_here, 16 * TOP_K)

            def low_half(c, w):
                act.wait_ge(out_ready, EF * (c + 1))
                positive(act, y_high_done, c)
                act.copy(y_low[:, 0:w // P], psO[:, 0:w // P, D:2 * D]).then_inc(y_low_done, 1)

            def deviation(c, w):
                act.wait_ge(v3_done, c + 1)
                act.activation(std3[:, 0:w // P], var3[:, 0:w // P], ACT.Sqrt, bias=eps[:, 0:1]).then_inc(s3_done, 1)

            def chunk(c, w):
                for e in range(EF):
                    j = EF * c + e
                    act.wait_ge(hid_ready, j + 1)
                    positive(act, h_lo_done, j - 1)
                    act.activation(hid[:, e % 2, 0:w], psT[:, BANK[e], 0:w], ACT.Gelu,
                                   bias=b1[:, e // FT, e % FT:e % FT + 1]).then_inc(gelu_done, 1)
                    act.wait_ge(gelu_done, j + 1)
                    positive(act, out_ready, EF * (c - 1) + e + 1)
                    act.copy(hid_hi[:, e, 0:w], hid[:, e % 2, 0:w]).then_inc(h_hi_done, 1)
                    if e == 1 and isinstance(c, int) and c == 0:
                        weights(1)
                    if e == 0 and not (isinstance(c, int) and c == 0):
                        low_half(c - 1, CH)
                    if e == 4 and not (isinstance(c, int) and c == 0):
                        deviation(c - 1, CH)
            chunk(0, WIDTHS[0])
            with act.Fori(1, LAST) as c:
                chunk(c, CH)
            chunk(LAST, WIDTHS[LAST])
            low_half(LAST, WIDTHS[LAST])
            deviation(LAST, WIDTHS[LAST])

        @block.vector
        def _(dve):
            chain = Chain(dve, dve_step)
            moments(dve, chain, stats, mean[:], var[:], tmp[:])
            dve.nop().then_inc(var_done, 1)
            dve.wait_ge(std_done, 1)
            chain(dve.reciprocal(rstd[:], tmp[:]))
            with dve.Fori(0, 2) as half:
                for q in range(NT // 2):
                    t = half * (NT // 2) + q
                    dve.tensor_scalar(xn[:, t], x1[:, t], mean[:, bass.ds(t, 1)], rstd[:, bass.ds(t, 1)],
                                      ALU.subtract, ALU.mult).then_inc(xn_done, 1)
            dve.wait_ge(consts_here, 64)
            dve.wait_ge(logits_ready, 1)
            lg, e1, rw, sc, e2 = (row[:, a] for a in (0, 1, 2, 3, 5))
            chain(dve.tensor_tensor(lg, psM[0:1, 16:16 + E], br[:], ALU.add))
            chain(dve.tensor_reduce(col[:, 0:1], lg, AX.X, ALU.max))
            dve.tensor_scalar(col[:, 0:1], col[:, 0:1], -1.0, None, ALU.mult).then_inc(ex_need, 1)
            dve.wait_ge(ex_done, 1)
            chain(dve.reciprocal(col[:, 6:7], col[:, 1:2]))
            chain(dve.tensor_scalar(rw, e1, col[:, 6:7], None, ALU.mult))
            chain(dve.tensor_scalar(sc, rw, float(N), 1e-30, ALU.mult, ALU.max))
            chain(dve.reciprocal(row[:, 6], sc))
            chain(dve.tensor_scalar(row[:, 6], row[:, 6], CAPACITY, 1.0, ALU.mult, ALU.min))
            chain(dve.tensor_tensor(row[:, 4], rw, row[:, 6], ALU.mult))
            chain(dve.tensor_reduce(col[:, 2:3], row[:, 4], AX.X, ALU.max))
            dve.tensor_scalar(col[:, 2:3], col[:, 2:3], -1.0, None, ALU.mult).then_inc(ex_need, 1)
            dve.wait_ge(ex_done, 2)
            chain(dve.reciprocal(col[:, 7:8], col[:, 3:4]))
            chain(dve.tensor_scalar(row[:, 7], e2, col[:, 7:8], None, ALU.mult))
            chain(dve.max(row[:, 8], row[:, 7]))
            dve.max_index(idx[:], row[:, 8], row[:, 7]).then_inc(idx_done, 1)
            dve.tensor_scalar(col[:, 4:5], row[:, 8, 0:1], -1.0, None, ALU.mult).then_inc(ex_need, 1)
            dve.wait_ge(ex_done, 3)
            chain(dve.reciprocal(col[:, 8:9], col[:, 5:6]))
            dve.tensor_scalar(row[:, 10, 0:TOP_K], row[:, 9, 0:TOP_K], col[:, 8:9], None, ALU.mult).then_inc(top_done, 1)
            for g in range(NG):
                for k in range(KD):
                    j = KD * g + k
                    n = GSIZE[g] * P
                    dve.wait_ge(x_hi_done, j + 1)
                    dve.tensor_tensor(xT_lo[:, k, g * CH:g * CH + n], psT[:, j % 3, 0:n],
                                      xT_hi[:, k, g * CH:g * CH + n].bitcast(F32), ALU.subtract).then_inc(x_lo_done, 1)
            dve.wait_ge(wb_done, 1)

            def weights(k):
                dve.wait_ge(w1_hi_done, k + 1)
                dve.tensor_tensor(w1_lo[:, k], w1r[k], w1_hi[:, k].bitcast(F32), ALU.subtract).then_inc(w1_lo_done, 1)
                dve.wait_ge(w2_here[k], 16)
                dve.tensor_scalar(w2r[k], w2r[k], wb[:, k:k + 1], None, ALU.mult).then_inc(w2_scaled, 1)
                dve.wait_ge(w2_hi_done, k + 1)
                dve.tensor_tensor(w2[:, k * FT:(k + 1) * FT, D:2 * D], w2r[k],
                                  w2[:, k * FT:(k + 1) * FT, 0:D].bitcast(F32), ALU.subtract).then_inc(w2_lo_done, 1)
            weights(0)

            def mixed_bias():
                dve.wait_ge(b2_here, 16 * TOP_K)
                chain(dve.tensor_scalar(b2s[:], b2[:, 0], wb[:, 0:1], None, ALU.mult))
                chain(dve.scalar_tensor_tensor(b2s[:], b2[:, 1], wb[:, 1:2], b2s[:], ALU.mult, ALU.add))

            def low_part(c, e, w):
                j = EF * c + e
                dve.wait_ge(h_hi_done, j + 1)
                dve.tensor_tensor(hid_lo[:, e, 0:w], hid[:, e % 2, 0:w], hid_hi[:, e, 0:w].bitcast(F32),
                                  ALU.subtract).then_inc(h_lo_done, 1)

            def bias(c, e, tiles):
                if 0 <= e < tiles:
                    t = GB * c + e
                    dve.tensor_tensor(xn[:, t], xn[:, t], b2s[:], ALU.add).then_inc(xb_done, 1)

            def high_half(c, tiles):
                dve.wait_ge(y_low_done, c + 1)
                dve.tensor_tensor(y[:, 0:tiles], psO[:, 0:tiles, 0:D], y_low[:, 0:tiles],
                                  ALU.add).then_inc(y_high_done, 1)

            def add_bias(c, tiles):
                dve.wait_ge(y_high_done, c + 1)
                dve.wait_ge(xb_done, GB * c + tiles)
                dve.tensor_tensor(y[:, 0:tiles], y[:, 0:tiles], xn[:, bass.ds(GB * c, tiles)],
                                  ALU.add).then_inc(y_done, 1)

            def statistics(c, tiles):
                dve.wait_ge(y_done, c + 1)
                for q in range(tiles):
                    last = dve.bn_stats(st[:, q], y[:, q])
                last.then_inc(v3_step, 1)
                dve.wait_ge(v3_step, 4 * c + 1)
                s_, m_, v_, p_ = st[:, 0:tiles], mean3[:, 0:tiles], var3[:, 0:tiles], tmp3[:, 0:tiles]
                dve.tensor_tensor(m_, s_[:, :, 1], s_[:, :, 4], ALU.add)
                dve.tensor_tensor(p_, s_[:, :, 1], s_[:, :, 4], ALU.subtract)
                dve.tensor_tensor(v_, s_[:, :, 2], s_[:, :, 5], ALU.add).then_inc(v3_step, 1)
                dve.wait_ge(v3_step, 4 * c + 2)
                dve.tensor_scalar(m_, m_, 0.5, None, ALU.mult)
                dve.scalar_tensor_tensor(p_, p_, 0.25, p_, ALU.mult, ALU.mult).then_inc(v3_step, 1)
                dve.wait_ge(v3_step, 4 * c + 3)
                dve.scalar_tensor_tensor(v_, v_, 1.0 / D, p_, ALU.mult, ALU.add).then_inc(v3_done, 1)

            def normalise(c, tiles):
                dve.wait_ge(s3_done, c + 1)
                dve.reciprocal(rstd3[:, 0:tiles], std3[:, 0:tiles]).then_inc(v3_step, 1)
                dve.wait_ge(v3_step, 4 * c + 4)
                positive(dve, stored, 16 * c)
                for q in range(tiles):
                    dve.tensor_scalar(o[:, q], y[:, q], mean3[:, q:q + 1], rstd3[:, q:q + 1],
                                      ALU.subtract, ALU.mult).then_inc(o_done, 1)

            def chunk(c, w):
                first = isinstance(c, int) and c == 0
                for e in range(EF):
                    low_part(c, e, w)
                    if first and e == 1:
                        weights(1)
                    if first and e == FT - 1:
                        mixed_bias()
                    if not first:
                        if e == 0:
                            high_half(c - 1, GB)
                        if e == 1:
                            add_bias(c - 1, GB)
                        if e == 2:
                            statistics(c - 1, GB)
                        if e == 5:
                            normalise(c - 1, GB)
                    bias(c, e - FT, w // P)
            chunk(0, WIDTHS[0])
            with dve.Fori(1, LAST) as c:
                chunk(c, CH)
            chunk(LAST, WIDTHS[LAST])
            tiles = GSIZE[LAST]
            high_half(LAST, tiles)
            add_bias(LAST, tiles)
            statistics(LAST, tiles)
            normalise(LAST, tiles)
            dve.wait_ge(o_done, GB * LAST + tiles)
            dve.wait_ge(oo_done, LAST)
            g = gamma[:].rearrange("p (o d) -> p o d", o=1).to_broadcast([P, tiles, D])
            dve.tensor_tensor(o[:, 0:tiles], o[:, 0:tiles], g, ALU.mult).then_inc(og_done, 1)
            dve.wait_ge(og_done, NCH)
            dve.tensor_tensor(o[:, 0:tiles], o[:, 0:tiles], x1[:, GB * LAST:NT], ALU.add).then_inc(oo_done, 1)

        @block.tensor
        def _(pe):
            pe.wait_ge(ones_set, 1)
            for t in range(NT):
                pe.wait_ge(xn_done, t + 1)
                rows = P if t < NT - 1 else ROWS_LAST
                last = pe.matmul(psM[0:1, D:2 * D], ones[0:rows, 0:1], xn[0:rows, t, :],
                                 start=(t == 0), stop=(t == NT - 1))
            last.then_inc(sum_ready, 1)
            pe.wait_ge(sum_done, 1)
            for k in range(KD):
                last = pe.matmul(psM[:, k:k + 1], total[:, k * P:(k + 1) * P], ones[0:1, 0:1], start=True, stop=True)
            last.then_inc(mean_ready, 1)
            pe.wait_ge(mT_done, 1)
            pe.wait_ge(consts_here, 64)
            for k in range(KD):
                last = pe.matmul(psM[0:1, 16:16 + E], mT[:, k:k + 1], wr[:, k], start=(k == 0), stop=(k == KD - 1))
            last.then_inc(logits_ready, 1)

            def x_transposes(j):
                g, k = j // KD, j % KD
                if j >= 3:
                    pe.wait_ge(x_lo_done, j - 2)
                for b in range(GSIZE[g]):
                    t = GB * g + b
                    last = pe.transpose(psT[:, j % 3, b * P:(b + 1) * P], xn[:, t, k * P:(k + 1) * P], ident[:])
                last.then_inc(xt_done, 1)
            for j in range(3):
                x_transposes(j)
            pe.wait_ge(top_done, 1)
            pe.matmul(psM[:, 32:32 + TOP_K], ones[0:1, :], row[:, 10, 0:TOP_K], start=True, stop=True).then_inc(wb_ready, 1)
            for j in range(3, KD * NG):
                x_transposes(j)
            pe.wait_ge(x_lo_done, KD * NG)

            def hidden(c, e, w):
                if e >= 3:
                    pe.wait_ge(gelu_done, EF * c + e - 2)
                elif not isinstance(c, int) or c:
                    before = max(b for b in range(EF) if BANK[b] == BANK[e])
                    pe.wait_ge(gelu_done, EF * (c - 1) + before + 1)
                ps = psT[:, BANK[e], 0:w]
                x = e // FT
                cols = slice(e % FT * P, (e % FT + 1) * P)
                terms = [(k, a, v) for k in range(KD) for a, v in ((w1_hi, xT_hi), (w1_hi, xT_lo), (w1_lo, xT_hi))]
                for n, (k, a, v) in enumerate(terms):
                    last = pe.matmul(ps, a[:, x, k, cols], v[:, k, bass.ds(c * CH, w)],
                                     start=(n == 0), stop=(n == len(terms) - 1))
                last.then_inc(hid_ready, 1)

            def output(c, e, w):
                pe.wait_ge(h_lo_done, EF * c + e + 1)
                if e == 0:
                    positive(pe, y_high_done, c)
                for q in range(w // P):
                    cols = slice(q * P, (q + 1) * P)
                    pe.matmul(psO[:, q, :], hid_hi[:, e, cols], w2[:, e, :], start=(e == 0), stop=False)
                    last = pe.matmul(psO[:, q, 0:D], hid_lo[:, e, cols], w2[:, e, 0:D], start=False,
                                     stop=(e == EF - 1))
                last.then_inc(out_ready, 1)

            def chunk(c, w, nxt):
                first = isinstance(c, int) and c == 0
                for e in range(EF):
                    if first and e % FT == 0:
                        pe.wait_ge(w2_lo_done, e // FT + 1)
                    output(c, e, w)
                    for h in AFTER.get(e, ()):
                        if first and h == FT:
                            pe.wait_ge(w1_lo_done, 2)
                        hidden(c, h, w)
                    if nxt:
                        for h in AFTER_NEXT.get(e, ()):
                            hidden(c + 1, h, nxt)
            pe.wait_ge(w1_lo_done, 1)
            for e in range(3):
                hidden(0, e, WIDTHS[0])
            chunk(0, WIDTHS[0], WIDTHS[1])
            with pe.Fori(1, LAST - 1) as c:
                chunk(c, CH, CH)
            chunk(LAST - 1, CH, WIDTHS[LAST])
            chunk(LAST, WIDTHS[LAST], 0)


def kernel(x, adj, L0_gnn_gat_W, L0_gnn_gat_a, L0_gnn_edge_Wih, L0_gnn_edge_Whh, L0_gnn_edge_bih, L0_gnn_edge_bhh,
           L0_gnn_node_Wih, L0_gnn_node_Whh, L0_gnn_node_bih, L0_gnn_node_bhh, L0_ffn_Wr, L0_ffn_br, L0_ffn_W1,
           L0_ffn_b1, L0_ffn_W2, L0_ffn_b2, L0_ffn_gamma, L0_ffn_beta):
    import numpy as np
    import concourse.bacc as bacc
    from concourse.bass_utils import run_bass_kernel_spmd

    def rows(a):
        a = np.asarray(a)
        return a.reshape((a.shape[0] // P, P) + a.shape[1:]).swapaxes(0, 1)

    adj = np.asarray(adj)
    xp = np.zeros((NP, D), np.float32)
    xp[:N] = np.asarray(x)
    ap = np.zeros((NP, NP), np.float32)
    ap[:N, :N] = adj
    at = ap.reshape(NT, P, NT, P).transpose(0, 3, 2, 1).copy()
    an = ap.reshape(NT, P, NP).copy()
    xt = xp.reshape(NT, P, D).copy()
    for copy in range(1, COPIES):
        c = slice(CROWS * copy, CROWS * (copy + 1))
        at[:, c, NT - 1] = at[:, 0:CROWS, NT - 1]
        an[:, :, TAIL + c.start:TAIL + c.stop] = an[:, :, TAIL:TAIL + CROWS]
        an[NT - 1, c] = an[NT - 1, 0:CROWS]
        xt[NT - 1, c] = xt[NT - 1, 0:CROWS]
    dg = np.zeros((NP,), np.float32)
    dg[:N] = np.diagonal(adj)
    eye = np.eye(P, dtype=np.float32)
    gw = np.asarray(L0_gnn_gat_W)
    ga = np.asarray(L0_gnn_gat_a)
    gru = (L0_gnn_edge_Wih, L0_gnn_edge_Whh, L0_gnn_node_Wih, L0_gnn_node_Whh)
    gb = (L0_gnn_edge_bih, L0_gnn_edge_bhh, L0_gnn_node_bih, L0_gnn_node_bhh)
    arrays = {
        "x_tiles": xt,
        "adj_t": at.reshape(NT, P, NP),
        "adj_n": an,
        "diag": dg.reshape(NT, P).T,
        "ident": eye,
        "notid": np.stack([1 - eye, 1 - np.tile(eye[:CROWS, :CROWS], (P // CROWS, P // CROWS))], axis=1),
        "gat_wt": gw.transpose(0, 2, 1).reshape(HEADS, KD, P, D).transpose(2, 0, 1, 3),
        "gat_w": gw.reshape(HEADS, KD, P, D).transpose(2, 0, 1, 3),
        "gat_a": ga.reshape(HEADS, 2, KD, P).transpose(3, 0, 1, 2),
        "gru_w": np.stack([rows(np.asarray(w).T) for w in gru]),
        "gru_b": np.stack([np.asarray(v).reshape(3 * KD, P).T for v in gb], axis=1),
        "wr": rows(L0_ffn_Wr),
        "br": np.asarray(L0_ffn_br).reshape(1, E),
        "w1": np.stack([rows(w) for w in np.asarray(L0_ffn_W1)]),
        "b1": np.asarray(L0_ffn_b1).reshape(E, FT, P).transpose(0, 2, 1),
        "w2": np.stack([rows(w) for w in np.asarray(L0_ffn_W2)]),
        "b2": np.repeat(np.asarray(L0_ffn_b2)[:, None, :], P, axis=1),
        "gamma": np.repeat(np.asarray(L0_ffn_gamma)[None, :], P, axis=0),
        "beta": np.repeat(np.asarray(L0_ffn_beta)[None, :], P, axis=0),
    }
    nc = bacc.Bacc("TRN2", target_bir_lowering=False, num_devices=1)
    sent, args = {}, []
    for name, a in arrays.items():
        a = np.ascontiguousarray(a)
        sent[f"in_{name}"] = a
        args.append(nc.dram_tensor(f"in_{name}", a.shape, mybir.dt.from_np(a.dtype), kind="ExternalInput").ap())
    out = nc.dram_tensor("out_tiles", (NT, P, D), F32, kind="ExternalOutput").ap()
    build(nc, *args, out)
    r = run_bass_kernel_spmd(nc, [sent], core_ids=[0])
    return r.results[0]["out_tiles"].reshape(NP, D)[:N]
```
